# Optimizing a Trainium2 kernel written in Bass

```python
import numpy as np
import jax
import jax.numpy as jnp

def _softmax(x, axis=-1):
    return jax.nn.softmax(x, axis=axis)

def _gelu(x):
    return jax.nn.gelu(x, approximate=True)

def _silu(x):
    return jax.nn.silu(x)

def _sigmoid(x):
    return jax.nn.sigmoid(x)

def _layernorm(x, axis=-1, eps=1e-05):
    m = jnp.mean(x, axis=axis, keepdims=True)
    v = jnp.var(x, axis=axis, keepdims=True)
    return (x - m) / jnp.sqrt(v + eps)

def _scatter_add(tgt, idx, src, axis=0):
    return tgt.at[idx].add(src)

def _segment_sum(src, seg, n):
    return jax.ops.segment_sum(src, seg, n)
kernel_name = 'mk_cond_resid_d4_seqx_r2_4a7519'

def setup_inputs(seed: int=0):
    np.random.seed(seed)
    _w = jnp.asarray

    def _rec_inputs():
        import jax
        import jax.numpy as jnp
        _rk = jax.random.key(seed)
        x = -0.0003929 + 0.9999 * jax.random.normal(jax.random.fold_in(_rk, 1), (16, 512, 512), jnp.float32)
        _lenS = 512 - jax.random.randint(jax.random.fold_in(_rk, 7), (16,), 0, max(1, 512 // 4) + 1, jnp.int32)
        _lenS2 = 512 - jax.random.randint(jax.random.fold_in(_rk, 8), (16,), 0, max(1, 512 // 4) + 1, jnp.int32)
        cond_1024 = 0.00061147 + 0.102565 * jax.random.normal(jax.random.fold_in(_rk, 11), (16, 512), jnp.float32)
        itok_BxS_2_50255 = jax.random.randint(jax.random.fold_in(_rk, 12), (16, 512), 2, 25128, jnp.int32)
        return (x, cond_1024, itok_BxS_2_50255)
    x, cond_1024, itok_BxS_2_50255 = _rec_inputs()

    def _L0_cond_setup():
        import jax, jax.numpy as jnp
        import numpy as np
        key = jax.random.key(seed)
        ks = jax.random.split(key, 8)
        B, L, D, N, K = (4, 2048, 512, 64, 4)
        return {'x': jax.random.normal(ks[0], (B, L, D), dtype=jnp.float32), 'conv_w': jax.random.normal(ks[1], (K, 1, D), dtype=jnp.float32) * 0.1, 'conv_b': jnp.zeros((D,), dtype=jnp.float32), 'Wp': jax.random.normal(ks[2], (D, 2 * N), dtype=jnp.float32) * (1.0 / np.sqrt(D)), 'bp': jnp.zeros((2 * N,), dtype=jnp.float32), 'Ws': jax.random.normal(ks[3], (D, N), dtype=jnp.float32) * (1.0 / np.sqrt(D)), 'bs': jnp.zeros((N,), dtype=jnp.float32), 'A_log': jax.random.normal(ks[4], (N,), dtype=jnp.float32) * 0.02, 'dt_log': jax.random.normal(ks[5], (N,), dtype=jnp.float32) * 0.02, 'Wo': jax.random.normal(ks[6], (N, D), dtype=jnp.float32) * (1.0 / np.sqrt(N)), 'bo': jnp.zeros((D,), dtype=jnp.float32)}
    _L0_cond_all = _L0_cond_setup()
    _L0_cond_in = {k: v for k, v in _L0_cond_all.items() if k in ('conv_b', 'Wp', 'bp', 'Ws', 'bs', 'A_log', 'dt_log', 'Wo', 'bo')}
    del _L0_cond_all

    def _L1_cond_setup():
        import jax, jax.numpy as jnp
        import numpy as np

        def _lstm(x, h0, Wx, Wh, b):
            H = h0.shape[1]
            xW = jnp.einsum('ntd,dk->ntk', x, Wx) + b
            c0 = jnp.zeros_like(h0)

            def step(carry, xw_t):
                prev_h, prev_c = carry
                a = xw_t + prev_h @ Wh
                i = jax.nn.sigmoid(a[:, :H])
                f = jax.nn.sigmoid(a[:, H:2 * H])
                o = jax.nn.sigmoid(a[:, 2 * H:3 * H])
                g = jnp.tanh(a[:, 3 * H:])
                next_c = f * prev_c + i * g
                next_h = o * jnp.tanh(next_c)
                return ((next_h, next_c), next_h)
            _, hs = jax.lax.scan(step, (h0, c0), jnp.swapaxes(xW, 0, 1))
            return jnp.swapaxes(hs, 0, 1)
        key = jax.random.key(seed)
        k_x, k_h0, k_wx, k_wh = jax.random.split(key, 4)
        N, T, D, H = (64, 256, 512, 512)
        x = jax.random.normal(k_x, (N, T, D), dtype=jnp.float32)
        h0 = jax.random.normal(k_h0, (N, H), dtype=jnp.float32)
        Wx = jax.random.normal(k_wx, (D, 4 * H), dtype=jnp.float32) / jnp.sqrt(jnp.float32(D))
        Wh = jax.random.normal(k_wh, (H, 4 * H), dtype=jnp.float32) / jnp.sqrt(jnp.float32(H))
        b = jnp.zeros((4 * H,), dtype=jnp.float32)
        return {'x': x, 'h0': h0, 'Wx': Wx, 'Wh': Wh, 'b': b}
    _L1_cond_all = _L1_cond_setup()
    _L1_cond_in = {k: v for k, v in _L1_cond_all.items() if k in ('Wx', 'Wh', 'b')}
    del _L1_cond_all

    def _L2_cond_setup():
        import jax, jax.numpy as jnp
        import numpy as np
        HASH_PRIME = 5099
        MIN_CAPACITY = 4
        key = jax.random.key(seed)
        ks = jax.random.split(key, 8)
        B, T, D, F, E = (8, 1024, 512, 1024, 16)
        return {'x': jax.random.normal(ks[0], (B, T, D), dtype=jnp.float32), 'token_ids': jax.random.randint(ks[1], (B, T), 0, 50257, dtype=jnp.int32), 'shift_state': jax.random.normal(ks[2], (B, D), dtype=jnp.float32), 'time_maa_k': jax.random.uniform(ks[3], (D,), dtype=jnp.float32), 'time_maa_r': jax.random.uniform(ks[4], (D,), dtype=jnp.float32), 'w_recept': jax.random.normal(ks[5], (D, D), dtype=jnp.float32) * 0.02, 'w_key': jax.random.normal(ks[6], (E, D, F), dtype=jnp.float32) * 0.02, 'w_value': jax.random.normal(ks[7], (E, F, D), dtype=jnp.float32) * 0.02}
    _L2_cond_all = _L2_cond_setup()
    _L2_cond_in = {k: v for k, v in _L2_cond_all.items() if k in ('time_maa_k', 'time_maa_r', 'w_recept', 'w_key', 'w_value')}
    del _L2_cond_all

    def _L3_cond_setup():
        import jax, jax.numpy as jnp
        import numpy as np
        TEMPERATURE = 2.0
        key = jax.random.key(seed)
        k1, k2 = jax.random.split(key)
        B, N, D = (16, 1024, 512)
        x = jax.random.normal(k1, (B, N, D), dtype=jnp.float32)
        random_values = jax.random.uniform(k2, (B, D), dtype=jnp.float32)
        return {'x': x, 'random_values': random_values}
    _L3_cond_all = _L3_cond_setup()
    _L3_cond_in = {k: v for k, v in _L3_cond_all.items() if k in ()}
    del _L3_cond_all
    return {'x': x, 'cond_1024': cond_1024, 'itok_BxS_2_50255': itok_BxS_2_50255, 'L0_cond_conv_b': _L0_cond_in['conv_b'], 'L0_cond_Wp': _L0_cond_in['Wp'], 'L0_cond_bp': _L0_cond_in['bp'], 'L0_cond_Ws': _L0_cond_in['Ws'], 'L0_cond_bs': _L0_cond_in['bs'], 'L0_cond_A_log': _L0_cond_in['A_log'], 'L0_cond_dt_log': _L0_cond_in['dt_log'], 'L0_cond_Wo': _L0_cond_in['Wo'], 'L0_cond_bo': _L0_cond_in['bo'], 'L1_cond_Wx': _L1_cond_in['Wx'], 'L1_cond_Wh': _L1_cond_in['Wh'], 'L1_cond_b': _L1_cond_in['b'], 'L2_cond_time_maa_k': _L2_cond_in['time_maa_k'], 'L2_cond_time_maa_r': _L2_cond_in['time_maa_r'], 'L2_cond_w_recept': _L2_cond_in['w_recept'], 'L2_cond_w_key': _L2_cond_in['w_key'], 'L2_cond_w_value': _L2_cond_in['w_value']}

def reference(x, cond_1024, itok_BxS_2_50255, L0_cond_conv_b, L0_cond_Wp, L0_cond_bp, L0_cond_Ws, L0_cond_bs, L0_cond_A_log, L0_cond_dt_log, L0_cond_Wo, L0_cond_bo, L1_cond_Wx, L1_cond_Wh, L1_cond_b, L2_cond_time_maa_k, L2_cond_time_maa_r, L2_cond_w_recept, L2_cond_w_key, L2_cond_w_value):
    import jax
    import jax.numpy as jnp

    def _L0_cond_ref(x, conv_w, conv_b, Wp, bp, Ws, bs, A_log, dt_log, Wo, bo):
        import jax, jax.numpy as jnp
        import numpy as np
        B, L, D = x.shape
        K = conv_w.shape[0]
        N = Ws.shape[1]
        x_pad = jnp.pad(x, ((0, 0), (K - 1, 0), (0, 0)))
        conv = conv_b + sum((x_pad[:, k:k + L, :] * conv_w[k, 0] for k in range(K)))
        proj = conv @ Wp + bp
        B_t = jax.nn.softplus(proj[..., :N])
        C_t = jnp.tanh(proj[..., N:])
        u = x @ Ws + bs
        A = -jax.nn.softplus(A_log)
        dt = jax.nn.softplus(dt_log)
        decay = 1.0 + dt * A

        def step(state, inputs):
            u_t, b_t, c_t = inputs
            state = decay * state + dt * b_t * u_t
            return (state, c_t * state)
        init = jnp.zeros((B, N), dtype=x.dtype)
        xs = tuple((jnp.swapaxes(a, 0, 1) for a in (u, B_t, C_t)))
        _, ys = jax.lax.scan(step, init, xs, unroll=4)
        y = jnp.swapaxes(ys, 0, 1)
        return y @ Wo + bo

    def _L1_cond_ref(x, h0, Wx, Wh, b):
        import jax, jax.numpy as jnp
        import numpy as np

        def _lstm(x, h0, Wx, Wh, b):
            H = h0.shape[1]
            xW = jnp.einsum('ntd,dk->ntk', x, Wx) + b
            c0 = jnp.zeros_like(h0)

            def step(carry, xw_t):
                prev_h, prev_c = carry
                a = xw_t + prev_h @ Wh
                i = jax.nn.sigmoid(a[:, :H])
                f = jax.nn.sigmoid(a[:, H:2 * H])
                o = jax.nn.sigmoid(a[:, 2 * H:3 * H])
                g = jnp.tanh(a[:, 3 * H:])
                next_c = f * prev_c + i * g
                next_h = o * jnp.tanh(next_c)
                return ((next_h, next_c), next_h)
            _, hs = jax.lax.scan(step, (h0, c0), jnp.swapaxes(xW, 0, 1))
            return jnp.swapaxes(hs, 0, 1)
        return _lstm(x, h0, Wx, Wh, b)

    def _L2_cond_ref(x, token_ids, shift_state, time_maa_k, time_maa_r, w_recept, w_key, w_value):
        import jax, jax.numpy as jnp
        import numpy as np
        HASH_PRIME = 5099
        MIN_CAPACITY = 4
        B, T, D = x.shape
        E = w_key.shape[0]
        N = B * T
        C = max(MIN_CAPACITY, N // E)
        xprev = jnp.concatenate([shift_state[:, None, :], x[:, :-1]], axis=1)
        dxprev = xprev - x
        xk = x + dxprev * time_maa_k
        xr = x + dxprev * time_maa_r
        e_idx = token_ids.reshape(N).astype(jnp.int32) * HASH_PRIME % E
        onehot = (e_idx[:, None] == jnp.arange(E, dtype=jnp.int32)[None, :]).astype(jnp.int32)
        pos = jnp.take_along_axis(jnp.cumsum(onehot, axis=0), e_idx[:, None], axis=1)[:, 0] - 1
        keep = pos < C
        slot = jnp.where(keep, e_idx * C + pos, E * C)
        xk_flat = xk.reshape(N, D)
        buf = jnp.zeros((E * C + 1, D), dtype=x.dtype).at[slot].set(xk_flat)
        expert_in = buf[:E * C].reshape(E, C, D)
        h = jnp.square(jax.nn.relu(jnp.einsum('ecd,edf->ecf', expert_in, w_key)))
        expert_out = jnp.einsum('ecf,efd->ecd', h, w_value)
        out_pad = jnp.concatenate([expert_out.reshape(E * C, D), jnp.zeros((1, D), dtype=x.dtype)], axis=0)
        y = out_pad[slot].reshape(B, T, D)
        r = jax.nn.sigmoid(jnp.einsum('btd,ed->bte', xr, w_recept))
        return r * y

    def _L3_cond_ref(x, random_values):
        import jax, jax.numpy as jnp
        import numpy as np
        TEMPERATURE = 2.0
        ax = jnp.abs(x)
        p = ax / jnp.sum(ax, axis=1, keepdims=True)
        pi = jnp.exp(p * TEMPERATURE)
        thresholds = pi / jnp.sum(pi, axis=1, keepdims=True)
        cum = jnp.cumsum(thresholds, axis=1) + 0.001
        rv = random_values[:, None, :]
        chosen_idx = jnp.sum(cum <= rv, axis=1, keepdims=True)
        gathered = jnp.take_along_axis(ax, chosen_idx, axis=1)
        mask = ax >= gathered
        return x * mask
    x = x + _L0_cond_ref(x, cond_1024[:, None, :], L0_cond_conv_b, L0_cond_Wp, L0_cond_bp, L0_cond_Ws, L0_cond_bs, L0_cond_A_log, L0_cond_dt_log, L0_cond_Wo, L0_cond_bo)
    x = x + _L1_cond_ref(x, cond_1024, L1_cond_Wx, L1_cond_Wh, L1_cond_b)
    x = x + _L2_cond_ref(x, itok_BxS_2_50255, cond_1024, L2_cond_time_maa_k, L2_cond_time_maa_r, L2_cond_w_recept, L2_cond_w_key, L2_cond_w_value)
    x = x + _L3_cond_ref(x, cond_1024)
    return x

_drawn_inputs = setup_inputs


def setup_inputs(seed=0):
    import zlib

    import numpy as np

    out = dict(_drawn_inputs(seed))
    spreads = {'L0_cond_conv_b': (0.0, 0.1),
     'L0_cond_bp': (0.0, 0.1),
     'L0_cond_bs': (0.0, 0.1),
     'L0_cond_bo': (0.0, 0.1),
     'L1_cond_b': (0.0, 0.1)}
    factors = {'L0_cond_A_log': 5.032, 'L0_cond_dt_log': 4.072, 'L2_cond_time_maa_r': 3.443}
    for name, (base, spread) in spreads.items():
        noise = np.random.default_rng([zlib.crc32(name.encode()), seed]).standard_normal(out[name].shape)
        drawn = base * np.exp(spread * noise) if base else spread * noise
        out[name] = jnp.asarray(drawn.astype(out[name].dtype))
    for name, factor in factors.items():
        out[name] = (out[name] * factor).astype(out[name].dtype)
    return out
```

```python
from contextlib import ExitStack

import concourse.bass as bass
from concourse import mybir

F32 = mybir.dt.float32
I32 = mybir.dt.int32
ALU = mybir.AluOpType
ACT = mybir.ActivationFunctionType
AX = mybir.AxisListType

P = 128
B, T, D = 16, 512, 512
KD = D // P
H = 512
N_STATE = 64
TAPS = 16
NTOK = B * T
STEPS = 8
TILE = STEPS * B
NTILE = T // STEPS
HALO = (TAPS - 1) * B
WIN = HALO + TILE
E = 16
FF = 1024
KF = FF // P
CAP = max(4, NTOK // E)
GCOLS = 4 * P
MIX = 512
NMIX = NTOK // MIX
SUB = MIX // P
HASH = 5099 % E


def build(nc, ins, out):
    x2_d = nc.dram_tensor("x2_scratch", (KD, P, NTOK), F32, kind="Internal").ap()
    r_d = nc.dram_tensor("gate_scratch", (KD, P, NTOK), F32, kind="Internal").ap()
    slot_d = nc.dram_tensor("slot_scratch", (NTOK,), I32, kind="Internal").ap()
    rows_d = nc.dram_tensor("expert_in_scratch", (E * CAP, D), F32, kind="Internal").ap()
    y_d = nc.dram_tensor("expert_out_scratch", (E * CAP + 1, D), F32, kind="Internal").ap()
    with ExitStack() as ctx:
        arena = ctx.enter_context(nc.sbuf_tensor("arena", [P, 52800], F32))
        banks = [ctx.enter_context(nc.psum_tensor(f"bank{i}", [P, 512], F32)) for i in range(8)]
        top = [0]

        def carve(*shape):
            n = 1
            for s in shape:
                n *= s
            a = arena[:, top[0]:top[0] + n]
            top[0] += n
            assert top[0] <= 52800, top[0]
            if len(shape) == 2:
                a = a.rearrange("p (a b) -> p a b", a=shape[0])
            if len(shape) == 3:
                a = a.rearrange("p (a b c) -> p a b c", a=shape[0], b=shape[1])
            return a

        ident = carve(P)
        cond = carve(KD, B)
        slot = carve(NTILE).bitcast(I32)
        keep = dict(ident=ident, cond=cond, slot=slot)
        base = top[0]
        route_phase(nc, ctx, ins, carve, banks, keep, slot_d, rows_d, y_d)
        top[0] = base
        recur_phase(nc, ctx, ins, carve, banks, keep, x2_d)
        top[0] = base
        mix_phase(nc, ctx, ins, carve, banks, keep, x2_d, r_d, rows_d)
        top[0] = base
        expert_phase(nc, ctx, ins, carve, banks, keep, rows_d, y_d)
        top[0] = base
        mask_phase(nc, ctx, ins, carve, banks, keep, x2_d, r_d, y_d, out)


def route_phase(nc, ctx, ins, carve, banks, keep, slot_d, rows_d, y_d):
    SEG = NTOK // P
    ident, cond, slot = keep["ident"], keep["cond"], keep["slot"]
    zeros = carve(4 * D)
    ids = carve(SEG).bitcast(I32)
    hashed = carve(SEG).bitcast(I32)
    expert = carve(SEG)
    expert_no = carve(E, SEG)
    slot_base = carve(E, SEG)
    onehot = carve(E, SEG)
    segment = carve(E, SEG)
    count = carve(E, SEG)
    before = carve(P)
    offset = carve(E)
    slot_f = carve(SEG)
    slot_i = carve(SEG).bitcast(I32)
    psum_off = banks[0]

    def sem(name):
        return ctx.enter_context(nc.semaphore(name))

    ids_landed, cond_landed = sem("rt_ids_landed"), sem("rt_cond_landed")
    zeroed, consts, steps = sem("rt_zeroed"), sem("rt_consts"), sem("rt_vector_steps")
    zero_stored, offsets_made = sem("rt_zero_stored"), sem("rt_offsets_made")
    slots_stored, slots_landed = sem("rt_slots_stored"), sem("rt_slots_landed")
    NZERO = E * CAP // (4 * P)
    with nc.Block() as block:
        @block.sync
        def _(sp):
            sp.dma_start(ids, ins["ids"]).then_inc(ids_landed, 16)
            sp.dma_start(cond, ins["condT"]).then_inc(cond_landed, 16)
            sp.wait_ge(zeroed, 1)
            for z in range(NZERO):
                sp.dma_start(rows_d[z * 4 * P:(z + 1) * 4 * P, :].rearrange("(p r) d -> p (r d)", r=4),
                             zeros).then_inc(zero_stored, 16)
            sp.dma_start(y_d[E * CAP:E * CAP + 1, :], zeros[0:1, 0:D]).then_inc(zero_stored, 16)
            sp.wait_ge(steps, 13)
            sp.dma_start(slot_d.rearrange("(p i) -> p i", p=P), slot_i).then_inc(slots_stored, 16)
            sp.wait_ge(slots_stored, 16)
            src = slot_d.rearrange("(b c t) -> t b c", b=B, t=STEPS)
            for t in range(STEPS):
                sp.dma_start(slot[t * B:(t + 1) * B, :], src[t], allow_slow_non_contiguous=True).then_inc(slots_landed, 16)
            sp.wait_ge(slots_landed, 16 * STEPS)
            sp.wait_ge(zero_stored, 16 * (NZERO + 1))
            sp.wait_ge(cond_landed, 16)

        @block.gpsimd
        def _(pool):
            nc.gpsimd.memset(zeros, 0.0).then_inc(zeroed, 1)
            nc.gpsimd.memset(ident, 0.0).then_inc(consts, 1)
            nc.gpsimd.memset(before, 0.0).then_inc(consts, 1)
            nc.gpsimd.memset(segment, 1.0).then_inc(consts, 1)
            nc.gpsimd.iota(expert_no, pattern=[[1, E], [0, SEG]], base=0, channel_multiplier=0,
                           allow_small_or_imprecise_dtypes=True).then_inc(consts, 1)
            nc.gpsimd.iota(slot_base, pattern=[[CAP, E], [0, SEG]], base=-1 - E * CAP, channel_multiplier=0,
                           allow_small_or_imprecise_dtypes=True).then_inc(consts, 1)
            pool.wait_ge(consts, 5)
            nc.gpsimd.affine_select(out=ident, in_=ident, compare_op=ALU.not_equal, fill=1.0, base=0,
                                    pattern=[[-1, P]], channel_multiplier=1).then_inc(consts, 1)
            nc.gpsimd.affine_select(out=before, in_=before, compare_op=ALU.is_ge, fill=1.0, base=0,
                                    pattern=[[-1, P]], channel_multiplier=1).then_inc(consts, 1)
            nc.gpsimd.memset(segment[:, :, 0:1], 0.0).then_inc(consts, 1)

        @block.tensor
        def _(pe):
            pe.wait_ge(consts, 8)
            pe.wait_ge(steps, 6)
            nc.tensor.matmul(psum_off[:, 0:E], before, count[:, :, SEG - 1], start=True,
                             stop=True).then_inc(offsets_made, 1)

        @block.vector
        def _(dve):
            v = nc.vector
            dve.wait_ge(ids_landed, 16)
            v.tensor_scalar(hashed, ids, E - 1, None, ALU.bitwise_and).then_inc(steps, 1)
            dve.wait_ge(steps, 1)
            v.tensor_scalar(ids, hashed, float(HASH), None, ALU.mult).then_inc(steps, 1)
            dve.wait_ge(steps, 2)
            v.tensor_scalar(hashed, ids, E - 1, None, ALU.bitwise_and).then_inc(steps, 1)
            dve.wait_ge(steps, 3)
            v.tensor_copy(expert, hashed).then_inc(steps, 1)
            dve.wait_ge(steps, 4)
            dve.wait_ge(consts, 8)
            v.tensor_tensor(onehot, expert.unsqueeze(1).broadcast_to([P, E, SEG]), expert_no,
                            ALU.is_equal).then_inc(steps, 1)
            dve.wait_ge(steps, 5)
            v.tensor_tensor_scan(count.rearrange("p e i -> p (e i)"), segment.rearrange("p e i -> p (e i)"),
                                 onehot.rearrange("p e i -> p (e i)"), 0.0, ALU.mult, ALU.add).then_inc(steps, 1)
            dve.wait_ge(offsets_made, 1)
            v.tensor_copy(offset, psum_off[:, 0:E]).then_inc(steps, 1)
            dve.wait_ge(steps, 7)
            v.tensor_tensor(count, count, offset.unsqueeze(2).broadcast_to([P, E, SEG]),
                            ALU.add).then_inc(steps, 1)
            dve.wait_ge(steps, 8)
            v.scalar_tensor_tensor(out=onehot, in0=count, scalar=float(CAP), in1=onehot, op0=ALU.is_le,
                                   op1=ALU.mult).then_inc(steps, 1)
            v.tensor_tensor(count, count, slot_base, ALU.add).then_inc(steps, 1)
            dve.wait_ge(steps, 10)
            v.tensor_tensor(count, count, onehot, ALU.mult).then_inc(steps, 1)
            dve.wait_ge(steps, 11)
            v.tensor_reduce(slot_f, count.rearrange("p e i -> p i e"), AX.X, ALU.add).then_inc(steps, 1)
            dve.wait_ge(steps, 12)
            v.tensor_scalar(slot_i, slot_f, float(E * CAP), None, ALU.add).then_inc(steps, 1)


def recur_phase(nc, ctx, ins, carve, banks, keep, x2_d):
    ident, cond = keep["ident"], keep["cond"]
    wh = carve(KD, 4 * H)
    wx = carve(KD, 4 * H)
    xw_bias = carve(4 * H)
    xw = [carve(4 * H) for _ in range(2)]
    xin = [carve(KD, WIN) for _ in range(2)]
    conv = [carve(KD, TILE) for _ in range(2)]
    x1 = [carve(KD, TILE) for _ in range(2)]
    x2 = [carve(KD, TILE) for _ in range(2)]
    wp = carve(KD, 2 * N_STATE)
    ws = carve(KD, N_STATE)
    wo = carve(D)[0:N_STATE]
    taps = cond
    conv_b, bo = carve(KD), carve(KD)
    bp_b, bp_c, bs, a_log, dt_log, delta, decay = [carve(1)[0:N_STATE] for _ in range(7)]
    scratch = carve(8)[0:N_STATE]
    decays = carve(B, STEPS)[0:N_STATE]
    pick = carve(STEPS, 32)
    hT = [carve(KD, 32) for _ in range(2)]
    sig = carve(3, P)
    gcand, cell, term_f, term_i, tcell, hid = [carve(P) for _ in range(6)]
    c_gate, z_abs, z_exp, z_ln, z_relu, drive_b, y = [carve(TILE)[0:N_STATE] for _ in range(7)]
    drive = carve(B, STEPS)[0:N_STATE]
    state = carve(B, STEPS)[0:N_STATE]
    gates = banks[0:2]
    turned = banks[2]
    xw_ps = banks[3:5]
    proj_ps, u_ps, o_ps = banks[5], banks[6], banks[7]

    names = ["weights_landed", "h0_landed", "bufs_zeroed", "pick_made", "small_ready",
             "conv_done", "proj_done", "u_done", "gate_c_ready", "soft_exp", "soft_ready", "bt_ready",
             "drive_ready", "carry_added", "state_ready", "y_ready", "o_done", "x1_ready", "sp_passed",
             "hT_free", "hT_ready", "hT_turned", "gates_done", "if_ready", "g_ready", "o_ready",
             "terms_ready", "c_ready", "tc_ready", "h_ready", "xw_summed", "xw_ready", "soft_abs"]
    s = {n: ctx.enter_context(nc.semaphore("rc_" + n)) for n in names}
    x_landed = [ctx.enter_context(nc.semaphore(f"rc_x_landed{i}")) for i in range(2)]
    x2_stored = [ctx.enter_context(nc.semaphore(f"rc_x2_stored{i}")) for i in range(2)]
    x_dram = ins["xT"]
    NLOOP = (NTILE - 4) // 2
    weights = [(wh, ins["Wh"]), (wx, ins["Wx"]), (xw_bias, ins["b"].partition_broadcast(P)),
               (wp, ins["Wp"]), (ws, ins["Ws"]), (wo, ins["Wo"]), (conv_b, ins["conv_b"]),
               (bo, ins["bo"]), (bp_b, ins["bp"][0]), (bp_c, ins["bp"][1]), (bs, ins["bs"]),
               (a_log, ins["A_log"]), (dt_log, ins["dt_log"])]

    def tiles(eng, body):
        for n in range(2):
            body(n, 0, n, 3)
        with eng.Fori(1, NLOOP) as pair:
            body(2 * pair, pair, 0, 3)
            body(2 * pair + 1, pair, 1, 3)
        for n in range(2 * NLOOP, NTILE):
            body(n, n // 2, n % 2, min(3, NTILE - 1 - n))

    with nc.Block() as block:
        @block.sync
        def _(sp):
            for dst, src in weights[2:]:
                sp.dma_start(dst, src).then_inc(s["weights_landed"], 16)
            sp.wait_ge(s["bufs_zeroed"], 2)
            sp.dma_start(xin[0][:, :, HALO:], x_dram[:, :, 0:TILE]).then_inc(x_landed[0], 16)
            sp.dma_start(xin[1][:, :, HALO - TILE:], x_dram[:, :, 0:2 * TILE]).then_inc(x_landed[1], 16)
            for dst, src in weights[:2]:
                sp.dma_start(dst, src).then_inc(s["weights_landed"], 16)
            for m in (2, 3):
                sp.wait_ge(s["x1_ready"], KD * (m - 1))
                sp.dma_start(xin[m % 2], x_dram[:, :, m * TILE - HALO:(m + 1) * TILE]).then_inc(x_landed[m % 2], 16)

            def tile(n, pair, par, ahead):
                if ahead == 3 and not (isinstance(n, int) and n + 4 >= NTILE):
                    sp.wait_ge(s["x1_ready"], KD * (n + 3))
                    sp.dma_start(xin[par], x_dram[:, :, bass.ds(n * TILE + 4 * TILE - HALO, WIN)])\
                        .then_inc(x_landed[par], 16)
                sp.wait_ge(s["hT_free"], STEPS * n + STEPS + 2)
                sp.sem_inc(s["sp_passed"], 1)
                sp.dma_start(x2_d.rearrange("c p n -> p c n")[:, :, bass.ds(n * TILE, TILE)], x2[par])\
                    .then_inc(x2_stored[par], 16)

            tiles(sp, tile)
            for par in range(2):
                sp.wait_ge(x2_stored[par], 16 * NTILE // 2)

        @block.gpsimd
        def _(pool):
            g = nc.gpsimd
            g.memset(xin[0][:, :, 0:HALO], 0.0).then_inc(s["bufs_zeroed"], 1)
            g.memset(xin[1][:, :, 0:HALO - TILE], 0.0).then_inc(s["bufs_zeroed"], 1)
            g.memset(cell, 0.0).then_inc(s["bufs_zeroed"], 1)
            g.memset(state, 0.0).then_inc(s["bufs_zeroed"], 1)
            for par in range(2):
                g.memset(hT[par], 0.0).then_inc(s["hT_free"], 1)
            g.memset(decays, 1.0).then_inc(s["pick_made"], 1)
            g.memset(pick, 0.0).then_inc(s["pick_made"], 1)
            pool.wait_ge(s["hT_free"], 2)
            g.tensor_copy(hT[0][:, :, 0:B], cond).then_inc(s["hT_ready"], 1)
            pool.wait_ge(s["pick_made"], 2)
            g.memset(decays[:, :, 0:1], 0.0).then_inc(s["pick_made"], 1)
            g.affine_select(out=pick[:, :, 0:B], in_=pick[:, :, 0:B], compare_op=ALU.not_equal, fill=1.0,
                            base=0, pattern=[[-B, STEPS], [-1, B]], channel_multiplier=1)\
                .then_inc(s["pick_made"], 1)

            def tile(n, pair, par, ahead):
                pool.wait_ge(s["x1_ready"], KD * (n + 1))
                if not (isinstance(n, int) and n < 2):
                    pool.wait_ge(x2_stored[par], 16 * pair)
                for st in range(STEPS):
                    pool.wait_ge(s["hT_ready"], STEPS * n + st + 2)
                    cols = slice(st * B, (st + 1) * B)
                    g.tensor_tensor(x2[par][:, :, cols], x1[par][:, :, cols], hT[(st + 1) % 2][:, :, 0:B], ALU.add)\
                        .then_inc(s["hT_free"], 1)

            tiles(pool, tile)

        @block.tensor
        def _(pe):
            mm = nc.tensor.matmul

            def project(n, par):
                pe.wait_ge(s["conv_done"], KD * TAPS * (n + 1))
                if not (isinstance(n, int) and n == 0):
                    pe.wait_ge(s["soft_abs"], n)
                for k in range(KD):
                    last = mm(proj_ps[:, 0:TILE], wp[:, k, :], conv[par][:, k, :], start=k == 0, stop=k == KD - 1)
                last.then_inc(s["proj_done"], 1)

            def inputs(n, par):
                if not (isinstance(n, int) and n == 0):
                    pe.wait_ge(s["drive_ready"], n)
                for k in range(KD):
                    last = mm(u_ps[0:N_STATE, 0:TILE], ws[:, k, :], xin[par][:, k, HALO:], start=k == 0,
                              stop=k == KD - 1)
                last.then_inc(s["u_done"], 1)

            def outputs(n, par):
                pe.wait_ge(s["y_ready"], n + 1)
                for m in range(KD):
                    last = mm(o_ps[:, m * P:(m + 1) * P], wo[:, m * P:(m + 1) * P], y, start=True, stop=True)
                last.then_inc(s["o_done"], 1)

            def input_gates(n, par, q, ks):
                if ks[0] == 0:
                    pe.wait_ge(s["x1_ready"], KD * (n + 1))
                    if not (isinstance(n, int) and n == 0 and q < 2):
                        pe.wait_ge(s["xw_ready"], KD * n + q - 1)
                for k in ks:
                    last = mm(xw_ps[q % 2][:, :], x1[par][:, k, :], wx[:, k, q * GCOLS:(q + 1) * GCOLS],
                              start=k == 0, stop=k == KD - 1)
                if ks[-1] == KD - 1:
                    last.then_inc(s["xw_summed"], 1)

            def pick_inputs(n, par, st):
                pe.wait_ge(s["xw_ready"], KD * (n + 1))
                for j in range(KD):
                    mm(gates[st % 2][32 * j:32 * j + 32, :], pick[:, st, :], xw[par][:, j * GCOLS:(j + 1) * GCOLS],
                       start=True, stop=False, skip_group_check=True)

            pe.wait_ge(s["weights_landed"], 16 * len(weights))
            for n in range(2):
                project(n, n)
                inputs(n, n)
                outputs(n, n)
            for q in range(KD):
                input_gates(0, 0, q, range(KD))
            pe.wait_ge(s["pick_made"], 4)
            pick_inputs(0, 0, 0)

            def tile(n, pair, par, ahead):
                for st in range(STEPS):
                    pe.wait_ge(s["hT_ready"], STEPS * n + st + 1)
                    for k in range(KD):
                        for j in range(KD):
                            last = mm(gates[st % 2][32 * j:32 * j + 32, :], hT[st % 2][:, k, :],
                                      wh[:, k, j * GCOLS:(j + 1) * GCOLS], start=False, stop=k == KD - 1,
                                      skip_group_check=True)
                    last.then_inc(s["gates_done"], 1)
                    if ahead >= 1:
                        input_gates(n + 1, 1 - par, st // 2, (0, 1) if st % 2 == 0 else (2, 3))
                    if ahead >= 2 and st == 0:
                        project(n + 2, par)
                        inputs(n + 2, par)
                    if ahead >= 2 and st == 6:
                        outputs(n + 2, par)
                    pe.wait_ge(s["h_ready"], STEPS * n + st + 1)
                    nc.tensor.transpose(turned[:, 0:P], hid, ident).then_inc(s["hT_turned"], 1)
                    if st < STEPS - 1:
                        pick_inputs(n, par, st + 1)
                    elif ahead >= 1:
                        pick_inputs(n + 1, 1 - par, 0)

            tiles(pe, tile)

        @block.scalar
        def _(act):
            a = nc.scalar.activation

            def soft_first(n):
                act.wait_ge(s["proj_done"], n + 1)
                if not (isinstance(n, int) and n == 0):
                    act.wait_ge(s["y_ready"], n)
                a(c_gate, proj_ps[N_STATE:2 * N_STATE, 0:TILE], ACT.Tanh, bias=bp_c).then_inc(s["gate_c_ready"], 1)
                a(z_relu, proj_ps[0:N_STATE, 0:TILE], ACT.Relu, bias=bp_b)
                a(z_abs, proj_ps[0:N_STATE, 0:TILE], ACT.Abs, bias=bp_b).then_inc(s["soft_abs"], 1)

            def soft_last(n):
                act.wait_ge(s["soft_abs"], n + 1)
                a(z_exp, z_abs, ACT.Exp, scale=-1.0).then_inc(s["soft_exp"], 1)
                act.wait_ge(s["soft_exp"], n + 3)
                a(z_ln, z_exp, ACT.Ln, bias=1.0).then_inc(s["soft_ready"], 1)

            act.wait_ge(s["weights_landed"], 16 * len(weights))
            for i, src in enumerate((dt_log, a_log)):
                a(scratch[:, i:i + 1], src, ACT.Abs).then_inc(s["small_ready"], 1)
            act.wait_ge(s["small_ready"], 2)
            for i in range(2):
                a(scratch[:, i:i + 1], scratch[:, i:i + 1], ACT.Exp, scale=-1.0).then_inc(s["soft_exp"], 1)
            act.wait_ge(s["soft_exp"], 2)
            for i in range(2):
                a(scratch[:, i:i + 1], scratch[:, i:i + 1], ACT.Ln, bias=1.0).then_inc(s["small_ready"], 1)
            for n in range(2):
                soft_first(n)
                soft_last(n)

            def tile(n, pair, par, ahead):
                for st in range(STEPS):
                    t1 = STEPS * n + st + 1
                    bank = gates[st % 2]
                    act.wait_ge(s["gates_done"], t1)
                    a(sig[:, 0:2, :].rearrange("p a b -> p (a b)"), bank[:, 0:2 * P], ACT.Sigmoid)\
                        .then_inc(s["if_ready"], 1)
                    a(gcand, bank[:, 3 * P:4 * P], ACT.Tanh).then_inc(s["g_ready"], 1)
                    a(sig[:, 2, :], bank[:, 2 * P:3 * P], ACT.Sigmoid).then_inc(s["o_ready"], 1)
                    act.wait_ge(s["c_ready"], t1)
                    a(tcell, cell, ACT.Tanh).then_inc(s["tc_ready"], 1)
                    if ahead >= 2 and st == 1:
                        soft_first(n + 2)
                    if ahead >= 2 and st == 2:
                        soft_last(n + 2)

            tiles(act, tile)

        @block.vector
        def _(dve):
            v = nc.vector

            def convolve(n, pair, par, lots):
                if 0 in lots:
                    dve.wait_ge(x_landed[par], 16 * (pair + 1))
                    if not (isinstance(n, int) and n < 2):
                        dve.wait_ge(s["proj_done"], n - 1)
                for i in lots:
                    for k in range(KD):
                        src = xin[par][:, k, i * B:i * B + TILE]
                        if i == 0:
                            v.tensor_scalar(conv[par][:, k, :], src, taps[:, k, 0:1], conv_b[:, k:k + 1], ALU.mult,
                                            ALU.add).then_inc(s["conv_done"], 1)
                        else:
                            dve.wait_ge(s["conv_done"], KD * TAPS * n + KD * (i - 1) + k + 1)
                            v.scalar_tensor_tensor(out=conv[par][:, k, :], in0=src, scalar=taps[:, k, i:i + 1],
                                                   in1=conv[par][:, k, :], op0=ALU.mult,
                                                   op1=ALU.add).then_inc(s["conv_done"], 1)

            def scan(n):
                dve.wait_ge(s["soft_ready"], n + 1)
                v.tensor_tensor(drive_b, z_relu, z_ln, ALU.add).then_inc(s["bt_ready"], 1)
                dve.wait_ge(s["bt_ready"], n + 1)
                dve.wait_ge(s["u_done"], n + 1)
                v.scalar_tensor_tensor(out=drive.rearrange("p b t -> p t b"),
                                       in0=u_ps[0:N_STATE, 0:TILE].rearrange("p (t b) -> p t b", b=B),
                                       scalar=bs, in1=drive_b.rearrange("p (t b) -> p t b", b=B), op0=ALU.add,
                                       op1=ALU.mult).then_inc(s["drive_ready"], 1)
                dve.wait_ge(s["drive_ready"], n + 1)
                v.scalar_tensor_tensor(out=drive[:, :, 0], in0=state[:, :, STEPS - 1], scalar=decay,
                                       in1=drive[:, :, 0], op0=ALU.mult, op1=ALU.add).then_inc(s["carry_added"], 1)
                dve.wait_ge(s["carry_added"], n + 1)
                v.tensor_tensor_scan(state.rearrange("p b t -> p (b t)"), decays.rearrange("p b t -> p (b t)"),
                                     drive.rearrange("p b t -> p (b t)"), 0.0, ALU.mult,
                                     ALU.add).then_inc(s["state_ready"], 1)
                dve.wait_ge(s["state_ready"], n + 1)
                dve.wait_ge(s["gate_c_ready"], n + 1)
                v.scalar_tensor_tensor(out=y.rearrange("p (t b) -> p t b", b=B),
                                       in0=state.rearrange("p b t -> p t b"), scalar=delta,
                                       in1=c_gate.rearrange("p (t b) -> p t b", b=B), op0=ALU.mult,
                                       op1=ALU.mult).then_inc(s["y_ready"], 1)

            def add_block(n, par):
                dve.wait_ge(s["o_done"], n + 1)
                if not (isinstance(n, int) and n < 2):
                    dve.wait_ge(s["hT_free"], STEPS * n - STEPS + 2)
                for m in range(KD):
                    v.scalar_tensor_tensor(out=x1[par][:, m, :], in0=o_ps[:, m * P:(m + 1) * P],
                                           scalar=bo[:, m:m + 1], in1=xin[par][:, m, HALO:], op0=ALU.add,
                                           op1=ALU.add).then_inc(s["x1_ready"], 1)

            def keep_inputs(n, par, q):
                dve.wait_ge(s["xw_summed"], KD * n + q + 1)
                cols = slice(q * GCOLS, (q + 1) * GCOLS)
                v.tensor_tensor(xw[par][:, cols], xw_ps[q % 2][:, :], xw_bias[:, cols],
                                ALU.add).then_inc(s["xw_ready"], 1)

            dve.wait_ge(s["weights_landed"], 16 * len(weights))
            dve.wait_ge(s["small_ready"], 4)
            v.scalar_tensor_tensor(out=delta, in0=dt_log, scalar=0.0, in1=scratch[:, 0:1], op0=ALU.max,
                                   op1=ALU.add).then_inc(s["small_ready"], 1)
            v.scalar_tensor_tensor(out=scratch[:, 2:3], in0=a_log, scalar=0.0, in1=scratch[:, 1:2], op0=ALU.max,
                                   op1=ALU.add).then_inc(s["small_ready"], 1)
            dve.wait_ge(s["small_ready"], 6)
            v.tensor_tensor(scratch[:, 3:4], delta, scratch[:, 2:3], ALU.mult).then_inc(s["small_ready"], 1)
            dve.wait_ge(s["small_ready"], 7)
            v.tensor_scalar(decay, scratch[:, 3:4], -1.0, 1.0, ALU.mult, ALU.add).then_inc(s["small_ready"], 1)
            dve.wait_ge(s["small_ready"], 8)
            dve.wait_ge(s["pick_made"], 3)
            flat = decays.rearrange("p b t -> p (b t)")
            v.tensor_scalar(flat, flat, decay, None, ALU.mult).then_inc(s["small_ready"], 1)
            dve.wait_ge(s["small_ready"], 9)
            dve.wait_ge(s["bufs_zeroed"], 4)
            convolve(0, 0, 0, range(TAPS))
            convolve(1, 0, 1, range(TAPS))
            for n in range(2):
                scan(n)
                add_block(n, n)
            for q in range(KD):
                keep_inputs(0, 0, q)
            convolve(2, 1, 0, range(TAPS))

            def tile(n, pair, par, ahead):
                for st in range(STEPS):
                    t1 = STEPS * n + st + 1
                    dve.wait_ge(s["if_ready"], t1)
                    v.tensor_tensor(term_f, sig[:, 1, :], cell, ALU.mult).then_inc(s["terms_ready"], 1)
                    dve.wait_ge(s["g_ready"], t1)
                    v.tensor_tensor(term_i, sig[:, 0, :], gcand, ALU.mult).then_inc(s["terms_ready"], 1)
                    dve.wait_ge(s["terms_ready"], 2 * t1)
                    v.tensor_tensor(cell, term_f, term_i, ALU.add).then_inc(s["c_ready"], 1)
                    dve.wait_ge(s["o_ready"], t1)
                    dve.wait_ge(s["tc_ready"], t1)
                    v.tensor_tensor(hid, sig[:, 2, :], tcell, ALU.mult).then_inc(s["h_ready"], 1)
                    dve.wait_ge(s["hT_turned"], t1)
                    dve.wait_ge(s["hT_free"], t1)
                    v.tensor_copy(hT[(st + 1) % 2].rearrange("p k b -> p (k b)"), turned[:, 0:P])\
                        .then_inc(s["hT_ready"], 1)
                    if ahead >= 1 and st % 2 == 1:
                        keep_inputs(n + 1, 1 - par, st // 2)
                    if ahead >= 2 and st == 3:
                        scan(n + 2)
                    if ahead >= 2 and st == 7:
                        add_block(n + 2, par)
                    if ahead >= 3:
                        convolve(n + 3, pair + 1 + par, 1 - par, (2 * st, 2 * st + 1))

            tiles(dve, tile)


def mix_phase(nc, ctx, ins, carve, banks, keep, x2_d, r_d, rows_d):
    ident, cond, slot = keep["ident"], keep["cond"], keep["slot"]
    wr = carve(KD, D)
    maa_k, maa_r = carve(KD), carve(KD)
    win = [carve(KD, B + MIX) for _ in range(2)]
    shift = [carve(KD, MIX) for _ in range(2)]
    xk = [carve(KD, MIX) for _ in range(2)]
    xr = [carve(KD, MIX) for _ in range(2)]
    gate = [carve(KD, MIX) for _ in range(2)]
    rows = [carve(SUB, D) for _ in range(2)]
    index = [[carve(1).bitcast(I32) for _ in range(SUB)] for _ in range(2)]
    r_ps, t_ps = banks[0:4], banks[4:8]
    names = ["weights_landed", "halo_ready", "shift_ready", "xk_ready", "xr_ready", "r_summed", "gate_ready",
             "rows_turned", "rows_ready", "index_ready", "passed"]
    s = {n: ctx.enter_context(nc.semaphore("mx_" + n)) for n in names}
    landed, gate_stored, scattered = ([ctx.enter_context(nc.semaphore(f"mx_{n}{i}")) for i in range(2)]
                                      for n in ("x2_landed", "gate_stored", "scattered"))

    def tiles(eng, body):
        body(0, 0, 0, True)
        body(1, 0, 1, True)
        with eng.Fori(1, NMIX // 2) as pair:
            body(2 * pair, pair, 0, False)
            body(2 * pair + 1, pair, 1, False)

    x2v, rv = x2_d.rearrange("c p n -> p c n"), r_d.rearrange("c p n -> p c n")
    with nc.Block() as block:
        @block.sync
        def _(sp):
            sp.dma_start(wr, ins["wr"]).then_inc(s["weights_landed"], 16)
            sp.dma_start(maa_k, ins["maa_k"]).then_inc(s["weights_landed"], 16)
            sp.dma_start(maa_r, ins["maa_r"]).then_inc(s["weights_landed"], 16)

            def tile(n, pair, par, first):
                if not first:
                    sp.wait_ge(s["xr_ready"], KD * (n - 1))
                if first and par == 0:
                    sp.dma_start(win[0][:, :, B:], x2v[:, :, 0:MIX]).then_inc(landed[0], 16)
                else:
                    sp.dma_start(win[par], x2v[:, :, bass.ds(n * MIX - B, B + MIX)]).then_inc(landed[par], 16)

            tiles(sp, tile)
            for par in range(2):
                sp.wait_ge(landed[par], 16 * NMIX // 2)

        @block.gpsimd
        def _(pool):
            nc.gpsimd.tensor_copy(win[0][:, :, 0:B], cond).then_inc(s["halo_ready"], 1)

            def tile(n, pair, par, first):
                if not first:
                    pool.wait_ge(scattered[par], 16 * SUB * pair)
                    pool.sem_inc(s["passed"], 1)
                for u in range(SUB):
                    nc.gpsimd.tensor_copy(index[par][u], slot[:, bass.ds(n * SUB + u, 1)])\
                        .then_inc(s["index_ready"], 1)
                pool.wait_ge(s["index_ready"], SUB * n + SUB)
                for u in range(SUB):
                    pool.wait_ge(s["rows_ready"], SUB * n + u + 1)
                    pool.sem_inc(s["passed"], 1)
                    nc.gpsimd.indirect_dma_start(
                        out=rows_d, out_offset=bass.IndirectOffsetOnAxis(ap=index[par][u], axis=0),
                        in_=rows[par][:, u, :], in_offset=None, bounds_check=E * CAP - 1,
                        oob_is_err=False).then_inc(scattered[par], 16)

            tiles(pool, tile)
            for par in range(2):
                pool.wait_ge(scattered[par], 16 * SUB * (NMIX // 2))

        @block.tensor
        def _(pe):
            pe.wait_ge(s["weights_landed"], 48)

            def tile(n, pair, par, first):
                for u in range(SUB):
                    pe.wait_ge(s["xk_ready"], KD * (n + 1))
                    if not (first and par == 0):
                        pe.wait_ge(s["rows_ready"], SUB * n + u - SUB + 1)
                    for k in range(KD):
                        last = nc.tensor.transpose(t_ps[u][:, k * P:(k + 1) * P], xk[par][:, k, u * P:(u + 1) * P],
                                                   ident)
                    last.then_inc(s["rows_turned"], 1)
                pe.wait_ge(s["xr_ready"], KD * (n + 1))
                for m in range(KD):
                    if not (first and par == 0):
                        pe.wait_ge(s["gate_ready"], KD * n + m - KD + 1)
                    for k in range(KD):
                        last = nc.tensor.matmul(r_ps[m][:, :], wr[:, k, m * P:(m + 1) * P], xr[par][:, k, :],
                                                start=k == 0, stop=k == KD - 1)
                    last.then_inc(s["r_summed"], 1)

            tiles(pe, tile)

        @block.scalar
        def _(act):
            def tile(n, pair, par, first):
                if not first:
                    act.wait_ge(scattered[par], 16 * SUB * pair)
                for u in range(SUB):
                    act.wait_ge(s["rows_turned"], SUB * n + u + 1)
                    nc.scalar.activation(rows[par][:, u, :], t_ps[u][:, :], ACT.Copy).then_inc(s["rows_ready"], 1)
                if not first:
                    act.wait_ge(gate_stored[par], 16 * pair)
                for m in range(KD):
                    act.wait_ge(s["r_summed"], KD * n + m + 1)
                    nc.scalar.activation(gate[par][:, m, :], r_ps[m][:, :], ACT.Sigmoid).then_inc(s["gate_ready"], 1)
                act.wait_ge(s["gate_ready"], KD * n + KD)
                act.dma_start(rv[:, :, bass.ds(n * MIX, MIX)], gate[par]).then_inc(gate_stored[par], 16)

            tiles(act, tile)
            for par in range(2):
                act.wait_ge(gate_stored[par], 16 * NMIX // 2)

        @block.vector
        def _(dve):
            v = nc.vector
            dve.wait_ge(s["weights_landed"], 48)
            dve.wait_ge(s["halo_ready"], 1)

            def tile(n, pair, par, first):
                dve.wait_ge(landed[par], 16 * (pair + 1))
                v.tensor_tensor(shift[par], win[par][:, :, 0:MIX], win[par][:, :, B:], ALU.subtract)\
                    .then_inc(s["shift_ready"], 1)
                dve.wait_ge(s["shift_ready"], n + 1)
                for dst, maa, done, used, per in ((xk, maa_k, "xk_ready", "rows_turned", SUB),
                                                  (xr, maa_r, "xr_ready", "r_summed", KD)):
                    if not first:
                        dve.wait_ge(s[used], per * (n - 1))
                    for k in range(KD):
                        v.scalar_tensor_tensor(out=dst[par][:, k, :], in0=shift[par][:, k, :],
                                               scalar=maa[:, k:k + 1], in1=win[par][:, k, B:], op0=ALU.mult,
                                               op1=ALU.add).then_inc(s[done], 1)

            tiles(dve, tile)


def expert_phase(nc, ctx, ins, carve, banks, keep, rows_d, y_d):
    ident = keep["ident"]
    NS = CAP // P
    wk = [carve(KD, FF) for _ in range(2)]
    wv = [carve(KF, D) for _ in range(2)]
    rows = [carve(NS, D) for _ in range(2)]
    xT = [carve(KD, CAP) for _ in range(2)]
    relu = [carve(CAP) for _ in range(2)]
    hid = carve(KF, CAP)
    y = [carve(NS, D) for _ in range(2)]
    t_ps, h_ps, y_ps = banks[0:2], banks[2:6], banks[6:8]
    names = ["turned", "xT_ready", "h_summed", "relu_ready", "hid_ready", "y_summed", "y_ready"]
    s = {n: ctx.enter_context(nc.semaphore("ex_" + n)) for n in names}
    landed, wk_landed, wv_landed, stored = ([ctx.enter_context(nc.semaphore(f"ex_{n}{i}")) for i in range(2)]
                                            for n in ("rows_landed", "wk_landed", "wv_landed", "y_stored"))

    def experts(eng, body):
        body(0, 0, 0, True)
        body(1, 0, 1, True)
        with eng.Fori(1, E // 2) as pair:
            body(2 * pair, pair, 0, False)
            body(2 * pair + 1, pair, 1, False)

    with nc.Block() as block:
        @block.sync
        def _(sp):
            def one(e, pair, par, first):
                if not first:
                    sp.wait_ge(s["turned"], KD * (e - 1))
                src = rows_d[bass.ds(e * CAP, CAP), :].rearrange("(a p) d -> p a d", p=P)
                sp.dma_start(rows[par], src).then_inc(landed[par], 16)
                if not first:
                    sp.wait_ge(s["h_summed"], KF * (e - 1))
                sp.dma_start(wk[par], ins["wk"][:, bass.ds(e * KD, KD), :]).then_inc(wk_landed[par], 16)
                if not first:
                    sp.wait_ge(s["y_summed"], NS * (e - 1))
                sp.dma_start(wv[par], ins["wv"][:, bass.ds(e * KF, KF), :]).then_inc(wv_landed[par], 16)

            experts(sp, one)

        @block.gpsimd
        def _(pool):
            def one(e, pair, par, first):
                pool.wait_ge(s["y_ready"], NS * (e + 1))
                dst = y_d[bass.ds(e * CAP, CAP), :].rearrange("(a p) d -> p a d", p=P)
                pool.dma_start(dst, y[par]).then_inc(stored[par], 16)

            experts(pool, one)
            for par in range(2):
                pool.wait_ge(stored[par], 16 * E // 2)

        @block.tensor
        def _(pe):
            def one(e, pair, par, first):
                pe.wait_ge(landed[par], 16 * (pair + 1))
                for k in range(KD):
                    if not (first and par == 0 and k < 2):
                        pe.wait_ge(s["xT_ready"], KD * e + k - 1)
                    for a in range(NS):
                        last = nc.tensor.transpose(t_ps[k % 2][:, a * P:(a + 1) * P],
                                                   rows[par][:, a, k * P:(k + 1) * P], ident)
                    last.then_inc(s["turned"], 1)
                pe.wait_ge(wk_landed[par], 16 * (pair + 1))
                pe.wait_ge(s["xT_ready"], KD * e + KD)
                for f in range(KF):
                    if not (first and par == 0 and f < 4):
                        pe.wait_ge(s["relu_ready"], KF * e + f - 3)
                    for k in range(KD):
                        last = nc.tensor.matmul(h_ps[f % 4][:, :], wk[par][:, k, f * P:(f + 1) * P], xT[par][:, k, :],
                                                start=k == 0, stop=k == KD - 1)
                    last.then_inc(s["h_summed"], 1)
                pe.wait_ge(wv_landed[par], 16 * (pair + 1))
                pe.wait_ge(s["hid_ready"], KF * e + KF)
                for a in range(NS):
                    if not (first and par == 0 and a < 2):
                        pe.wait_ge(s["y_ready"], NS * e + a - 1)
                    for f in range(KF):
                        last = nc.tensor.matmul(y_ps[a % 2][:, :], hid[:, f, a * P:(a + 1) * P], wv[par][:, f, :],
                                                start=f == 0, stop=f == KF - 1)
                    last.then_inc(s["y_summed"], 1)

            experts(pe, one)

        @block.scalar
        def _(act):
            def one(e, pair, par, first):
                for f in range(KF):
                    act.wait_ge(s["h_summed"], KF * e + f + 1)
                    if not (first and par == 0 and f < 2):
                        act.wait_ge(s["hid_ready"], KF * e + f - 1)
                    nc.scalar.activation(relu[f % 2], h_ps[f % 4][:, :], ACT.Relu).then_inc(s["relu_ready"], 1)
                if not first:
                    act.wait_ge(stored[par], 16 * pair)
                for a in range(NS):
                    act.wait_ge(s["y_summed"], NS * e + a + 1)
                    nc.scalar.activation(y[par][:, a, :], y_ps[a % 2][:, :], ACT.Copy).then_inc(s["y_ready"], 1)

            experts(act, one)

        @block.vector
        def _(dve):
            def one(e, pair, par, first):
                for k in range(KD):
                    dve.wait_ge(s["turned"], KD * e + k + 1)
                    nc.vector.tensor_copy(xT[par][:, k, :], t_ps[k % 2][:, :]).then_inc(s["xT_ready"], 1)
                for f in range(KF):
                    dve.wait_ge(s["relu_ready"], KF * e + f + 1)
                    if not (first and par == 0) and f == 0:
                        dve.wait_ge(s["y_summed"], NS * e)
                    nc.vector.tensor_tensor(hid[:, f, :], relu[f % 2], relu[f % 2], ALU.mult)\
                        .then_inc(s["hid_ready"], 1)

            experts(dve, one)


def mask_phase(nc, ctx, ins, carve, banks, keep, x2_d, r_d, y_d, out):
    ident, cond, slot = keep["ident"], keep["cond"], keep["slot"]
    x3 = carve(KD, B, T)
    x2 = [carve(KD, P) for _ in range(2)]
    gate = [carve(KD, P) for _ in range(2)]
    rows = [carve(D) for _ in range(4)]
    index = [carve(1).bitcast(I32) for _ in range(4)]
    gated = [carve(KD, P) for _ in range(2)]
    ax = [carve(T + 1) for _ in range(2)]
    pi = [carve(T) for _ in range(2)]
    cum = carve(T)
    flag = carve(T + 1)
    places = carve(T + 1)
    masked = [carve(T) for _ in range(2)]
    final = [carve(T) for _ in range(2)]
    total, half, inv, pi_sum, limit, chosen, level, rv = [carve(2) for _ in range(8)]
    ones = carve(T)
    t_ps = banks[0:2]
    names = ["index_ready", "passed", "turned", "gated_ready", "x3_ready", "places_made", "abs_ready", "inv_ready", "pi_ready",
             "half_ready", "rv_ready", "limit_ready", "cum_ready", "chosen_ready", "level_ready", "masked_ready", "final_ready"]
    s = {n: ctx.enter_context(nc.semaphore("mk_" + n)) for n in names}
    gathered = [ctx.enter_context(nc.semaphore(f"mk_gathered{i}")) for i in range(4)]
    landed, stored = ([ctx.enter_context(nc.semaphore(f"mk_{n}{i}")) for i in range(2)] for n in ("landed", "stored"))
    QUAD = NTILE // 4
    NU = KD * B

    def tiles(eng, body):
        for i in range(4):
            body(i, 0, i, True)
        with eng.Fori(1, QUAD) as quad:
            for i in range(4):
                body(4 * quad + i, quad, i, False)

    def units(eng, body):
        for par in range(2):
            body(par, par, 0, "first")
        with eng.Fori(1, NU // 2 - 1) as pair:
            for par in range(2):
                body(2 * pair + par, par, pair, "mid")
        for par in range(2):
            body(NU - 2 + par, par, NU // 2 - 1, "last")

    x3_flat = x3.rearrange("p c b t -> p (c b t)")
    x2v, rv_d = x2_d.rearrange("c p n -> p c n"), r_d.rearrange("c p n -> p c n")
    cond_flat = cond.rearrange("p c b -> p (c b)")

    def x3_of(u):
        return x3_flat[:, bass.ds(u * T, T)]

    with nc.Block() as block:
        @block.sync
        def _(sp):
            def tile(n, quad, i, first):
                if not (first and i < 2):
                    sp.wait_ge(s["x3_ready"], n - 1)
                sp.dma_start(x2[i % 2], x2v[:, :, bass.ds(n * P, P)]).then_inc(landed[i % 2], 16)
                sp.dma_start(gate[i % 2], rv_d[:, :, bass.ds(n * P, P)]).then_inc(landed[i % 2], 16)

            tiles(sp, tile)

            def unit(u, par, pair, kind):
                sp.wait_ge(s["final_ready"], u + 1)
                sp.dma_start(out[:, bass.ds(u * T, T)], final[par]).then_inc(stored[par], 16)

            units(sp, unit)
            for par in range(2):
                sp.wait_ge(stored[par], 16 * NU // 2)

        @block.gpsimd
        def _(pool):
            g = nc.gpsimd
            g.iota(places, pattern=[[1, T + 1]], base=0, channel_multiplier=0,
                   allow_small_or_imprecise_dtypes=True).then_inc(s["places_made"], 1)
            for par in range(2):
                g.memset(ax[par][:, T:T + 1], 3.0e38).then_inc(s["places_made"], 1)
            g.memset(ones, 1.0).then_inc(s["places_made"], 1)

            def tile(n, quad, i, first):
                if not first:
                    pool.wait_ge(s["turned"], n - 3)
                    pool.sem_inc(s["passed"], 1)
                g.tensor_copy(index[i], slot[:, bass.ds(n, 1)]).then_inc(s["index_ready"], 1)
                pool.wait_ge(s["index_ready"], n + 1)
                pool.sem_inc(s["passed"], 1)
                g.indirect_dma_start(out=rows[i], out_offset=None, in_=y_d,
                                     in_offset=bass.IndirectOffsetOnAxis(ap=index[i], axis=0)
                                     ).then_inc(gathered[i], 16)

            tiles(pool, tile)

            def unit(u, par, pair, kind):
                pool.wait_ge(s["masked_ready"], u + 1)
                if kind != "first":
                    pool.wait_ge(stored[par], 16 * pair)
                g.tensor_tensor(final[par], masked[par], x3_of(u), ALU.add)\
                    .then_inc(s["final_ready"], 1)

            units(pool, unit)

        @block.tensor
        def _(pe):
            def tile(n, quad, i, first):
                pe.wait_ge(gathered[i], 16 * (quad + 1))
                if not (first and i < 2):
                    pe.wait_ge(s["gated_ready"], n - 1)
                for k in range(KD):
                    last = nc.tensor.transpose(t_ps[i % 2][:, k * P:(k + 1) * P], rows[i][:, k * P:(k + 1) * P], ident)
                last.then_inc(s["turned"], 1)

            tiles(pe, tile)

        @block.scalar
        def _(act):
            act.wait_ge(s["places_made"], 4)
            act.wait_ge(s["x3_ready"], NTILE)

            def absolute(u, par, kind):
                if kind != "first":
                    act.wait_ge(s["masked_ready"], u - 1)
                nc.scalar.activation(ax[par][:, 0:T], x3_of(u), ACT.Abs,
                                     accum_out=total[:, par:par + 1]).then_inc(s["abs_ready"], 1)

            def unit(u, par, pair, kind):
                if kind == "first" and par == 0:
                    absolute(0, 0, "first")
                act.wait_ge(s["inv_ready"], u + 1)
                if kind != "first":
                    act.wait_ge(s["masked_ready"], u - 1)
                nc.scalar.activation(pi[par], ax[par][:, 0:T], ACT.Exp, scale=inv[:, par:par + 1],
                                     accum_out=pi_sum[:, par:par + 1]).then_inc(s["pi_ready"], 1)
                if not (kind == "last" and par == 1):
                    absolute(u + 1, 1 - par, "first" if kind == "first" and par == 0 else "mid")

            units(act, unit)

        @block.vector
        def _(dve):
            v = nc.vector

            def tile(n, quad, i, first):
                par = i % 2
                dve.wait_ge(s["turned"], n + 1)
                dve.wait_ge(landed[par], 32 * (2 * quad + i // 2 + 1))
                v.tensor_tensor(gated[par].rearrange("p c n -> p (c n)"), t_ps[par][:, :],
                                gate[par].rearrange("p c n -> p (c n)"), ALU.mult).then_inc(s["gated_ready"], 1)
                dve.wait_ge(s["gated_ready"], n + 1)
                for k in range(KD):
                    dst = x3[:, k, :, bass.ds(n * STEPS, STEPS)].rearrange("p b t -> p t b")
                    last = v.tensor_tensor(dst, gated[par][:, k, :].rearrange("p (t b) -> p t b", b=B),
                                           x2[par][:, k, :].rearrange("p (t b) -> p t b", b=B), ALU.add)
                last.then_inc(s["x3_ready"], 1)

            tiles(dve, tile)
            dve.wait_ge(s["x3_ready"], NTILE)
            dve.wait_ge(s["places_made"], 4)

            def invert(u, par):
                c = slice(par, par + 1)
                dve.wait_ge(s["abs_ready"], u + 1)
                v.tensor_scalar(half[:, c], total[:, c], 0.5, None, ALU.mult).then_inc(s["half_ready"], 1)
                dve.wait_ge(s["half_ready"], u + 1)
                v.reciprocal(inv[:, c], half[:, c]).then_inc(s["inv_ready"], 1)

            def unit(u, par, pair, kind):
                c = slice(par, par + 1)
                if kind == "first" and par == 0:
                    invert(0, 0)
                rcol = cond_flat[:, bass.ds(u, 1)]
                v.tensor_scalar(rv[:, c], rcol, -0.001, None, ALU.add).then_inc(s["rv_ready"], 1)
                dve.wait_ge(s["pi_ready"], u + 1)
                v.tensor_tensor_scan(cum, ones, pi[par], 0.0, ALU.mult, ALU.add).then_inc(s["cum_ready"], 1)
                dve.wait_ge(s["rv_ready"], u + 1)
                v.tensor_tensor(limit[:, c], rv[:, c], pi_sum[:, c], ALU.mult).then_inc(s["limit_ready"], 1)
                if not (kind == "last" and par == 1):
                    invert(u + 1, 1 - par)
                dve.wait_ge(s["cum_ready"], u + 1)
                dve.wait_ge(s["limit_ready"], u + 1)
                v.tensor_scalar(flag[:, 0:T], cum, limit[:, c], None, ALU.is_le, ALU.add,
                                accum_out=chosen[:, c]).then_inc(s["chosen_ready"], 1)
                dve.wait_ge(s["chosen_ready"], u + 1)
                v.scalar_tensor_tensor(out=flag, in0=places, scalar=chosen[:, c], in1=ax[par], op0=ALU.is_equal,
                                       op1=ALU.mult, accum_out=level[:, c]).then_inc(s["level_ready"], 1)
                dve.wait_ge(s["level_ready"], u + 1)
                if kind != "first":
                    dve.wait_ge(s["final_ready"], u - 1)
                v.scalar_tensor_tensor(out=masked[par], in0=ax[par][:, 0:T], scalar=level[:, c],
                                       in1=x3_of(u), op0=ALU.is_ge, op1=ALU.mult).then_inc(s["masked_ready"], 1)

            units(dve, unit)


def kernel(**inputs):
    import numpy as _np
    import concourse.bacc as _bacc
    from concourse.bass_utils import run_bass_kernel_spmd as _run

    a = {k: _np.asarray(v) for k, v in inputs.items()}

    def gate_blocks(w):
        lead = w.shape[:-1]
        return _np.swapaxes(w.reshape(lead + (4, KD, P)), -3, -2).reshape(lead + (4 * H,))

    arrays = {
        "xT": a["x"].transpose(2, 1, 0).reshape(KD, P, NTOK),
        "ids": a["itok_BxS_2_50255"].reshape(P, NTOK // P),
        "condT": a["cond_1024"].T,
        "Wh": gate_blocks(a["L1_cond_Wh"]), "Wx": gate_blocks(a["L1_cond_Wx"]), "b": gate_blocks(a["L1_cond_b"]),
        "Wp": a["L0_cond_Wp"], "Ws": a["L0_cond_Ws"], "Wo": a["L0_cond_Wo"], "conv_b": a["L0_cond_conv_b"],
        "bo": a["L0_cond_bo"], "bp": a["L0_cond_bp"], "bs": a["L0_cond_bs"], "A_log": a["L0_cond_A_log"],
        "dt_log": a["L0_cond_dt_log"], "wr": a["L2_cond_w_recept"].T, "maa_k": a["L2_cond_time_maa_k"],
        "maa_r": a["L2_cond_time_maa_r"], "wk": a["L2_cond_w_key"].reshape(E * D, FF),
        "wv": a["L2_cond_w_value"].reshape(E * FF, D),
    }
    arrays = {k: _np.ascontiguousarray(v) for k, v in arrays.items()}
    nc = _bacc.Bacc("TRN2", target_bir_lowering=False, num_devices=1)
    ins = {k: nc.dram_tensor("in_" + k, v.shape, mybir.dt.from_np(v.dtype), kind="ExternalInput").ap()
           for k, v in arrays.items()}
    ins["xT"] = ins["xT"].rearrange("c p n -> p c n")
    for k in ("condT", "Wh", "Wx", "Wp", "Ws", "wr", "wk", "wv"):
        ins[k] = ins[k].rearrange("(k p) n -> p k n", p=P)
    for k in ("conv_b", "bo", "maa_k", "maa_r"):
        ins[k] = ins[k].rearrange("(k p) -> p k", p=P)
    for k in ("bs", "A_log", "dt_log"):
        ins[k] = ins[k].rearrange("(p o) -> p o", o=1)
    ins["bp"] = ins["bp"].rearrange("(h p o) -> h p o", h=2, o=1)
    out = nc.dram_tensor("out_0", (P, KD * B * T), F32, kind="ExternalOutput").ap()
    with nc.allow_non_contiguous_dma(reason="a few per-feature parameter columns"):
        build(nc, ins, out)
    r = _run(nc, [{"in_" + k: v for k, v in arrays.items()}], core_ids=[0])
    got = r.results[0]["out_0"].reshape(P, KD, B, T)
    return _np.ascontiguousarray(got.transpose(2, 3, 1, 0)).reshape(B, T, D)
```

```python
from contextlib import ExitStack

import concourse.bass as bass
from concourse import mybir

F32 = mybir.dt.float32
I32 = mybir.dt.int32
F32R = mybir.dt.float32r
ALU = mybir.AluOpType
ACT = mybir.ActivationFunctionType
AX = mybir.AxisListType

P = 128
B, T, D = 16, 512, 512
KD = D // P
H = 512
N_STATE = 64
TAPS = 16
NTOK = B * T
STEPS = 8
TILE = STEPS * B
NTILE = T // STEPS
HALO = (TAPS - 1) * B
WIN = HALO + TILE
E = 16
FF = 1024
KF = FF // P
CAP = max(4, NTOK // E)
GCOLS = 4 * P
MIX = 512
NMIX = NTOK // MIX
SUB = MIX // P
HASH = 5099 % E


class Carver:
    SLAB = 212800

    def __init__(self, nc, ctx):
        self.nc, self.top, self.last, self.made = nc, 0, 0, 0
        self.base = -(-nc.sbuf_base // 32) * 32
        ctx.enter_context(nc.sbuf_tensor("slab", [P, self.SLAB // 4], F32))

    def __call__(self, *shape, dt=F32, at=None):
        size = 4
        for n in shape:
            size *= n
        self.last = self.top if at is None else at
        if at is None:
            self.top += -(-size // 32) * 32
        assert self.top <= self.SLAB, self.top
        self.made += 1
        return self.nc.alloc_sbuf_tensor_at(f"buf{self.made}", [P, *shape], dt, offset=self.base + self.last)[:]


def build(nc, ins, out):
    x2_d = nc.dram_tensor("x2_scratch", (KD, P, NTOK), F32, kind="Internal").ap()
    xw_d = nc.dram_tensor("input_gates_scratch", (2, KD, TILE, GCOLS), F32, kind="Internal").ap()
    r_d = nc.dram_tensor("gate_scratch", (KD, P, NTOK), F32, kind="Internal").ap()
    slot_d = nc.dram_tensor("slot_scratch", (NTOK,), I32, kind="Internal").ap()
    rows_d = nc.dram_tensor("expert_in_scratch", (E * CAP, D), F32, kind="Internal").ap()
    y_d = nc.dram_tensor("expert_out_scratch", (E * CAP + 1, D), F32, kind="Internal").ap()
    with ExitStack() as ctx:
        carve = Carver(nc, ctx)
        banks = [ctx.enter_context(nc.psum_tensor(f"bank{i}", [P, 512], F32)) for i in range(8)]

        ident = carve(P)
        cond = carve(KD, B)
        slot = carve(NTILE).bitcast(I32)
        keep = dict(ident=ident, cond=cond, slot=slot)
        base = carve.top
        route_phase(nc, ctx, ins, carve, banks, keep, slot_d, rows_d, y_d)
        carve.top = base
        recur_phase(nc, ctx, ins, carve, banks, keep, x2_d, xw_d)
        carve.top = base
        mix_phase(nc, ctx, ins, carve, banks, keep, x2_d, r_d, rows_d)
        carve.top = base
        expert_phase(nc, ctx, ins, carve, banks, keep, rows_d, y_d)
        carve.top = base
        mask_phase(nc, ctx, ins, carve, banks, keep, x2_d, r_d, y_d, out)


def route_phase(nc, ctx, ins, carve, banks, keep, slot_d, rows_d, y_d):
    SEG = NTOK // P
    ident, cond, slot = keep["ident"], keep["cond"], keep["slot"]
    zeros = carve(4 * D)
    ids = carve(SEG).bitcast(I32)
    hashed = carve(SEG).bitcast(I32)
    expert = carve(SEG)
    expert_no = carve(E, SEG)
    slot_base = carve(E, SEG)
    onehot = carve(E, SEG)
    segment = carve(E, SEG)
    count = carve(E, SEG)
    before = carve(P)
    offset = carve(E)
    slot_f = carve(SEG)
    slot_i = carve(SEG).bitcast(I32)
    psum_off = banks[0]

    def sem(name):
        return ctx.enter_context(nc.semaphore(name))

    ids_landed, cond_landed = sem("rt_ids_landed"), sem("rt_cond_landed")
    zeroed, consts, steps = sem("rt_zeroed"), sem("rt_consts"), sem("rt_vector_steps")
    zero_stored, offsets_made = sem("rt_zero_stored"), sem("rt_offsets_made")
    slots_stored, slots_landed = sem("rt_slots_stored"), sem("rt_slots_landed")
    NZERO = E * CAP // (4 * P)
    with nc.Block() as block:
        @block.sync
        def _(sp):
            sp.dma_start(ids, ins["ids"]).then_inc(ids_landed, 16)
            sp.dma_start(cond, ins["condT"]).then_inc(cond_landed, 16)
            sp.wait_ge(zeroed, 1)
            for z in range(NZERO):
                sp.dma_start(rows_d[z * 4 * P:(z + 1) * 4 * P, :].rearrange("(p r) d -> p (r d)", r=4),
                             zeros).then_inc(zero_stored, 16)
            sp.dma_start(y_d[E * CAP:E * CAP + 1, :], zeros[0:1, 0:D]).then_inc(zero_stored, 16)
            sp.wait_ge(steps, 13)
            sp.dma_start(slot_d.rearrange("(p i) -> p i", p=P), slot_i).then_inc(slots_stored, 16)
            sp.wait_ge(slots_stored, 16)
            src = slot_d.rearrange("(b c t) -> t b c", b=B, t=STEPS)
            for t in range(STEPS):
                sp.dma_start(slot[t * B:(t + 1) * B, :], src[t], allow_slow_non_contiguous=True).then_inc(slots_landed, 16)
            sp.wait_ge(slots_landed, 16 * STEPS)
            sp.wait_ge(zero_stored, 16 * (NZERO + 1))
            sp.wait_ge(cond_landed, 16)

        @block.gpsimd
        def _(pool):
            nc.gpsimd.memset(zeros, 0.0).then_inc(zeroed, 1)
            nc.gpsimd.memset(ident, 0.0).then_inc(consts, 1)
            nc.gpsimd.memset(before, 0.0).then_inc(consts, 1)
            nc.gpsimd.memset(segment, 1.0).then_inc(consts, 1)
            nc.gpsimd.iota(expert_no, pattern=[[1, E], [0, SEG]], base=0, channel_multiplier=0,
                           allow_small_or_imprecise_dtypes=True).then_inc(consts, 1)
            nc.gpsimd.iota(slot_base, pattern=[[CAP, E], [0, SEG]], base=-1 - E * CAP, channel_multiplier=0,
                           allow_small_or_imprecise_dtypes=True).then_inc(consts, 1)
            pool.wait_ge(consts, 5)
            nc.gpsimd.affine_select(out=ident, in_=ident, compare_op=ALU.not_equal, fill=1.0, base=0,
                                    pattern=[[-1, P]], channel_multiplier=1).then_inc(consts, 1)
            nc.gpsimd.affine_select(out=before, in_=before, compare_op=ALU.is_ge, fill=1.0, base=0,
                                    pattern=[[-1, P]], channel_multiplier=1).then_inc(consts, 1)
            nc.gpsimd.memset(segment[:, :, 0:1], 0.0).then_inc(consts, 1)

        @block.tensor
        def _(pe):
            pe.wait_ge(consts, 8)
            pe.wait_ge(steps, 6)
            nc.tensor.matmul(psum_off[:, 0:E], before, count[:, :, SEG - 1], start=True,
                             stop=True).then_inc(offsets_made, 1)

        @block.vector
        def _(dve):
            v = nc.vector
            dve.wait_ge(ids_landed, 16)
            v.tensor_scalar(hashed, ids, E - 1, None, ALU.bitwise_and).then_inc(steps, 1)
            dve.wait_ge(steps, 1)
            v.tensor_scalar(ids, hashed, float(HASH), None, ALU.mult).then_inc(steps, 1)
            dve.wait_ge(steps, 2)
            v.tensor_scalar(hashed, ids, E - 1, None, ALU.bitwise_and).then_inc(steps, 1)
            dve.wait_ge(steps, 3)
            v.tensor_copy(expert, hashed).then_inc(steps, 1)
            dve.wait_ge(steps, 4)
            dve.wait_ge(consts, 8)
            v.tensor_tensor(onehot, expert.unsqueeze(1).broadcast_to([P, E, SEG]), expert_no,
                            ALU.is_equal).then_inc(steps, 1)
            dve.wait_ge(steps, 5)
            v.tensor_tensor_scan(count.rearrange("p e i -> p (e i)"), segment.rearrange("p e i -> p (e i)"),
                                 onehot.rearrange("p e i -> p (e i)"), 0.0, ALU.mult, ALU.add).then_inc(steps, 1)
            dve.wait_ge(offsets_made, 1)
            v.tensor_copy(offset, psum_off[:, 0:E]).then_inc(steps, 1)
            dve.wait_ge(steps, 7)
            v.tensor_tensor(count, count, offset.unsqueeze(2).broadcast_to([P, E, SEG]),
                            ALU.add).then_inc(steps, 1)
            dve.wait_ge(steps, 8)
            v.scalar_tensor_tensor(out=onehot, in0=count, scalar=float(CAP), in1=onehot, op0=ALU.is_le,
                                   op1=ALU.mult).then_inc(steps, 1)
            v.tensor_tensor(count, count, slot_base, ALU.add).then_inc(steps, 1)
            dve.wait_ge(steps, 10)
            v.tensor_tensor(count, count, onehot, ALU.mult).then_inc(steps, 1)
            dve.wait_ge(steps, 11)
            v.tensor_reduce(slot_f, count.rearrange("p e i -> p i e"), AX.X, ALU.add).then_inc(steps, 1)
            dve.wait_ge(steps, 12)
            v.tensor_scalar(slot_i, slot_f, float(E * CAP), None, ALU.add).then_inc(steps, 1)


def recur_phase(nc, ctx, ins, carve, banks, keep, x2_d, xw_d):
    ident, cond = keep["ident"], keep["cond"]
    taps = cond
    wh = carve(KD, 4 * H)
    wx_hi = carve(KD, 4 * H, dt=F32R)
    wx_lo = carve(KD, 4 * H, dt=F32R)
    wx_raw = carve(KD, 4 * H, at=carve.last)
    xw_bias = carve(KD, GCOLS)
    xw = carve(KD, GCOLS)
    laid = [carve(STEPS, GCOLS) for _ in range(2)]
    window = [carve(KD, WIN) for _ in range(2)]
    center = [carve(KD, TILE) for _ in range(2)]
    conv = [carve(KD, TILE) for _ in range(2)]
    x1 = [carve(KD, TILE) for _ in range(2)]
    x1_hi, x1_lo = ([carve(KD, TILE, dt=F32R) for _ in range(2)] for _ in range(2))
    x2 = [carve(KD, TILE) for _ in range(2)]
    wp = carve(KD, 2 * N_STATE)
    ws = carve(KD, N_STATE)
    wo = carve(D)[0:N_STATE + 1]
    conv_b = carve(KD)
    bp_b, bp_c, bs, a_log, dt_log, delta, decay = [carve(1)[0:N_STATE] for _ in range(7)]
    scratch = carve(8)[0:N_STATE]
    decays = carve(B, STEPS)[0:N_STATE]
    hT = [carve(KD, 32) for _ in range(2)]
    pre_ifg, pre_o = carve(3 * P), carve(P)
    sig_if, sig_o = carve(2, P), carve(P)
    gcand, cell, term_f, term_i, tanh_cT = [carve(P) for _ in range(5)]
    c_gate, z_abs, z_exp, z_ln, z_relu, drive_b = [carve(TILE)[0:N_STATE] for _ in range(6)]
    y = carve(TILE)[0:N_STATE + 1]
    drive = carve(B, STEPS)[0:N_STATE]
    state = carve(B, STEPS)[0:N_STATE]
    ifg_ps, o_gate_ps, cell_turned, o_turned = banks[0:4]
    xw_ps = banks[4:6]
    proj_ps, u_ps, out_ps = banks[6][:, 0:TILE], banks[6][0:N_STATE, TILE:2 * TILE], banks[7]

    names = ["weights_landed", "wx_landed", "wx_hi_ready", "wx_ready", "bufs_zeroed", "y_ones",
             "small_ready", "conv_done", "proj_done", "u_done", "gate_c_ready", "soft_exp", "soft_ready",
             "bt_ready", "drive_ready", "carry_added", "state_ready", "y_ready", "out_done", "x1_ready",
             "x1_hi_ready", "x1_split", "hT_free", "hT_ready", "c_turned", "o_turned", "ifg_done", "o_done", "pre_if_ready",
             "pre_g_ready", "pre_o_ready", "if_ready", "g_ready", "o_ready", "terms_ready", "c_ready",
             "tc_ready", "xw_summed", "xw_ready", "soft_abs", "sp_passed", "pool_passed"]
    s = {n: ctx.enter_context(nc.semaphore("rc_" + n)) for n in names}
    window_landed, center_landed, laid_landed, x2_stored, xw_stored = (
        [ctx.enter_context(nc.semaphore(f"rc_{n}{i}")) for i in range(2)]
        for n in ("window_landed", "center_landed", "laid_landed", "x2_stored", "xw_stored"))
    x_dram = ins["xT"]
    NLOOP = (NTILE - 4) // 2
    weights = [(taps, ins["condT"]), (conv_b, ins["conv_b"]),
               (wp, ins["Wp"]), (ws, ins["Ws"]), (wo[0:N_STATE], ins["Wo"]), (wo[N_STATE:], ins["bo"]),
               (bp_b, ins["bp"][0]), (bp_c, ins["bp"][1]), (bs, ins["bs"]),
               (a_log, ins["A_log"]), (dt_log, ins["dt_log"]),
               (xw_bias, ins["b"].partition_broadcast(P).rearrange("p (k n) -> p k n", k=KD)), (wh, ins["Wh"])]
    PRODUCTS = [5, 5, 9, 9, 9, 9, 2, 0]
    BEFORE_CELL, BEFORE_O = 4, 1
    KEEP_AT = {2: 0, 3: 1, 4: 2, 6: 3}
    PROJECT_AT, INPUTS_AT, SOFT_AT, SCAN_AT, OUTPUTS_AT = 0, 1, 0, 6, 7

    def tiles(eng, body):
        for n in range(2):
            body(n, 0, n, 3)
        with eng.Fori(1, NLOOP) as pair:
            body(2 * pair, pair, 0, 3)
            body(2 * pair + 1, pair, 1, 3)
        for n in range(2 * NLOOP, NTILE):
            body(n, n // 2, n % 2, min(3, NTILE - 1 - n))

    def later(n, first):
        return not (isinstance(n, int) and n < first)

    with nc.Block() as block:
        @block.sync
        def _(sp):
            def load_center(m, par):
                if later(m, 2):
                    sp.wait_ge(s["x1_ready"], m - 1)
                    sp.sem_inc(s["sp_passed"], 1)
                sp.dma_start(center[par], x_dram[:, :, bass.ds(m * TILE, TILE)]).then_inc(center_landed[par], 16)

            def load_window(m, par):
                if later(m, 2):
                    sp.wait_ge(s["conv_done"], KD * TAPS * (m - 1))
                sp.dma_start(window[par], x_dram[:, :, bass.ds(m * TILE - HALO, WIN)])\
                    .then_inc(window_landed[par], 16)

            def lay_out(m, par):
                def out(q):
                    sp.wait_ge(s["xw_ready"], KD * m + q + 1)
                    sp.dma_start(xw_d[par, q], xw[:, q, :]).then_inc(xw_stored[q % 2], 16)

                def back(q):
                    sp.wait_ge(xw_stored[q % 2], 32 * m + 16 * (q // 2) + 16)
                    sp.dma_start(laid[par][32 * q:32 * q + B, :, :],
                                 xw_d[par, q].rearrange("(t b) n -> b t n", b=B)).then_inc(laid_landed[par], 16)

                out(0)
                for q in range(1, KD):
                    out(q)
                    back(q - 1)
                back(KD - 1)

            sp.wait_ge(s["bufs_zeroed"], 6)
            for dst, src in weights[:2]:
                sp.dma_start(dst, src).then_inc(s["weights_landed"], 16)
            sp.dma_start(window[0][:, :, HALO:], x_dram[:, :, 0:TILE]).then_inc(window_landed[0], 16)
            sp.dma_start(window[1][:, :, HALO - TILE:], x_dram[:, :, 0:2 * TILE]).then_inc(window_landed[1], 16)
            for dst, src in weights[2:-1]:
                sp.dma_start(dst, src).then_inc(s["weights_landed"], 16)
            for m in range(2):
                load_center(m, m)
            sp.dma_start(wx_raw, ins["Wx"]).then_inc(s["wx_landed"], 16)
            sp.dma_start(*weights[-1]).then_inc(s["weights_landed"], 16)
            for m in (2, 3):
                load_window(m, m % 2)
            lay_out(0, 0)
            load_center(2, 0)

            def tile(n, pair, par, ahead):
                if ahead == 3:
                    load_center(n + 3, 1 - par)
                if ahead >= 1:
                    lay_out(n + 1, 1 - par)
                sp.wait_ge(s["hT_free"], STEPS * n + STEPS + 2)
                sp.sem_inc(s["sp_passed"], 1)
                sp.dma_start(x2_d.rearrange("c p n -> p c n")[:, :, bass.ds(n * TILE, TILE)], x2[par])\
                    .then_inc(x2_stored[par], 16)
                if ahead == 3 and not (isinstance(n, int) and n + 4 >= NTILE):
                    load_window(n + 4, par)

            tiles(sp, tile)
            for par in range(2):
                sp.wait_ge(x2_stored[par], 16 * NTILE // 2)

        @block.gpsimd
        def _(pool):
            g = nc.gpsimd
            g.memset(window[0][:, :, 0:HALO], 0.0).then_inc(s["bufs_zeroed"], 1)
            g.memset(window[1][:, :, 0:HALO - TILE], 0.0).then_inc(s["bufs_zeroed"], 1)
            g.memset(cell, 0.0).then_inc(s["bufs_zeroed"], 1)
            g.memset(state, 0.0).then_inc(s["bufs_zeroed"], 1)
            for par in range(2):
                g.memset(laid[par], 0.0).then_inc(s["bufs_zeroed"], 1)
            for par in range(2):
                g.memset(hT[par], 0.0).then_inc(s["hT_free"], 1)
            g.memset(decays, 1.0).then_inc(s["bufs_zeroed"], 1)
            pool.wait_ge(s["hT_free"], 2)
            pool.wait_ge(s["weights_landed"], 16 * len(weights))
            g.tensor_copy(hT[0][:, :, 0:B], cond).then_inc(s["hT_ready"], 1)
            pool.wait_ge(s["bufs_zeroed"], 7)
            g.memset(decays[:, :, 0:1], 0.0).then_inc(s["bufs_zeroed"], 1)

            def split_low(n, par):
                pool.wait_ge(s["x1_hi_ready"], n + 1)
                if later(n, 2):
                    pool.wait_ge(s["xw_summed"], KD * n - KD)
                g.tensor_tensor(x1_lo[par], x1[par], x1_hi[par].bitcast(F32), ALU.subtract)\
                    .then_inc(s["x1_split"], 1)

            for n in range(2):
                split_low(n, n)

            def tile(n, pair, par, ahead):
                if later(n, 2):
                    pool.wait_ge(x2_stored[par], 16 * pair)
                for st in range(STEPS):
                    pool.wait_ge(s["hT_ready"], STEPS * n + st + 2)
                    cols = slice(st * B, (st + 1) * B)
                    g.tensor_tensor(x2[par][:, :, cols], x1[par][:, :, cols], hT[(st + 1) % 2][:, :, 0:B], ALU.add)\
                        .then_inc(s["hT_free"], 1)
                if ahead >= 2:
                    split_low(n + 2, par)

            tiles(pool, tile)

        @block.tensor
        def _(pe):
            mm = nc.tensor.matmul

            def project(n, par):
                pe.wait_ge(s["conv_done"], KD * TAPS * (n + 1))
                if later(n, 1):
                    pe.wait_ge(s["drive_ready"], n)
                for k in range(KD):
                    last = mm(proj_ps, wp[:, k, :], conv[par][:, k, :], start=k == 0, stop=k == KD - 1)
                last.then_inc(s["proj_done"], 1)

            def inputs(n, par):
                pe.wait_ge(center_landed[par], 16 * (n // 2 + 1) if isinstance(n, int) else 8 * (n - par) + 16)
                pe.wait_ge(s["soft_abs"], n + 1)
                for k in range(KD):
                    last = mm(u_ps, ws[:, k, :], center[par][:, k, :], start=k == 0,
                              stop=k == KD - 1)
                last.then_inc(s["u_done"], 1)

            def outputs(n, par):
                pe.wait_ge(s["y_ready"], n + 1)
                for m in range(KD):
                    last = mm(out_ps[:, m * P:(m + 1) * P], wo[:, m * P:(m + 1) * P], y, start=True, stop=True)
                last.then_inc(s["out_done"], 1)

            def input_products(n, par, start, count):
                for i in range(start, start + count):
                    q, k, part = i // (KD * 3), i // 3 % KD, i % 3
                    cols = slice(q * GCOLS, (q + 1) * GCOLS)
                    if i == 0:
                        pe.wait_ge(s["x1_split"], n + 1)
                    if k == 0 and part == 0 and (later(n, 1) or q >= 2):
                        pe.wait_ge(s["xw_ready"], KD * n + q - 1)
                    last = mm(xw_ps[q % 2][:, :], (x1_lo if part == 2 else x1_hi)[par][:, k, :],
                              (wx_lo if part == 1 else wx_hi)[:, k, cols], start=k == 0 and part == 0,
                              stop=k == KD - 1 and part == 2)
                    if k == KD - 1 and part == 2:
                        last.then_inc(s["xw_summed"], 1)

            pe.wait_ge(s["weights_landed"], 16 * len(weights))
            pe.wait_ge(s["bufs_zeroed"], 8)
            pe.wait_ge(s["y_ones"], 1)
            for n in range(2):
                project(n, n)
                inputs(n, n)
                outputs(n, n)
            pe.wait_ge(s["wx_ready"], KD)
            input_products(0, 0, 0, 3 * KD * KD)

            def tile(n, pair, par, ahead):
                done = 0
                for st in range(STEPS):
                    pe.wait_ge(s["hT_ready"], STEPS * n + st + 1)
                    for bank, c0, c1, done_sem in ((ifg_ps, 0, 3 * P, "ifg_done"), (o_gate_ps, 3 * P, 4 * P, "o_done")):
                        for k in range(KD):
                            for j in range(KD):
                                last = mm(bank[32 * j:32 * j + 32, 0:c1 - c0], hT[st % 2][:, k, :],
                                          wh[:, k, j * GCOLS + c0:j * GCOLS + c1], start=k == 0, stop=k == KD - 1,
                                          skip_group_check=True)
                        last.then_inc(s[done_sem], 1)
                    share = PRODUCTS[st] if ahead >= 1 else 0
                    first = min(share, BEFORE_CELL)
                    second = min(share - first, BEFORE_O)
                    input_products(n + 1, 1 - par, done, first)
                    pe.wait_ge(s["c_ready"], STEPS * n + st + 1)
                    nc.tensor.transpose(cell_turned[:, 0:P], cell, ident).then_inc(s["c_turned"], 1)
                    input_products(n + 1, 1 - par, done + first, second)
                    pe.wait_ge(s["o_ready"], STEPS * n + st + 1)
                    nc.tensor.transpose(o_turned[:, 0:P], sig_o, ident).then_inc(s["o_turned"], 1)
                    input_products(n + 1, 1 - par, done + first + second, share - first - second)
                    done += share
                    if ahead >= 2 and st == PROJECT_AT:
                        project(n + 2, par)
                    if ahead >= 2 and st == INPUTS_AT:
                        inputs(n + 2, par)
                    if ahead >= 2 and st == OUTPUTS_AT:
                        outputs(n + 2, par)

            tiles(pe, tile)

        @block.scalar
        def _(act):
            a = nc.scalar.activation

            def soft_first(n):
                act.wait_ge(s["proj_done"], n + 1)
                if later(n, 1):
                    act.wait_ge(s["y_ready"], n)
                a(c_gate, proj_ps[N_STATE:2 * N_STATE, :], ACT.Tanh, bias=bp_c).then_inc(s["gate_c_ready"], 1)
                a(z_relu, proj_ps[0:N_STATE, :], ACT.Relu, bias=bp_b)
                a(z_abs, proj_ps[0:N_STATE, :], ACT.Abs, bias=bp_b).then_inc(s["soft_abs"], 1)

            def soft_last(n):
                act.wait_ge(s["soft_abs"], n + 1)
                a(z_exp, z_abs, ACT.Exp, scale=-1.0).then_inc(s["soft_exp"], 1)
                act.wait_ge(s["soft_exp"], n + 3)
                a(z_ln, z_exp, ACT.Ln, bias=1.0).then_inc(s["soft_ready"], 1)

            def split_high(n, par):
                act.wait_ge(s["x1_ready"], n + 1)
                if later(n, 2):
                    act.wait_ge(s["xw_summed"], KD * n - KD)
                a(x1_hi[par], x1[par], ACT.Copy).then_inc(s["x1_hi_ready"], 1)

            act.wait_ge(s["weights_landed"], 16 * len(weights))
            for i, src in enumerate((dt_log, a_log)):
                a(scratch[:, i:i + 1], src, ACT.Abs).then_inc(s["small_ready"], 1)
            act.wait_ge(s["small_ready"], 2)
            for i in range(2):
                a(scratch[:, i:i + 1], scratch[:, i:i + 1], ACT.Exp, scale=-1.0).then_inc(s["soft_exp"], 1)
            act.wait_ge(s["soft_exp"], 2)
            for i in range(2):
                a(scratch[:, i:i + 1], scratch[:, i:i + 1], ACT.Ln, bias=1.0).then_inc(s["small_ready"], 1)
            act.wait_ge(s["wx_landed"], 16)
            for k in range(KD):
                a(wx_hi[:, k, :], wx_raw[:, k, :], ACT.Copy).then_inc(s["wx_hi_ready"], 1)
            for n in range(2):
                soft_first(n)
                soft_last(n)
                split_high(n, n)

            def tile(n, pair, par, ahead):
                for st in range(STEPS):
                    t1 = STEPS * n + st + 1
                    act.wait_ge(s["pre_if_ready"], t1)
                    a(sig_if, pre_ifg[:, 0:2 * P].rearrange("p (a b) -> p a b", a=2), ACT.Sigmoid)\
                        .then_inc(s["if_ready"], 1)
                    act.wait_ge(s["pre_g_ready"], t1)
                    a(gcand, pre_ifg[:, 2 * P:], ACT.Tanh).then_inc(s["g_ready"], 1)
                    act.wait_ge(s["pre_o_ready"], t1)
                    a(sig_o, pre_o, ACT.Sigmoid).then_inc(s["o_ready"], 1)
                    act.wait_ge(s["c_turned"], t1)
                    a(tanh_cT, cell_turned[:, 0:P], ACT.Tanh).then_inc(s["tc_ready"], 1)
                    if ahead >= 2 and st == SOFT_AT:
                        soft_first(n + 2)
                    if ahead >= 2 and st == SOFT_AT + 1:
                        soft_last(n + 2)
                    if ahead >= 2 and st == STEPS - 1:
                        split_high(n + 2, par)

            tiles(act, tile)

        @block.vector
        def _(dve):
            v = nc.vector

            def convolve(n, pair, par, lots):
                if 0 in lots:
                    dve.wait_ge(window_landed[par], 16 * (pair + 1))
                    if later(n, 2):
                        dve.wait_ge(s["proj_done"], n - 1)
                for i in lots:
                    for k in range(KD):
                        src = window[par][:, k, i * B:i * B + TILE]
                        if i == 0:
                            v.tensor_scalar(conv[par][:, k, :], src, taps[:, k, 0:1], conv_b[:, k:k + 1], ALU.mult,
                                            ALU.add).then_inc(s["conv_done"], 1)
                        else:
                            dve.wait_ge(s["conv_done"], KD * TAPS * n + KD * (i - 1) + k + 1)
                            v.scalar_tensor_tensor(out=conv[par][:, k, :], in0=src, scalar=taps[:, k, i:i + 1],
                                                   in1=conv[par][:, k, :], op0=ALU.mult,
                                                   op1=ALU.add).then_inc(s["conv_done"], 1)

            def scan(n):
                dve.wait_ge(s["soft_ready"], n + 1)
                v.tensor_tensor(drive_b, z_relu, z_ln, ALU.add).then_inc(s["bt_ready"], 1)
                dve.wait_ge(s["bt_ready"], n + 1)
                dve.wait_ge(s["u_done"], n + 1)
                v.scalar_tensor_tensor(out=drive.rearrange("p b t -> p t b"),
                                       in0=u_ps.rearrange("p (t b) -> p t b", b=B),
                                       scalar=bs, in1=drive_b.rearrange("p (t b) -> p t b", b=B), op0=ALU.add,
                                       op1=ALU.mult).then_inc(s["drive_ready"], 1)
                dve.wait_ge(s["drive_ready"], n + 1)
                v.scalar_tensor_tensor(out=drive[:, :, 0], in0=state[:, :, STEPS - 1], scalar=decay,
                                       in1=drive[:, :, 0], op0=ALU.mult, op1=ALU.add).then_inc(s["carry_added"], 1)
                dve.wait_ge(s["carry_added"], n + 1)
                v.tensor_tensor_scan(state.rearrange("p b t -> p (b t)"), decays.rearrange("p b t -> p (b t)"),
                                     drive.rearrange("p b t -> p (b t)"), 0.0, ALU.mult,
                                     ALU.add).then_inc(s["state_ready"], 1)
                dve.wait_ge(s["state_ready"], n + 1)
                dve.wait_ge(s["gate_c_ready"], n + 1)
                v.scalar_tensor_tensor(out=y[0:N_STATE].rearrange("p (t b) -> p t b", b=B),
                                       in0=state.rearrange("p b t -> p t b"), scalar=delta,
                                       in1=c_gate.rearrange("p (t b) -> p t b", b=B), op0=ALU.mult,
                                       op1=ALU.mult).then_inc(s["y_ready"], 1)

            def add_block(n, par):
                dve.wait_ge(s["out_done"], n + 1)
                if later(n, 2):
                    dve.wait_ge(s["hT_free"], STEPS * n - STEPS + 2)
                v.tensor_tensor(x1[par].rearrange("p k n -> p (k n)"), out_ps[:, :],
                                center[par].rearrange("p k n -> p (k n)"), ALU.add).then_inc(s["x1_ready"], 1)

            def keep_inputs(n, q):
                dve.wait_ge(s["xw_summed"], KD * n + q + 1)
                v.tensor_tensor(xw[:, q, :], xw_ps[q % 2][:, :], xw_bias[:, q, :], ALU.add)\
                    .then_inc(s["xw_ready"], 1)

            dve.wait_ge(s["weights_landed"], 16 * len(weights))
            dve.wait_ge(s["small_ready"], 4)
            v.scalar_tensor_tensor(out=delta, in0=dt_log, scalar=0.0, in1=scratch[:, 0:1], op0=ALU.max,
                                   op1=ALU.add).then_inc(s["small_ready"], 1)
            v.scalar_tensor_tensor(out=scratch[:, 2:3], in0=a_log, scalar=0.0, in1=scratch[:, 1:2], op0=ALU.max,
                                   op1=ALU.add).then_inc(s["small_ready"], 1)
            dve.wait_ge(s["small_ready"], 6)
            v.tensor_tensor(scratch[:, 3:4], delta, scratch[:, 2:3], ALU.mult).then_inc(s["small_ready"], 1)
            dve.wait_ge(s["small_ready"], 7)
            v.tensor_scalar(decay, scratch[:, 3:4], -1.0, 1.0, ALU.mult, ALU.add).then_inc(s["small_ready"], 1)
            dve.wait_ge(s["small_ready"], 8)
            nc.vector.memset(y[N_STATE:], 1.0).then_inc(s["y_ones"], 1)
            dve.wait_ge(s["bufs_zeroed"], 8)
            flat = decays.rearrange("p b t -> p (b t)")
            v.tensor_scalar(flat, flat, decay, None, ALU.mult).then_inc(s["small_ready"], 1)
            dve.wait_ge(s["small_ready"], 9)
            convolve(0, 0, 0, range(TAPS))
            for k in range(KD):
                dve.wait_ge(s["wx_hi_ready"], k + 1)
                v.tensor_tensor(wx_lo[:, k, :], wx_raw[:, k, :], wx_hi[:, k, :].bitcast(F32), ALU.subtract)\
                    .then_inc(s["wx_ready"], 1)
            scan(0)
            add_block(0, 0)
            convolve(1, 0, 1, range(TAPS))
            scan(1)
            add_block(1, 1)
            for q in range(KD):
                keep_inputs(0, q)
            convolve(2, 1, 0, range(TAPS))

            def tile(n, pair, par, ahead):
                dve.wait_ge(laid_landed[par], 16 * KD * (pair + 1))
                for st in range(STEPS):
                    t1 = STEPS * n + st + 1
                    dve.wait_ge(s["ifg_done"], t1)
                    v.tensor_tensor(pre_ifg[:, 0:2 * P], ifg_ps[:, 0:2 * P], laid[par][:, st, 0:2 * P], ALU.add)\
                        .then_inc(s["pre_if_ready"], 1)
                    v.tensor_tensor(pre_ifg[:, 2 * P:], ifg_ps[:, 2 * P:3 * P], laid[par][:, st, 2 * P:3 * P],
                                    ALU.add).then_inc(s["pre_g_ready"], 1)
                    dve.wait_ge(s["if_ready"], t1)
                    v.tensor_tensor(term_f, sig_if[:, 1, :], cell, ALU.mult).then_inc(s["terms_ready"], 1)
                    dve.wait_ge(s["g_ready"], t1)
                    v.tensor_tensor(term_i, sig_if[:, 0, :], gcand, ALU.mult).then_inc(s["terms_ready"], 1)
                    dve.wait_ge(s["o_done"], t1)
                    v.tensor_tensor(pre_o, o_gate_ps[:, 0:P], laid[par][:, st, 3 * P:], ALU.add)\
                        .then_inc(s["pre_o_ready"], 1)
                    dve.wait_ge(s["terms_ready"], 2 * t1)
                    v.tensor_tensor(cell, term_f, term_i, ALU.add).then_inc(s["c_ready"], 1)
                    dve.wait_ge(s["hT_free"], t1)
                    dve.wait_ge(s["o_turned"], t1)
                    dve.wait_ge(s["tc_ready"], t1)
                    v.tensor_tensor(hT[(st + 1) % 2].rearrange("p k b -> p (k b)"), o_turned[:, 0:P], tanh_cT,
                                    ALU.mult).then_inc(s["hT_ready"], 1)
                    if ahead >= 1 and st in KEEP_AT:
                        keep_inputs(n + 1, KEEP_AT[st])
                    if ahead >= 2 and st == SCAN_AT:
                        scan(n + 2)
                    if ahead >= 2 and st == STEPS - 1:
                        add_block(n + 2, par)
                    if ahead >= 3:
                        convolve(n + 3, pair + 1 + par, 1 - par, (2 * st, 2 * st + 1))

            tiles(dve, tile)


def mix_phase(nc, ctx, ins, carve, banks, keep, x2_d, r_d, rows_d):
    ident, cond, slot = keep["ident"], keep["cond"], keep["slot"]
    wr = carve(KD, D)
    maa_k, maa_r = carve(KD), carve(KD)
    win = [carve(KD, B + MIX) for _ in range(2)]
    shift = [carve(KD, MIX) for _ in range(2)]
    xk = [carve(KD, MIX) for _ in range(2)]
    xr = [carve(KD, MIX) for _ in range(2)]
    gate = [carve(KD, MIX) for _ in range(2)]
    rows = [carve(SUB, D) for _ in range(2)]
    index = [[carve(1).bitcast(I32) for _ in range(SUB)] for _ in range(2)]
    r_ps, t_ps = banks[0:4], banks[4:8]
    names = ["weights_landed", "halo_ready", "shift_ready", "xk_ready", "xr_ready", "r_summed", "gate_ready",
             "rows_turned", "rows_ready", "index_ready", "passed"]
    s = {n: ctx.enter_context(nc.semaphore("mx_" + n)) for n in names}
    landed, gate_stored, scattered = ([ctx.enter_context(nc.semaphore(f"mx_{n}{i}")) for i in range(2)]
                                      for n in ("x2_landed", "gate_stored", "scattered"))

    def tiles(eng, body):
        body(0, 0, 0, True)
        body(1, 0, 1, True)
        with eng.Fori(1, NMIX // 2) as pair:
            body(2 * pair, pair, 0, False)
            body(2 * pair + 1, pair, 1, False)

    x2v, rv = x2_d.rearrange("c p n -> p c n"), r_d.rearrange("c p n -> p c n")
    with nc.Block() as block:
        @block.sync
        def _(sp):
            sp.dma_start(wr, ins["wr"]).then_inc(s["weights_landed"], 16)
            sp.dma_start(maa_k, ins["maa_k"]).then_inc(s["weights_landed"], 16)
            sp.dma_start(maa_r, ins["maa_r"]).then_inc(s["weights_landed"], 16)

            def tile(n, pair, par, first):
                if not first:
                    sp.wait_ge(s["xr_ready"], KD * (n - 1))
                if first and par == 0:
                    sp.dma_start(win[0][:, :, B:], x2v[:, :, 0:MIX]).then_inc(landed[0], 16)
                else:
                    sp.dma_start(win[par], x2v[:, :, bass.ds(n * MIX - B, B + MIX)]).then_inc(landed[par], 16)

            tiles(sp, tile)
            for par in range(2):
                sp.wait_ge(landed[par], 16 * NMIX // 2)

        @block.gpsimd
        def _(pool):
            nc.gpsimd.tensor_copy(win[0][:, :, 0:B], cond).then_inc(s["halo_ready"], 1)

            def tile(n, pair, par, first):
                if not first:
                    pool.wait_ge(scattered[par], 16 * SUB * pair)
                    pool.sem_inc(s["passed"], 1)
                for u in range(SUB):
                    nc.gpsimd.tensor_copy(index[par][u], slot[:, bass.ds(n * SUB + u, 1)])\
                        .then_inc(s["index_ready"], 1)
                pool.wait_ge(s["index_ready"], SUB * n + SUB)
                for u in range(SUB):
                    pool.wait_ge(s["rows_ready"], SUB * n + u + 1)
                    pool.sem_inc(s["passed"], 1)
                    nc.gpsimd.indirect_dma_start(
                        out=rows_d, out_offset=bass.IndirectOffsetOnAxis(ap=index[par][u], axis=0),
                        in_=rows[par][:, u, :], in_offset=None, bounds_check=E * CAP - 1,
                        oob_is_err=False).then_inc(scattered[par], 16)

            tiles(pool, tile)
            for par in range(2):
                pool.wait_ge(scattered[par], 16 * SUB * (NMIX // 2))

        @block.tensor
        def _(pe):
            pe.wait_ge(s["weights_landed"], 48)

            def tile(n, pair, par, first):
                for u in range(SUB):
                    pe.wait_ge(s["xk_ready"], KD * (n + 1))
                    if not (first and par == 0):
                        pe.wait_ge(s["rows_ready"], SUB * n + u - SUB + 1)
                    for k in range(KD):
                        last = nc.tensor.transpose(t_ps[u][:, k * P:(k + 1) * P], xk[par][:, k, u * P:(u + 1) * P],
                                                   ident)
                    last.then_inc(s["rows_turned"], 1)
                pe.wait_ge(s["xr_ready"], KD * (n + 1))
                for m in range(KD):
                    if not (first and par == 0):
                        pe.wait_ge(s["gate_ready"], KD * n + m - KD + 1)
                    for k in range(KD):
                        last = nc.tensor.matmul(r_ps[m][:, :], wr[:, k, m * P:(m + 1) * P], xr[par][:, k, :],
                                                start=k == 0, stop=k == KD - 1)
                    last.then_inc(s["r_summed"], 1)

            tiles(pe, tile)

        @block.scalar
        def _(act):
            def tile(n, pair, par, first):
                if not first:
                    act.wait_ge(scattered[par], 16 * SUB * pair)
                for u in range(SUB):
                    act.wait_ge(s["rows_turned"], SUB * n + u + 1)
                    nc.scalar.activation(rows[par][:, u, :], t_ps[u][:, :], ACT.Copy).then_inc(s["rows_ready"], 1)
                if not first:
                    act.wait_ge(gate_stored[par], 16 * pair)
                for m in range(KD):
                    act.wait_ge(s["r_summed"], KD * n + m + 1)
                    nc.scalar.activation(gate[par][:, m, :], r_ps[m][:, :], ACT.Sigmoid).then_inc(s["gate_ready"], 1)
                act.wait_ge(s["gate_ready"], KD * n + KD)
                act.dma_start(rv[:, :, bass.ds(n * MIX, MIX)], gate[par]).then_inc(gate_stored[par], 16)

            tiles(act, tile)
            for par in range(2):
                act.wait_ge(gate_stored[par], 16 * NMIX // 2)

        @block.vector
        def _(dve):
            v = nc.vector
            dve.wait_ge(s["weights_landed"], 48)
            dve.wait_ge(s["halo_ready"], 1)

            def tile(n, pair, par, first):
                dve.wait_ge(landed[par], 16 * (pair + 1))
                v.tensor_tensor(shift[par], win[par][:, :, 0:MIX], win[par][:, :, B:], ALU.subtract)\
                    .then_inc(s["shift_ready"], 1)
                dve.wait_ge(s["shift_ready"], n + 1)
                for dst, maa, done, used, per in ((xk, maa_k, "xk_ready", "rows_turned", SUB),
                                                  (xr, maa_r, "xr_ready", "r_summed", KD)):
                    if not first:
                        dve.wait_ge(s[used], per * (n - 1))
                    for k in range(KD):
                        v.scalar_tensor_tensor(out=dst[par][:, k, :], in0=shift[par][:, k, :],
                                               scalar=maa[:, k:k + 1], in1=win[par][:, k, B:], op0=ALU.mult,
                                               op1=ALU.add).then_inc(s[done], 1)

            tiles(dve, tile)


def split_products(nc, out, left, right, first, last):
    nc.tensor.matmul(out, left[0], right[0], start=first, stop=False)
    nc.tensor.matmul(out, left[0], right[1], start=False, stop=False)
    return nc.tensor.matmul(out, left[1], right[0], start=False, stop=last)


def expert_phase(nc, ctx, ins, carve, banks, keep, rows_d, y_d):
    ident = keep["ident"]
    NS = CAP // P
    wk_raw, wv_raw = carve(KD, FF), carve(KF, D)
    wk_hi, wk_lo = carve(KD, FF, dt=F32R), carve(KD, FF, dt=F32R)
    wv_hi, wv_lo = carve(KF, D, dt=F32R), carve(KF, D, dt=F32R)
    rows = [carve(NS, D) for _ in range(2)]
    xT_hi, xT_lo = ([carve(KD, CAP, dt=F32R) for _ in range(2)] for _ in range(2))
    relu = [carve(CAP) for _ in range(2)]
    square = [carve(CAP) for _ in range(2)]
    hid_hi, hid_lo = carve(KF, CAP, dt=F32R), carve(KF, CAP, dt=F32R)
    y = [carve(D) for _ in range(2)]
    t_ps, h_ps, y_ps = banks[0:2], banks[2:6], banks[6:8]
    names = ["turned", "xT_hi_ready", "xT_ready", "h_summed", "relu_ready", "square_ready", "hid_hi_ready",
             "hid_ready", "y_summed", "y_ready", "wk_landed", "wv_landed", "wk_hi_ready", "wk_ready",
             "wv_hi_ready", "wv_ready"]
    s = {n: ctx.enter_context(nc.semaphore("ex_" + n)) for n in names}
    landed, stored = ([ctx.enter_context(nc.semaphore(f"ex_{n}{i}")) for i in range(2)]
                      for n in ("rows_landed", "y_stored"))

    def experts(eng, body):
        for e in range(2):
            body(e, e)
        with eng.Fori(1, E // 2 - 1) as pair:
            for par in range(2):
                body(2 * pair + par, par)
        for e in range(E - 2, E):
            body(e, e % 2)

    def later(e, n):
        return not (isinstance(e, int) and e < n)

    def is_last(e):
        return isinstance(e, int) and e == E - 1

    with nc.Block() as block:
        @block.sync
        def _(sp):
            def load_rows(e, par):
                if later(e, 2):
                    sp.wait_ge(s["turned"], KD * (e - 1))
                src = rows_d[bass.ds(e * CAP, CAP), :].rearrange("(a p) d -> p a d", p=P)
                sp.dma_start(rows[par], src).then_inc(landed[par], 16)

            load_rows(0, 0)

            def one(e, par):
                if later(e, 1):
                    sp.wait_ge(s["wk_ready"], KD * e)
                sp.dma_start(wk_raw, ins["wk"][:, bass.ds(e * KD, KD), :]).then_inc(s["wk_landed"], 16)
                if not is_last(e):
                    load_rows(e + 1, 1 - par)
                if later(e, 1):
                    sp.wait_ge(s["wv_ready"], KF * e)
                sp.dma_start(wv_raw, ins["wv"][:, bass.ds(e * KF, KF), :]).then_inc(s["wv_landed"], 16)

            experts(sp, one)

        @block.gpsimd
        def _(pool):
            def one(e, par):
                for a in range(NS):
                    pool.wait_ge(s["y_ready"], NS * e + a + 1)
                    pool.dma_start(y_d[bass.ds(e * CAP + a * P, P), :], y[a % 2]).then_inc(stored[a % 2], 16)

            experts(pool, one)
            for par in range(2):
                pool.wait_ge(stored[par], 16 * E * NS // 2)

        @block.tensor
        def _(pe):
            def turn(e, par):
                pe.wait_ge(landed[par], 16 * (e // 2 + 1) if isinstance(e, int) else 8 * (e - par) + 16)
                for k in range(KD):
                    if later(e, 1) or k >= 2:
                        pe.wait_ge(s["xT_ready"], KD * e + k - 1)
                    for a in range(NS):
                        last = nc.tensor.transpose(t_ps[k % 2][:, a * P:(a + 1) * P],
                                                   rows[par][:, a, k * P:(k + 1) * P], ident)
                    last.then_inc(s["turned"], 1)

            turn(0, 0)

            def one(e, par):
                pe.wait_ge(s["wk_ready"], KD * (e + 1))
                pe.wait_ge(s["xT_ready"], KD * (e + 1))
                for f in range(KF):
                    if later(e, 1) or f >= 4:
                        pe.wait_ge(s["relu_ready"], KF * e + f - 3)
                    cols = slice(f * P, (f + 1) * P)
                    for k in range(KD):
                        last = split_products(nc, h_ps[f % 4][:, :], (wk_hi[:, k, cols], wk_lo[:, k, cols]),
                                              (xT_hi[par][:, k, :], xT_lo[par][:, k, :]), k == 0, k == KD - 1)
                    last.then_inc(s["h_summed"], 1)
                if not is_last(e):
                    turn(e + 1, 1 - par)
                pe.wait_ge(s["wv_ready"], KF * (e + 1))
                pe.wait_ge(s["hid_ready"], KF * (e + 1))
                for a in range(NS):
                    if later(e, 1) or a >= 2:
                        pe.wait_ge(s["y_ready"], NS * e + a - 1)
                    cols = slice(a * P, (a + 1) * P)
                    for f in range(KF):
                        last = split_products(nc, y_ps[a % 2][:, :], (hid_hi[:, f, cols], hid_lo[:, f, cols]),
                                              (wv_hi[:, f, :], wv_lo[:, f, :]), f == 0, f == KF - 1)
                    last.then_inc(s["y_summed"], 1)

            experts(pe, one)

        @block.scalar
        def _(act):
            def split_wk(e):
                act.wait_ge(s["wk_landed"], 16 * (e + 1))
                if later(e, 1):
                    act.wait_ge(s["h_summed"], KF * e)
                for k in range(KD):
                    nc.scalar.activation(wk_hi[:, k, :], wk_raw[:, k, :], ACT.Copy).then_inc(s["wk_hi_ready"], 1)

            split_wk(0)

            def one(e, par):
                act.wait_ge(s["wv_landed"], 16 * (e + 1))
                if later(e, 1):
                    act.wait_ge(s["y_summed"], NS * e)
                for f in range(KF):
                    act.wait_ge(s["h_summed"], KF * e + f + 1)
                    if later(e, 1) or f >= 2:
                        act.wait_ge(s["square_ready"], KF * e + f - 1)
                    nc.scalar.activation(relu[f % 2], h_ps[f % 4][:, :], ACT.Relu).then_inc(s["relu_ready"], 1)
                    act.wait_ge(s["relu_ready"], KF * e + f + 1)
                    if later(e, 1) or f >= 2:
                        act.wait_ge(s["hid_ready"], KF * e + f - 1)
                    nc.scalar.activation(square[f % 2], relu[f % 2], ACT.Square).then_inc(s["square_ready"], 1)
                    nc.scalar.activation(wv_hi[:, f, :], wv_raw[:, f, :], ACT.Copy).then_inc(s["wv_hi_ready"], 1)
                if not is_last(e):
                    split_wk(e + 1)
                for a in range(NS):
                    act.wait_ge(s["y_summed"], NS * e + a + 1)
                    if later(e, 1):
                        act.wait_ge(stored[a % 2], 8 * NS * e + 16 * (a // 2))
                    elif a >= 2:
                        act.wait_ge(stored[a % 2], 16 * (a // 2))
                    nc.scalar.activation(y[a % 2], y_ps[a % 2][:, :], ACT.Copy).then_inc(s["y_ready"], 1)

            experts(act, one)

        @block.vector
        def _(dve):
            v = nc.vector

            def split_x(e, par):
                for k in range(KD):
                    dve.wait_ge(s["turned"], KD * e + k + 1)
                    v.tensor_copy(xT_hi[par][:, k, :], t_ps[k % 2][:, :]).then_inc(s["xT_hi_ready"], 1)
                    dve.wait_ge(s["xT_hi_ready"], KD * e + k + 1)
                    v.tensor_tensor(xT_lo[par][:, k, :], t_ps[k % 2][:, :], xT_hi[par][:, k, :].bitcast(F32),
                                    ALU.subtract).then_inc(s["xT_ready"], 1)

            def split_wk(e):
                for k in range(KD):
                    dve.wait_ge(s["wk_hi_ready"], KD * e + k + 1)
                    v.tensor_tensor(wk_lo[:, k, :], wk_raw[:, k, :], wk_hi[:, k, :].bitcast(F32),
                                    ALU.subtract).then_inc(s["wk_ready"], 1)

            split_x(0, 0)
            split_wk(0)

            def one(e, par):
                for f in range(KF):
                    dve.wait_ge(s["square_ready"], KF * e + f + 1)
                    if f == 0 and later(e, 1):
                        dve.wait_ge(s["y_summed"], NS * e)
                    v.tensor_copy(hid_hi[:, f, :], square[f % 2]).then_inc(s["hid_hi_ready"], 1)
                    dve.wait_ge(s["hid_hi_ready"], KF * e + f + 1)
                    v.tensor_tensor(hid_lo[:, f, :], square[f % 2], hid_hi[:, f, :].bitcast(F32),
                                    ALU.subtract).then_inc(s["hid_ready"], 1)
                    dve.wait_ge(s["wv_hi_ready"], KF * e + f + 1)
                    v.tensor_tensor(wv_lo[:, f, :], wv_raw[:, f, :], wv_hi[:, f, :].bitcast(F32),
                                    ALU.subtract).then_inc(s["wv_ready"], 1)
                if not is_last(e):
                    split_x(e + 1, 1 - par)
                    split_wk(e + 1)

            experts(dve, one)


def mask_phase(nc, ctx, ins, carve, banks, keep, x2_d, r_d, y_d, out):
    ident, cond, slot = keep["ident"], keep["cond"], keep["slot"]
    x3 = carve(KD, B, T)
    x2 = [carve(KD, P) for _ in range(2)]
    gate = [carve(KD, P) for _ in range(2)]
    rows = [carve(D) for _ in range(4)]
    index = [carve(1).bitcast(I32) for _ in range(4)]
    gated = [carve(KD, P) for _ in range(2)]
    ax = [carve(T + 1) for _ in range(2)]
    pi = [carve(T) for _ in range(2)]
    cum = carve(T)
    flag = carve(T + 1)
    places = carve(T + 1)
    masked = [carve(T) for _ in range(2)]
    final = [carve(T) for _ in range(2)]
    total, half, inv, pi_sum, limit, chosen, level, rv = [carve(2) for _ in range(8)]
    ones = carve(T)
    t_ps = banks[0:2]
    names = ["index_ready", "passed", "turned", "gated_ready", "x3_ready", "places_made", "abs_ready", "inv_ready", "pi_ready",
             "half_ready", "rv_ready", "limit_ready", "cum_ready", "chosen_ready", "level_ready", "masked_ready", "final_ready"]
    s = {n: ctx.enter_context(nc.semaphore("mk_" + n)) for n in names}
    gathered = [ctx.enter_context(nc.semaphore(f"mk_gathered{i}")) for i in range(4)]
    landed, stored = ([ctx.enter_context(nc.semaphore(f"mk_{n}{i}")) for i in range(2)] for n in ("landed", "stored"))
    QUAD = NTILE // 4
    NU = KD * B

    def tiles(eng, body):
        for i in range(4):
            body(i, 0, i, True)
        with eng.Fori(1, QUAD) as quad:
            for i in range(4):
                body(4 * quad + i, quad, i, False)

    def units(eng, body):
        for par in range(2):
            body(par, par, 0, "first")
        with eng.Fori(1, NU // 2 - 1) as pair:
            for par in range(2):
                body(2 * pair + par, par, pair, "mid")
        for par in range(2):
            body(NU - 2 + par, par, NU // 2 - 1, "last")

    x3_flat = x3.rearrange("p c b t -> p (c b t)")
    x2v, rv_d = x2_d.rearrange("c p n -> p c n"), r_d.rearrange("c p n -> p c n")
    cond_flat = cond.rearrange("p c b -> p (c b)")

    def x3_of(u):
        return x3_flat[:, bass.ds(u * T, T)]

    with nc.Block() as block:
        @block.sync
        def _(sp):
            def tile(n, quad, i, first):
                if not (first and i < 2):
                    sp.wait_ge(s["x3_ready"], n - 1)
                sp.dma_start(x2[i % 2], x2v[:, :, bass.ds(n * P, P)]).then_inc(landed[i % 2], 16)
                sp.dma_start(gate[i % 2], rv_d[:, :, bass.ds(n * P, P)]).then_inc(landed[i % 2], 16)

            tiles(sp, tile)

            def unit(u, par, pair, kind):
                sp.wait_ge(s["final_ready"], u + 1)
                sp.dma_start(out[:, bass.ds(u * T, T)], final[par]).then_inc(stored[par], 16)

            units(sp, unit)
            for par in range(2):
                sp.wait_ge(stored[par], 16 * NU // 2)

        @block.gpsimd
        def _(pool):
            g = nc.gpsimd
            g.iota(places, pattern=[[1, T + 1]], base=0, channel_multiplier=0,
                   allow_small_or_imprecise_dtypes=True).then_inc(s["places_made"], 1)
            for par in range(2):
                g.memset(ax[par][:, T:T + 1], 3.0e38).then_inc(s["places_made"], 1)
            g.memset(ones, 1.0).then_inc(s["places_made"], 1)

            def tile(n, quad, i, first):
                if not first:
                    pool.wait_ge(s["turned"], n - 3)
                    pool.sem_inc(s["passed"], 1)
                g.tensor_copy(index[i], slot[:, bass.ds(n, 1)]).then_inc(s["index_ready"], 1)
                pool.wait_ge(s["index_ready"], n + 1)
                pool.sem_inc(s["passed"], 1)
                g.indirect_dma_start(out=rows[i], out_offset=None, in_=y_d,
                                     in_offset=bass.IndirectOffsetOnAxis(ap=index[i], axis=0)
                                     ).then_inc(gathered[i], 16)

            tiles(pool, tile)

            def unit(u, par, pair, kind):
                pool.wait_ge(s["masked_ready"], u + 1)
                if kind != "first":
                    pool.wait_ge(stored[par], 16 * pair)
                g.tensor_tensor(final[par], masked[par], x3_of(u), ALU.add)\
                    .then_inc(s["final_ready"], 1)

            units(pool, unit)

        @block.tensor
        def _(pe):
            def tile(n, quad, i, first):
                pe.wait_ge(gathered[i], 16 * (quad + 1))
                if not (first and i < 2):
                    pe.wait_ge(s["gated_ready"], n - 1)
                for k in range(KD):
                    last = nc.tensor.transpose(t_ps[i % 2][:, k * P:(k + 1) * P], rows[i][:, k * P:(k + 1) * P], ident)
                last.then_inc(s["turned"], 1)

            tiles(pe, tile)

        @block.scalar
        def _(act):
            act.wait_ge(s["places_made"], 4)
            act.wait_ge(s["x3_ready"], NTILE)

            def absolute(u, par, kind):
                if kind != "first":
                    act.wait_ge(s["masked_ready"], u - 1)
                nc.scalar.activation(ax[par][:, 0:T], x3_of(u), ACT.Abs,
                                     accum_out=total[:, par:par + 1]).then_inc(s["abs_ready"], 1)

            def unit(u, par, pair, kind):
                if kind == "first" and par == 0:
                    absolute(0, 0, "first")
                act.wait_ge(s["inv_ready"], u + 1)
                if kind != "first":
                    act.wait_ge(s["masked_ready"], u - 1)
                nc.scalar.activation(pi[par], ax[par][:, 0:T], ACT.Exp, scale=inv[:, par:par + 1],
                                     accum_out=pi_sum[:, par:par + 1]).then_inc(s["pi_ready"], 1)
                if not (kind == "last" and par == 1):
                    absolute(u + 1, 1 - par, "first" if kind == "first" and par == 0 else "mid")

            units(act, unit)

        @block.vector
        def _(dve):
            v = nc.vector

            def tile(n, quad, i, first):
                par = i % 2
                dve.wait_ge(s["turned"], n + 1)
                dve.wait_ge(landed[par], 32 * (2 * quad + i // 2 + 1))
                v.tensor_tensor(gated[par].rearrange("p c n -> p (c n)"), t_ps[par][:, :],
                                gate[par].rearrange("p c n -> p (c n)"), ALU.mult).then_inc(s["gated_ready"], 1)
                dve.wait_ge(s["gated_ready"], n + 1)
                for k in range(KD):
                    dst = x3[:, k, :, bass.ds(n * STEPS, STEPS)].rearrange("p b t -> p t b")
                    last = v.tensor_tensor(dst, gated[par][:, k, :].rearrange("p (t b) -> p t b", b=B),
                                           x2[par][:, k, :].rearrange("p (t b) -> p t b", b=B), ALU.add)
                last.then_inc(s["x3_ready"], 1)

            tiles(dve, tile)
            dve.wait_ge(s["x3_ready"], NTILE)
            dve.wait_ge(s["places_made"], 4)

            def invert(u, par):
                c = slice(par, par + 1)
                dve.wait_ge(s["abs_ready"], u + 1)
                v.tensor_scalar(half[:, c], total[:, c], 0.5, None, ALU.mult).then_inc(s["half_ready"], 1)
                dve.wait_ge(s["half_ready"], u + 1)
                v.reciprocal(inv[:, c], half[:, c]).then_inc(s["inv_ready"], 1)

            def unit(u, par, pair, kind):
                c = slice(par, par + 1)
                if kind == "first" and par == 0:
                    invert(0, 0)
                rcol = cond_flat[:, bass.ds(u, 1)]
                v.tensor_scalar(rv[:, c], rcol, -0.001, None, ALU.add).then_inc(s["rv_ready"], 1)
                dve.wait_ge(s["pi_ready"], u + 1)
                v.tensor_tensor_scan(cum, ones, pi[par], 0.0, ALU.mult, ALU.add).then_inc(s["cum_ready"], 1)
                dve.wait_ge(s["rv_ready"], u + 1)
                v.tensor_tensor(limit[:, c], rv[:, c], pi_sum[:, c], ALU.mult).then_inc(s["limit_ready"], 1)
                if not (kind == "last" and par == 1):
                    invert(u + 1, 1 - par)
                dve.wait_ge(s["cum_ready"], u + 1)
                dve.wait_ge(s["limit_ready"], u + 1)
                v.tensor_scalar(flag[:, 0:T], cum, limit[:, c], None, ALU.is_le, ALU.add,
                                accum_out=chosen[:, c]).then_inc(s["chosen_ready"], 1)
                dve.wait_ge(s["chosen_ready"], u + 1)
                v.scalar_tensor_tensor(out=flag, in0=places, scalar=chosen[:, c], in1=ax[par], op0=ALU.is_equal,
                                       op1=ALU.mult, accum_out=level[:, c]).then_inc(s["level_ready"], 1)
                dve.wait_ge(s["level_ready"], u + 1)
                if kind != "first":
                    dve.wait_ge(s["final_ready"], u - 1)
                v.scalar_tensor_tensor(out=masked[par], in0=ax[par][:, 0:T], scalar=level[:, c],
                                       in1=x3_of(u), op0=ALU.is_ge, op1=ALU.mult).then_inc(s["masked_ready"], 1)

            units(dve, unit)


def kernel(**inputs):
    import numpy as _np
    import concourse.bacc as _bacc
    from concourse.bass_utils import run_bass_kernel_spmd as _run

    a = {k: _np.asarray(v) for k, v in inputs.items()}

    def gate_blocks(w):
        lead = w.shape[:-1]
        by_gate = w.reshape(lead + (4, KD, P))[..., (0, 1, 3, 2), :, :]
        return _np.swapaxes(by_gate, -3, -2).reshape(lead + (4 * H,))

    arrays = {
        "xT": a["x"].transpose(2, 1, 0).reshape(KD, P, NTOK),
        "ids": a["itok_BxS_2_50255"].reshape(P, NTOK // P),
        "condT": a["cond_1024"].T,
        "Wh": gate_blocks(a["L1_cond_Wh"]), "Wx": gate_blocks(a["L1_cond_Wx"]), "b": gate_blocks(a["L1_cond_b"]),
        "Wp": a["L0_cond_Wp"], "Ws": a["L0_cond_Ws"], "Wo": a["L0_cond_Wo"], "conv_b": a["L0_cond_conv_b"],
        "bo": a["L0_cond_bo"], "bp": a["L0_cond_bp"], "bs": a["L0_cond_bs"], "A_log": a["L0_cond_A_log"],
        "dt_log": a["L0_cond_dt_log"], "wr": a["L2_cond_w_recept"].T, "maa_k": a["L2_cond_time_maa_k"],
        "maa_r": a["L2_cond_time_maa_r"], "wk": a["L2_cond_w_key"].reshape(E * D, FF),
        "wv": a["L2_cond_w_value"].reshape(E * FF, D),
    }
    arrays = {k: _np.ascontiguousarray(v) for k, v in arrays.items()}
    nc = _bacc.Bacc("TRN2", target_bir_lowering=False, num_devices=1)
    ins = {k: nc.dram_tensor("in_" + k, v.shape, mybir.dt.from_np(v.dtype), kind="ExternalInput").ap()
           for k, v in arrays.items()}
    ins["xT"] = ins["xT"].rearrange("c p n -> p c n")
    for k in ("condT", "Wh", "Wx", "Wp", "Ws", "wr", "wk", "wv"):
        ins[k] = ins[k].rearrange("(k p) n -> p k n", p=P)
    ins["bo"] = ins["bo"].rearrange("(o n) -> o n", o=1)
    for k in ("conv_b", "maa_k", "maa_r"):
        ins[k] = ins[k].rearrange("(k p) -> p k", p=P)
    for k in ("bs", "A_log", "dt_log"):
        ins[k] = ins[k].rearrange("(p o) -> p o", o=1)
    ins["bp"] = ins["bp"].rearrange("(h p o) -> h p o", h=2, o=1)
    out = nc.dram_tensor("out_0", (P, KD * B * T), F32, kind="ExternalOutput").ap()
    with nc.allow_non_contiguous_dma(reason="a few per-feature parameter columns"):
        build(nc, ins, out)
    r = _run(nc, [{"in_" + k: v for k, v in arrays.items()}], core_ids=[0])
    got = r.results[0]["out_0"].reshape(P, KD, B, T)
    return _np.ascontiguousarray(got.transpose(2, 3, 1, 0)).reshape(B, T, D)
```

```python
from contextlib import ExitStack

import concourse.bass as bass
from concourse import mybir

F32 = mybir.dt.float32
I32 = mybir.dt.int32
F32R = mybir.dt.float32r
ALU = mybir.AluOpType
ACT = mybir.ActivationFunctionType
AX = mybir.AxisListType

P = 128
B, T, D = 16, 512, 512
KD = D // P
H = 512
N_STATE = 64
TAPS = 16
NTOK = B * T
STEPS = 8
TILE = STEPS * B
NTILE = T // STEPS
HALO = (TAPS - 1) * B
WIN = HALO + TILE
E = 16
FF = 1024
KF = FF // P
CAP = max(4, NTOK // E)
GCOLS = 4 * P
MIX = 256
NMIX = NTOK // MIX
SUB = MIX // P
HASH = 5099 % E
ZROWS = 4


class Carver:
    SLAB = 212800

    def __init__(self, nc, ctx):
        self.nc, self.top, self.last, self.made = nc, 0, 0, 0
        self.base = -(-nc.sbuf_base // 32) * 32
        ctx.enter_context(nc.sbuf_tensor("slab", [P, self.SLAB // 4], F32))

    def __call__(self, *shape, dt=F32, at=None):
        size = 4
        for n in shape:
            size *= n
        self.last = self.top if at is None else at
        if at is None:
            self.top += -(-size // 32) * 32
        assert self.top <= self.SLAB, self.top
        self.made += 1
        return self.nc.alloc_sbuf_tensor_at(f"buf{self.made}", [P, *shape], dt, offset=self.base + self.last)[:]


def build(nc, ins, out):
    x2_d = nc.dram_tensor("x2_scratch", (KD, P, NTOK), F32, kind="Internal").ap()
    xw_d = nc.dram_tensor("input_gates_scratch", (2, KD, TILE, GCOLS), F32, kind="Internal").ap()
    slot_d = nc.dram_tensor("slot_scratch", (NTOK,), I32, kind="Internal").ap()
    rows_d = nc.dram_tensor("expert_in_scratch", (E * CAP, D), F32, kind="Internal").ap()
    y_d = nc.dram_tensor("expert_out_scratch", (E * CAP + 1, D), F32, kind="Internal").ap()
    with ExitStack() as ctx:
        carve = Carver(nc, ctx)
        banks = [ctx.enter_context(nc.psum_tensor(f"bank{i}", [P, 512], F32)) for i in range(8)]

        ident = carve(P)
        cond = carve(KD, B)
        slot = carve(NTILE).bitcast(I32)
        keep = dict(ident=ident, cond=cond, slot=slot)
        base = carve.top
        early = early_weights(nc, ctx, ins, carve)
        after_early = carve.top
        route_phase(nc, ctx, ins, carve, banks, keep, early, slot_d)
        carve.top = after_early
        recur_phase(nc, ctx, ins, carve, banks, keep, early, x2_d, xw_d, rows_d, y_d)
        carve.top = base
        expert_phase(nc, ctx, ins, carve, banks, keep, rows_d, y_d)
        carve.top = base
        keep["x3"] = carve(KD, B, T)
        base = carve.top
        combine_phase(nc, ctx, ins, carve, banks, keep, x2_d, y_d)
        carve.top = base
        mask_phase(nc, ctx, carve, keep, out)


def early_weights(nc, ctx, ins, carve):
    w = {"wh": carve(KD, 4 * H), "wx_lo": carve(KD, 4 * H, dt=F32R)}
    w["wx_raw"] = carve(KD, 4 * H, at=carve.last)
    w["xw_bias"] = carve(KD, GCOLS)
    w["wp"], w["ws"] = carve(KD, 2 * N_STATE), carve(KD, N_STATE)
    w["wo"] = carve(D)[0:N_STATE + 1]
    w["conv_b"], w["maa_k"] = carve(KD), carve(KD)
    for name in ("bp_b", "bp_c", "bs", "a_log", "dt_log"):
        w[name] = carve(1)[0:N_STATE]
    w["small_loads"] = [
        (w["conv_b"], ins["conv_b"]), (w["wp"], ins["Wp"]), (w["ws"], ins["Ws"]), (w["wo"][0:N_STATE], ins["Wo"]),
        (w["wo"][N_STATE:], ins["bo"]), (w["bp_b"], ins["bp"][0]), (w["bp_c"], ins["bp"][1]), (w["bs"], ins["bs"]),
        (w["a_log"], ins["A_log"]), (w["dt_log"], ins["dt_log"]), (w["maa_k"], ins["maa_k"]),
        (w["xw_bias"], ins["b"].partition_broadcast(P).rearrange("p (k n) -> p k n", k=KD))]
    for name in ("small_landed", "wx_landed", "wh_landed"):
        w[name] = ctx.enter_context(nc.semaphore("early_" + name))
    return w


def route_phase(nc, ctx, ins, carve, banks, keep, early, slot_d):
    SEG = NTOK // P
    ident, cond, slot = keep["ident"], keep["cond"], keep["slot"]
    ids = carve(SEG).bitcast(I32)
    hashed = carve(SEG).bitcast(I32)
    expert = carve(SEG)
    expert_no = carve(E, SEG)
    slot_base = carve(E, SEG)
    onehot = carve(E, SEG)
    segment = carve(E, SEG)
    count = carve(E, SEG)
    before = carve(P)
    offset = carve(E)
    slot_f = carve(SEG)
    slot_i = carve(SEG).bitcast(I32)
    psum_off = banks[0]

    def sem(name):
        return ctx.enter_context(nc.semaphore(name))

    ids_landed, cond_landed = sem("rt_ids_landed"), sem("rt_cond_landed")
    consts, steps, offsets_made = sem("rt_consts"), sem("rt_vector_steps"), sem("rt_offsets_made")
    slots_stored, slots_landed = sem("rt_slots_stored"), sem("rt_slots_landed")
    with nc.Block() as block:
        @block.sync
        def _(sp):
            sp.dma_start(ids, ins["ids"]).then_inc(ids_landed, 16)
            sp.dma_start(cond, ins["condT"]).then_inc(cond_landed, 16)
            sp.wait_ge(steps, 13)
            sp.dma_start(slot_d.rearrange("(p i) -> p i", p=P), slot_i).then_inc(slots_stored, 16)
            sp.wait_ge(slots_stored, 16)
            src = slot_d.rearrange("(b c t) -> t b c", b=B, t=STEPS)
            for t in range(STEPS):
                sp.dma_start(slot[t * B:(t + 1) * B, :], src[t], allow_slow_non_contiguous=True)\
                    .then_inc(slots_landed, 16)
            sp.wait_ge(slots_landed, 16 * STEPS)
            sp.wait_ge(cond_landed, 16)

        @block.scalar
        def _(act):
            for dst, src in early["small_loads"]:
                act.dma_start(dst, src).then_inc(early["small_landed"], 16)
            act.dma_start(early["wx_raw"], ins["Wx"]).then_inc(early["wx_landed"], 16)
            act.dma_start(early["wh"], ins["Wh"]).then_inc(early["wh_landed"], 16)

        @block.gpsimd
        def _(pool):
            nc.gpsimd.memset(ident, 0.0).then_inc(consts, 1)
            nc.gpsimd.memset(before, 0.0).then_inc(consts, 1)
            nc.gpsimd.memset(segment, 1.0).then_inc(consts, 1)
            nc.gpsimd.iota(expert_no, pattern=[[1, E], [0, SEG]], base=0, channel_multiplier=0,
                           allow_small_or_imprecise_dtypes=True).then_inc(consts, 1)
            nc.gpsimd.iota(slot_base, pattern=[[CAP, E], [0, SEG]], base=-1 - E * CAP, channel_multiplier=0,
                           allow_small_or_imprecise_dtypes=True).then_inc(consts, 1)
            pool.wait_ge(consts, 5)
            nc.gpsimd.affine_select(out=ident, in_=ident, compare_op=ALU.not_equal, fill=1.0, base=0,
                                    pattern=[[-1, P]], channel_multiplier=1).then_inc(consts, 1)
            nc.gpsimd.affine_select(out=before, in_=before, compare_op=ALU.is_ge, fill=1.0, base=0,
                                    pattern=[[-1, P]], channel_multiplier=1).then_inc(consts, 1)
            nc.gpsimd.memset(segment[:, :, 0:1], 0.0).then_inc(consts, 1)

        @block.tensor
        def _(pe):
            pe.wait_ge(consts, 8)
            pe.wait_ge(steps, 6)
            nc.tensor.matmul(psum_off[:, 0:E], before, count[:, :, SEG - 1], start=True,
                             stop=True).then_inc(offsets_made, 1)

        @block.vector
        def _(dve):
            v = nc.vector
            dve.wait_ge(ids_landed, 16)
            v.tensor_scalar(hashed, ids, E - 1, None, ALU.bitwise_and).then_inc(steps, 1)
            dve.wait_ge(steps, 1)
            v.tensor_scalar(ids, hashed, float(HASH), None, ALU.mult).then_inc(steps, 1)
            dve.wait_ge(steps, 2)
            v.tensor_scalar(hashed, ids, E - 1, None, ALU.bitwise_and).then_inc(steps, 1)
            dve.wait_ge(steps, 3)
            v.tensor_copy(expert, hashed).then_inc(steps, 1)
            dve.wait_ge(steps, 4)
            dve.wait_ge(consts, 8)
            v.tensor_tensor(onehot, expert.unsqueeze(1).broadcast_to([P, E, SEG]), expert_no,
                            ALU.is_equal).then_inc(steps, 1)
            dve.wait_ge(steps, 5)
            v.tensor_tensor_scan(count.rearrange("p e i -> p (e i)"), segment.rearrange("p e i -> p (e i)"),
                                 onehot.rearrange("p e i -> p (e i)"), 0.0, ALU.mult, ALU.add).then_inc(steps, 1)
            dve.wait_ge(offsets_made, 1)
            v.tensor_copy(offset, psum_off[:, 0:E]).then_inc(steps, 1)
            dve.wait_ge(steps, 7)
            v.tensor_tensor(count, count, offset.unsqueeze(2).broadcast_to([P, E, SEG]),
                            ALU.add).then_inc(steps, 1)
            dve.wait_ge(steps, 8)
            v.scalar_tensor_tensor(out=onehot, in0=count, scalar=float(CAP), in1=onehot, op0=ALU.is_le,
                                   op1=ALU.mult).then_inc(steps, 1)
            v.tensor_tensor(count, count, slot_base, ALU.add).then_inc(steps, 1)
            dve.wait_ge(steps, 10)
            v.tensor_tensor(count, count, onehot, ALU.mult).then_inc(steps, 1)
            dve.wait_ge(steps, 11)
            v.tensor_reduce(slot_f, count.rearrange("p e i -> p i e"), AX.X, ALU.add).then_inc(steps, 1)
            dve.wait_ge(steps, 12)
            v.tensor_scalar(slot_i, slot_f, float(E * CAP), None, ALU.add).then_inc(steps, 1)


def recur_phase(nc, ctx, ins, carve, banks, keep, early, x2_d, xw_d, rows_d, y_d):
    ident, cond, slot = keep["ident"], keep["cond"], keep["slot"]
    taps = cond
    wh, wx_lo, wx_raw, xw_bias, wp, ws, wo, conv_b, bp_b, bp_c, bs, a_log, dt_log = (
        early[n] for n in ("wh", "wx_lo", "wx_raw", "xw_bias", "wp", "ws", "wo", "conv_b", "bp_b", "bp_c", "bs",
                           "a_log", "dt_log"))
    small_landed, small_loads = early["small_landed"], 16 * len(early["small_loads"])
    wx_hi = carve(KD, 4 * H, dt=F32R)
    xw = carve(KD, GCOLS)
    laid = [carve(STEPS, GCOLS) for _ in range(2)]
    window = [carve(KD, WIN) for _ in range(2)]
    center = [carve(KD, TILE) for _ in range(2)]
    conv = [carve(KD, TILE) for _ in range(2)]
    x1 = [carve(KD, TILE) for _ in range(2)]
    x1_hi, x1_lo = ([carve(KD, TILE, dt=F32R) for _ in range(2)] for _ in range(2))
    x2 = [carve(KD, B + TILE) for _ in range(2)]
    over = carve.top
    shift, scaled, xk = [carve(KD, TILE) for _ in range(3)]
    rows = carve(D)
    zeros = carve(ZROWS * D, at=over)
    index = carve(1).bitcast(I32)
    maa_k = early["maa_k"]
    delta, decay = carve(1)[0:N_STATE], carve(1)[0:N_STATE]
    scratch = carve(8)[0:N_STATE]
    decays = carve(B, STEPS)[0:N_STATE]
    hT = [carve(KD, 32) for _ in range(2)]
    pre_ifg, pre_o = carve(3 * P), carve(P)
    sig_if, sig_o = carve(2, P), carve(P)
    gcand, cell, term_f, term_i, tanh_c, hid = [carve(P) for _ in range(6)]
    c_gate, z_abs, z_exp, z_ln, z_relu, drive_b = [carve(TILE)[0:N_STATE] for _ in range(6)]
    y = carve(TILE)[0:N_STATE + 1]
    drive = carve(B, STEPS)[0:N_STATE]
    state = carve(B, STEPS)[0:N_STATE]
    ifg_ps, o_gate_ps, xw_ps = banks[0], banks[1], banks[2:4]
    proj_ps, u_ps, out_ps, rows_ps = banks[4][:, 0:TILE], banks[5][0:N_STATE, 0:TILE], banks[6], banks[7]

    names = ["zeros_made", "zero_stored", "wx_hi_ready", "wx_ready", "bufs_zeroed", "y_ones", "small_ready",
             "conv_done", "proj_done", "u_done", "gate_c_ready", "soft_exp", "soft_ready", "bt_ready",
             "drive_ready", "carry_added", "state_ready", "y_ready", "out_done", "x1_ready", "x1_hi_ready",
             "x1_split", "hT_free", "hT_ready", "ifg_done", "o_done", "pre_if_ready", "pre_g_ready",
             "pre_o_ready", "if_ready", "g_ready", "o_tanh_ready", "terms_ready", "c_ready", "h_ready",
             "xw_summed", "xw_ready", "soft_abs", "sp_passed", "pool_passed", "halo_ready", "shift_ready",
             "scaled_ready", "mixed", "rows_turned", "rows_ready", "index_ready", "scattered"]
    s = {n: ctx.enter_context(nc.semaphore("rc_" + n)) for n in names}
    window_landed, center_landed, laid_landed, x2_stored, xw_stored = (
        [ctx.enter_context(nc.semaphore(f"rc_{n}{i}")) for i in range(2)]
        for n in ("window_landed", "center_landed", "laid_landed", "x2_stored", "xw_stored"))
    x_dram = ins["xT"]
    NLOOP = (NTILE - 4) // 2
    PRODUCTS = [4, 4, 8, 8, 8, 8, 8, 0]
    KEEP_AT = {2: 0, 3: 1, 5: 2, 6: 3}
    TAPS_AT = [0, 3, 5, 7, 9, 10, 12, 14, 16]
    PROJECT_AT, INPUTS_AT, SOFT_AT, SCAN_AT, OUTPUTS_AT = 0, 1, 0, 4, 7
    SCALE_AT, MIX_AT, TURN_AT, SCATTER_AT = 2, 3, 7, 7

    def tiles(eng, body):
        for n in range(2):
            body(n, 0, n, 3)
        with eng.Fori(1, NLOOP) as pair:
            body(2 * pair, pair, 0, 3)
            body(2 * pair + 1, pair, 1, 3)
        for n in range(2 * NLOOP, NTILE):
            body(n, n // 2, n % 2, min(3, NTILE - 1 - n))

    def later(n, first):
        return not (isinstance(n, int) and n < first)

    with nc.Block() as block:
        @block.sync
        def _(sp):
            def load_center(m, par):
                if later(m, 2):
                    sp.wait_ge(s["x1_ready"], m - 1)
                    sp.sem_inc(s["sp_passed"], 1)
                sp.dma_start(center[par], x_dram[:, :, bass.ds(m * TILE, TILE)]).then_inc(center_landed[par], 16)

            def load_window(m, par):
                if later(m, 2):
                    sp.wait_ge(s["conv_done"], KD * TAPS * (m - 1))
                sp.dma_start(window[par], x_dram[:, :, bass.ds(m * TILE - HALO, WIN)])\
                    .then_inc(window_landed[par], 16)

            def lay_out(m, par):
                def out(q):
                    sp.wait_ge(s["xw_ready"], KD * m + q + 1)
                    sp.dma_start(xw_d[par, q], xw[:, q, :]).then_inc(xw_stored[q % 2], 16)

                def back(q):
                    sp.wait_ge(xw_stored[q % 2], 32 * m + 16 * (q // 2) + 16)
                    sp.dma_start(laid[par][32 * q:32 * q + B, :, :],
                                 xw_d[par, q].rearrange("(t b) n -> b t n", b=B)).then_inc(laid_landed[par], 16)

                out(0)
                for q in range(1, KD):
                    out(q)
                    back(q - 1)
                back(KD - 1)

            sp.wait_ge(s["bufs_zeroed"], 6)
            sp.dma_start(window[0][:, :, HALO:], x_dram[:, :, 0:TILE]).then_inc(window_landed[0], 16)
            sp.dma_start(window[1][:, :, HALO - TILE:], x_dram[:, :, 0:2 * TILE]).then_inc(window_landed[1], 16)
            for m in range(2):
                load_center(m, m)
            for m in (2, 3):
                load_window(m, m % 2)
            lay_out(0, 0)
            load_center(2, 0)

            def tile(n, pair, par, ahead):
                if ahead == 3:
                    load_center(n + 3, 1 - par)
                if ahead >= 1:
                    lay_out(n + 1, 1 - par)
                sp.wait_ge(s["hT_free"], STEPS * n + STEPS + 2)
                sp.sem_inc(s["sp_passed"], 1)
                sp.dma_start(x2_d.rearrange("c p n -> p c n")[:, :, bass.ds(n * TILE, TILE)], x2[par][:, :, B:])\
                    .then_inc(x2_stored[par], 16)
                if ahead == 3 and not (isinstance(n, int) and n + 4 >= NTILE):
                    load_window(n + 4, par)

            tiles(sp, tile)
            for par in range(2):
                sp.wait_ge(x2_stored[par], 16 * NTILE // 2)

        @block.gpsimd
        def _(pool):
            g = nc.gpsimd
            g.memset(window[0][:, :, 0:HALO], 0.0).then_inc(s["bufs_zeroed"], 1)
            g.memset(window[1][:, :, 0:HALO - TILE], 0.0).then_inc(s["bufs_zeroed"], 1)
            g.memset(cell, 0.0).then_inc(s["bufs_zeroed"], 1)
            g.memset(state, 0.0).then_inc(s["bufs_zeroed"], 1)
            for par in range(2):
                g.memset(laid[par], 0.0).then_inc(s["bufs_zeroed"], 1)
            for par in range(2):
                g.memset(hT[par], 0.0).then_inc(s["hT_free"], 1)
            g.memset(decays, 1.0).then_inc(s["bufs_zeroed"], 1)
            g.memset(zeros, 0.0).then_inc(s["zeros_made"], 1)
            pool.wait_ge(s["hT_free"], 2)
            g.tensor_copy(hT[0][:, :, 0:B], cond).then_inc(s["hT_ready"], 1)
            g.tensor_copy(x2[0][:, :, 0:B], cond).then_inc(s["halo_ready"], 1)
            pool.wait_ge(s["bufs_zeroed"], 7)
            g.memset(decays[:, :, 0:1], 0.0).then_inc(s["bufs_zeroed"], 1)

            def split_low(n, par):
                pool.wait_ge(s["x1_hi_ready"], n + 1)
                if later(n, 2):
                    pool.wait_ge(s["xw_summed"], KD * n - KD)
                g.tensor_tensor(x1_lo[par], x1[par], x1_hi[par].bitcast(F32), ALU.subtract)\
                    .then_inc(s["x1_split"], 1)

            for k in range(KD):
                pool.wait_ge(s["wx_hi_ready"], k + 1)
                g.tensor_tensor(wx_lo[:, k, :], wx_raw[:, k, :], wx_hi[:, k, :].bitcast(F32), ALU.subtract)\
                    .then_inc(s["wx_ready"], 1)
            pool.wait_ge(s["zeros_made"], 1)
            for z in range(0, E * CAP, ZROWS * P):
                pool.dma_start(rows_d[z:z + ZROWS * P, :].rearrange("(p r) d -> p (r d)", r=ZROWS), zeros)\
                    .then_inc(s["zero_stored"], 16)
            pool.dma_start(y_d[E * CAP:E * CAP + 1, :], zeros[0:1, 0:D]).then_inc(s["zero_stored"], 16)
            for n in range(2):
                split_low(n, n)

            def mix_shift(m, par):
                if later(m, 1):
                    pool.wait_ge(s["scaled_ready"], KD * m)
                pool.wait_ge(s["halo_ready"], m + 1)
                pool.wait_ge(s["hT_free"], STEPS * m + STEPS + 2)
                g.tensor_tensor(shift, x2[par][:, :, 0:TILE], x2[par][:, :, B:], ALU.subtract)\
                    .then_inc(s["shift_ready"], 1)

            def mix_add(m, par):
                if later(m, 1):
                    pool.wait_ge(s["rows_turned"], m)
                pool.wait_ge(s["scaled_ready"], KD * m + KD)
                g.tensor_tensor(xk, scaled, x2[par][:, :, B:], ALU.add).then_inc(s["mixed"], 1)

            def pick_index(m):
                if later(m, 1):
                    pool.wait_ge(s["scattered"], 16 * m)
                    pool.sem_inc(s["pool_passed"], 1)
                g.tensor_copy(index, slot[:, m:m + 1] if isinstance(m, int) else slot[:, bass.ds(m, 1)])\
                    .then_inc(s["index_ready"], 1)

            def scatter(m):
                pool.wait_ge(s["index_ready"], m + 1)
                pool.wait_ge(s["rows_ready"], m + 1)
                pool.sem_inc(s["pool_passed"], 1)
                g.indirect_dma_start(out=rows_d, out_offset=bass.IndirectOffsetOnAxis(ap=index, axis=0),
                                     in_=rows, in_offset=None, bounds_check=E * CAP - 1,
                                     oob_is_err=False).then_inc(s["scattered"], 16)

            def tile(n, pair, par, ahead):
                if later(n, 2):
                    pool.wait_ge(x2_stored[par], 16 * pair)
                    pool.wait_ge(s["mixed"], n - 1)
                if later(n, 1):
                    pool.wait_ge(s["hT_free"], STEPS * n + 2)
                    pool.sem_inc(s["pool_passed"], 1)
                    g.tensor_copy(x2[par][:, :, 0:B], x2[1 - par][:, :, TILE:]).then_inc(s["halo_ready"], 1)
                    if isinstance(n, int) and n == 1:
                        pool.wait_ge(s["zero_stored"], 16 * (E * CAP // (ZROWS * P) + 1))
                    mix_shift(n - 1, 1 - par)
                for st in range(STEPS):
                    pool.wait_ge(s["hT_ready"], STEPS * n + st + 2)
                    cols, to = slice(st * B, (st + 1) * B), slice((st + 1) * B, (st + 2) * B)
                    g.tensor_tensor(x2[par][:, :, to], x1[par][:, :, cols], hT[(st + 1) % 2][:, :, 0:B], ALU.add)\
                        .then_inc(s["hT_free"], 1)
                    if later(n, 1) and st == MIX_AT:
                        mix_add(n - 1, 1 - par)
                        pick_index(n - 1)
                    if later(n, 1) and st == SCATTER_AT:
                        scatter(n - 1)
                if ahead >= 2:
                    split_low(n + 2, par)

            tiles(pool, tile)
            mix_shift(NTILE - 1, 1)
            mix_add(NTILE - 1, 1)
            pick_index(NTILE - 1)
            scatter(NTILE - 1)
            pool.wait_ge(s["scattered"], 16 * NTILE)

        @block.tensor
        def _(pe):
            mm = nc.tensor.matmul

            def project(n, par):
                pe.wait_ge(s["conv_done"], KD * TAPS * (n + 1))
                if later(n, 1):
                    pe.wait_ge(s["soft_abs"], n)
                for k in range(KD):
                    last = mm(proj_ps, wp[:, k, :], conv[par][:, k, :], start=k == 0, stop=k == KD - 1)
                last.then_inc(s["proj_done"], 1)

            def inputs(n, par):
                pe.wait_ge(center_landed[par], 16 * (n // 2 + 1) if isinstance(n, int) else 8 * (n - par) + 16)
                if later(n, 1):
                    pe.wait_ge(s["drive_ready"], n)
                for k in range(KD):
                    last = mm(u_ps, ws[:, k, :], center[par][:, k, :], start=k == 0,
                              stop=k == KD - 1)
                last.then_inc(s["u_done"], 1)

            def outputs(n, par):
                pe.wait_ge(s["y_ready"], n + 1)
                if later(n, 1):
                    pe.wait_ge(s["x1_ready"], n)
                for m in range(KD):
                    last = mm(out_ps[:, m * P:(m + 1) * P], wo[:, m * P:(m + 1) * P], y, start=True, stop=True)
                last.then_inc(s["out_done"], 1)

            def turn_rows(m, par):
                if later(m, 1):
                    pe.wait_ge(s["rows_ready"], m)
                pe.wait_ge(s["mixed"], m + 1)
                for k in range(KD):
                    last = nc.tensor.transpose(rows_ps[:, k * P:(k + 1) * P], xk[:, k, :], ident)
                last.then_inc(s["rows_turned"], 1)

            def input_products(n, par, start, count):
                for i in range(start, start + count):
                    q, k, part = i // (KD * 3), i // 3 % KD, i % 3
                    cols = slice(q * GCOLS, (q + 1) * GCOLS)
                    if i == 0:
                        pe.wait_ge(s["x1_split"], n + 1)
                    if k == 0 and part == 0 and (later(n, 1) or q >= 2):
                        pe.wait_ge(s["xw_ready"], KD * n + q - 1)
                    last = mm(xw_ps[q % 2][:, :], (x1_lo if part == 2 else x1_hi)[par][:, k, :],
                              (wx_lo if part == 1 else wx_hi)[:, k, cols], start=k == 0 and part == 0,
                              stop=k == KD - 1 and part == 2)
                    if k == KD - 1 and part == 2:
                        last.then_inc(s["xw_summed"], 1)

            pe.wait_ge(small_landed, small_loads)
            pe.wait_ge(s["bufs_zeroed"], 8)
            pe.wait_ge(s["y_ones"], 1)
            for n in range(2):
                project(n, n)
                inputs(n, n)
                outputs(n, n)
                if n == 0:
                    pe.wait_ge(s["wx_ready"], KD)
                    input_products(0, 0, 0, 3 * KD * KD)
            pe.wait_ge(early["wh_landed"], 16)

            def tile(n, pair, par, ahead):
                done = 0
                for st in range(STEPS):
                    pe.wait_ge(s["hT_ready"], STEPS * n + st + 1)
                    for bank, c0, c1, done_sem in ((ifg_ps, 0, 3 * P, "ifg_done"), (o_gate_ps, 3 * P, 4 * P, "o_done")):
                        for k in range(KD):
                            for j in range(KD):
                                last = mm(bank[32 * j:32 * j + 32, 0:c1 - c0], hT[st % 2][:, k, :],
                                          wh[:, k, j * GCOLS + c0:j * GCOLS + c1], start=k == 0, stop=k == KD - 1,
                                          skip_group_check=True)
                        last.then_inc(s[done_sem], 1)
                    share = PRODUCTS[st] if ahead >= 1 else 0
                    input_products(n + 1, 1 - par, done, share)
                    done += share
                    if ahead >= 2 and st == PROJECT_AT:
                        project(n + 2, par)
                    if ahead >= 2 and st == INPUTS_AT:
                        inputs(n + 2, par)
                    if later(n, 1) and st == TURN_AT:
                        turn_rows(n - 1, 1 - par)
                    if ahead >= 2 and st == OUTPUTS_AT:
                        outputs(n + 2, par)

            tiles(pe, tile)
            turn_rows(NTILE - 1, 1)

        @block.scalar
        def _(act):
            a = nc.scalar.activation

            def soft_first(n):
                act.wait_ge(s["proj_done"], n + 1)
                if later(n, 1):
                    act.wait_ge(s["y_ready"], n)
                a(c_gate, proj_ps[N_STATE:2 * N_STATE, :], ACT.Tanh, bias=bp_c).then_inc(s["gate_c_ready"], 1)
                a(z_relu, proj_ps[0:N_STATE, :], ACT.Relu, bias=bp_b)
                a(z_abs, proj_ps[0:N_STATE, :], ACT.Abs, bias=bp_b).then_inc(s["soft_abs"], 1)

            def soft_last(n):
                act.wait_ge(s["soft_abs"], n + 1)
                a(z_exp, z_abs, ACT.Exp, scale=-1.0).then_inc(s["soft_exp"], 1)
                act.wait_ge(s["soft_exp"], n + 3)
                a(z_ln, z_exp, ACT.Ln, bias=1.0).then_inc(s["soft_ready"], 1)

            def split_high(n, par):
                act.wait_ge(s["x1_ready"], n + 1)
                if later(n, 2):
                    act.wait_ge(s["xw_summed"], KD * n - KD)
                a(x1_hi[par], x1[par], ACT.Copy).then_inc(s["x1_hi_ready"], 1)

            def scale_shift(m):
                act.wait_ge(s["shift_ready"], m + 1)
                if later(m, 1):
                    act.wait_ge(s["mixed"], m)
                for k in range(KD):
                    a(scaled[:, k, :], shift[:, k, :], ACT.Identity, scale=maa_k[:, k:k + 1])\
                        .then_inc(s["scaled_ready"], 1)

            def keep_rows(m):
                act.wait_ge(s["rows_turned"], m + 1)
                if later(m, 1):
                    act.wait_ge(s["scattered"], 16 * m)
                a(rows, rows_ps[:, :], ACT.Copy).then_inc(s["rows_ready"], 1)

            act.wait_ge(small_landed, small_loads)
            for i, src in enumerate((dt_log, a_log)):
                a(scratch[:, i:i + 1], src, ACT.Abs).then_inc(s["small_ready"], 1)
            act.wait_ge(s["small_ready"], 2)
            for i in range(2):
                a(scratch[:, i:i + 1], scratch[:, i:i + 1], ACT.Exp, scale=-1.0).then_inc(s["soft_exp"], 1)
            act.wait_ge(s["soft_exp"], 2)
            for i in range(2):
                a(scratch[:, i:i + 1], scratch[:, i:i + 1], ACT.Ln, bias=1.0).then_inc(s["small_ready"], 1)
            act.wait_ge(early["wx_landed"], 16)
            for k in range(KD):
                a(wx_hi[:, k, :], wx_raw[:, k, :], ACT.Copy).then_inc(s["wx_hi_ready"], 1)
            for n in range(2):
                soft_first(n)
                soft_last(n)
                split_high(n, n)

            def tile(n, pair, par, ahead):
                for st in range(STEPS):
                    t1 = STEPS * n + st + 1
                    act.wait_ge(s["pre_if_ready"], t1)
                    a(sig_if, pre_ifg[:, 0:2 * P].rearrange("p (a b) -> p a b", a=2), ACT.Sigmoid)\
                        .then_inc(s["if_ready"], 1)
                    act.wait_ge(s["pre_g_ready"], t1)
                    a(gcand, pre_ifg[:, 2 * P:], ACT.Tanh).then_inc(s["g_ready"], 1)
                    act.wait_ge(s["pre_o_ready"], t1)
                    a(sig_o, pre_o, ACT.Sigmoid).then_inc(s["o_tanh_ready"], 1)
                    act.wait_ge(s["c_ready"], t1)
                    a(tanh_c, cell, ACT.Tanh).then_inc(s["o_tanh_ready"], 1)
                    if ahead >= 2 and st == SOFT_AT:
                        soft_first(n + 2)
                    if ahead >= 2 and st == SOFT_AT + 1:
                        soft_last(n + 2)
                    if later(n, 1) and st == SCALE_AT:
                        scale_shift(n - 1)
                    if later(n, 1) and st == TURN_AT:
                        keep_rows(n - 1)
                    if ahead >= 2 and st == STEPS - 1:
                        split_high(n + 2, par)

            tiles(act, tile)
            scale_shift(NTILE - 1)
            keep_rows(NTILE - 1)

        @block.vector
        def _(dve):
            v = nc.vector

            def convolve(n, pair, par, lots):
                if 0 in lots:
                    dve.wait_ge(window_landed[par], 16 * (pair + 1))
                    if later(n, 2):
                        dve.wait_ge(s["proj_done"], n - 1)
                for i in lots:
                    for k in range(KD):
                        src = window[par][:, k, i * B:i * B + TILE]
                        if i == 0:
                            v.tensor_scalar(conv[par][:, k, :], src, taps[:, k, 0:1], conv_b[:, k:k + 1], ALU.mult,
                                            ALU.add).then_inc(s["conv_done"], 1)
                        else:
                            dve.wait_ge(s["conv_done"], KD * TAPS * n + KD * (i - 1) + k + 1)
                            v.scalar_tensor_tensor(out=conv[par][:, k, :], in0=src, scalar=taps[:, k, i:i + 1],
                                                   in1=conv[par][:, k, :], op0=ALU.mult,
                                                   op1=ALU.add).then_inc(s["conv_done"], 1)

            def scan(n):
                dve.wait_ge(s["soft_ready"], n + 1)
                v.tensor_tensor(drive_b, z_relu, z_ln, ALU.add).then_inc(s["bt_ready"], 1)
                dve.wait_ge(s["bt_ready"], n + 1)
                dve.wait_ge(s["u_done"], n + 1)
                v.scalar_tensor_tensor(out=drive.rearrange("p b t -> p t b"),
                                       in0=u_ps.rearrange("p (t b) -> p t b", b=B),
                                       scalar=bs, in1=drive_b.rearrange("p (t b) -> p t b", b=B), op0=ALU.add,
                                       op1=ALU.mult).then_inc(s["drive_ready"], 1)
                dve.wait_ge(s["drive_ready"], n + 1)
                v.scalar_tensor_tensor(out=drive[:, :, 0], in0=state[:, :, STEPS - 1], scalar=decay,
                                       in1=drive[:, :, 0], op0=ALU.mult, op1=ALU.add).then_inc(s["carry_added"], 1)
                dve.wait_ge(s["carry_added"], n + 1)
                v.tensor_tensor_scan(state.rearrange("p b t -> p (b t)"), decays.rearrange("p b t -> p (b t)"),
                                     drive.rearrange("p b t -> p (b t)"), 0.0, ALU.mult,
                                     ALU.add).then_inc(s["state_ready"], 1)
                dve.wait_ge(s["state_ready"], n + 1)
                dve.wait_ge(s["gate_c_ready"], n + 1)
                v.scalar_tensor_tensor(out=y[0:N_STATE].rearrange("p (t b) -> p t b", b=B),
                                       in0=state.rearrange("p b t -> p t b"), scalar=delta,
                                       in1=c_gate.rearrange("p (t b) -> p t b", b=B), op0=ALU.mult,
                                       op1=ALU.mult).then_inc(s["y_ready"], 1)

            def add_block(n, par):
                dve.wait_ge(s["out_done"], n + 1)
                if later(n, 2):
                    dve.wait_ge(s["hT_free"], STEPS * n - STEPS + 2)
                v.tensor_tensor(x1[par].rearrange("p k n -> p (k n)"), out_ps[:, :],
                                center[par].rearrange("p k n -> p (k n)"), ALU.add).then_inc(s["x1_ready"], 1)

            def keep_inputs(n, q):
                dve.wait_ge(s["xw_summed"], KD * n + q + 1)
                v.tensor_tensor(xw[:, q, :], xw_ps[q % 2][:, :], xw_bias[:, q, :], ALU.add)\
                    .then_inc(s["xw_ready"], 1)

            dve.wait_ge(small_landed, small_loads)
            dve.wait_ge(s["small_ready"], 4)
            v.scalar_tensor_tensor(out=delta, in0=dt_log, scalar=0.0, in1=scratch[:, 0:1], op0=ALU.max,
                                   op1=ALU.add).then_inc(s["small_ready"], 1)
            v.scalar_tensor_tensor(out=scratch[:, 2:3], in0=a_log, scalar=0.0, in1=scratch[:, 1:2], op0=ALU.max,
                                   op1=ALU.add).then_inc(s["small_ready"], 1)
            dve.wait_ge(s["small_ready"], 6)
            v.tensor_tensor(scratch[:, 3:4], delta, scratch[:, 2:3], ALU.mult).then_inc(s["small_ready"], 1)
            dve.wait_ge(s["small_ready"], 7)
            v.tensor_scalar(decay, scratch[:, 3:4], -1.0, 1.0, ALU.mult, ALU.add).then_inc(s["small_ready"], 1)
            dve.wait_ge(s["small_ready"], 8)
            nc.vector.memset(y[N_STATE:], 1.0).then_inc(s["y_ones"], 1)
            dve.wait_ge(s["bufs_zeroed"], 8)
            flat = decays.rearrange("p b t -> p (b t)")
            v.tensor_scalar(flat, flat, decay, None, ALU.mult).then_inc(s["small_ready"], 1)
            dve.wait_ge(s["small_ready"], 9)
            convolve(0, 0, 0, range(TAPS))
            scan(0)
            add_block(0, 0)
            convolve(1, 0, 1, range(TAPS - 4))
            for q in range(KD):
                keep_inputs(0, q)
            convolve(1, 0, 1, range(TAPS - 4, TAPS))
            scan(1)
            add_block(1, 1)
            convolve(2, 1, 0, range(TAPS))

            def tile(n, pair, par, ahead):
                dve.wait_ge(laid_landed[par], 16 * KD * (pair + 1))
                for st in range(STEPS):
                    t1 = STEPS * n + st + 1
                    dve.wait_ge(s["ifg_done"], t1)
                    v.tensor_tensor(pre_ifg[:, 0:2 * P], ifg_ps[:, 0:2 * P], laid[par][:, st, 0:2 * P], ALU.add)\
                        .then_inc(s["pre_if_ready"], 1)
                    dve.wait_ge(s["hT_free"], t1)
                    v.tensor_tensor(pre_ifg[:, 2 * P:], ifg_ps[:, 2 * P:3 * P], laid[par][:, st, 2 * P:3 * P],
                                    ALU.add).then_inc(s["pre_g_ready"], 1)
                    dve.wait_ge(s["if_ready"], t1)
                    v.tensor_tensor(term_f, sig_if[:, 1, :], cell, ALU.mult).then_inc(s["terms_ready"], 1)
                    dve.wait_ge(s["g_ready"], t1)
                    v.tensor_tensor(term_i, sig_if[:, 0, :], gcand, ALU.mult).then_inc(s["terms_ready"], 1)
                    dve.wait_ge(s["o_done"], t1)
                    v.tensor_tensor(pre_o, o_gate_ps[:, 0:P], laid[par][:, st, 3 * P:], ALU.add)\
                        .then_inc(s["pre_o_ready"], 1)
                    dve.wait_ge(s["terms_ready"], 2 * t1)
                    v.tensor_tensor(cell, term_f, term_i, ALU.add).then_inc(s["c_ready"], 1)
                    dve.wait_ge(s["o_tanh_ready"], 2 * t1)
                    v.tensor_tensor(hid, sig_o, tanh_c, ALU.mult).then_inc(s["h_ready"], 1)
                    dve.wait_ge(s["h_ready"], t1)
                    v.transpose(hT[(st + 1) % 2].rearrange("p k b -> p (k b)"), hid).then_inc(s["hT_ready"], 1)
                    if ahead >= 1 and st in KEEP_AT:
                        keep_inputs(n + 1, KEEP_AT[st])
                    if ahead >= 2 and st == SCAN_AT:
                        scan(n + 2)
                    if ahead >= 2 and st == STEPS - 1:
                        add_block(n + 2, par)
                    if ahead >= 3:
                        convolve(n + 3, pair + 1 + par, 1 - par, range(TAPS_AT[st], TAPS_AT[st + 1]))

            tiles(dve, tile)


def split_products(nc, out, left, right, first, last):
    nc.tensor.matmul(out, left[0], right[0], start=first, stop=False)
    nc.tensor.matmul(out, left[0], right[1], start=False, stop=False)
    return nc.tensor.matmul(out, left[1], right[0], start=False, stop=last)


def expert_phase(nc, ctx, ins, carve, banks, keep, rows_d, y_d):
    ident = keep["ident"]
    NS = CAP // P
    TURN_FROM = 3
    wk_raw, wv_raw = carve(KD, FF), carve(KF, D)
    wk_hi, wk_lo = carve(KD, FF, dt=F32R), carve(KD, FF, dt=F32R)
    wv_hi, wv_lo = carve(KF, D, dt=F32R), carve(KF, D, dt=F32R)
    rows = [carve(NS, D) for _ in range(2)]
    xT_hi, xT_lo = ([carve(KD, CAP, dt=F32R) for _ in range(2)] for _ in range(2))
    relu = [carve(CAP) for _ in range(2)]
    square = [carve(CAP) for _ in range(2)]
    hid_hi, hid_lo = carve(KF, CAP, dt=F32R), carve(KF, CAP, dt=F32R)
    y = [carve(D) for _ in range(2)]
    t_ps, h_ps, y_ps = banks[0:2], banks[2:6], banks[6:8]
    names = ["turned", "xT_hi_ready", "xT_ready", "h_summed", "relu_ready", "square_ready", "hid_hi_ready",
             "hid_ready", "y_summed", "y_ready", "wk_landed", "wv_landed", "wk_hi_ready", "wk_ready",
             "wv_hi_ready", "wv_ready"]
    s = {n: ctx.enter_context(nc.semaphore("ex_" + n)) for n in names}
    landed, stored = ([ctx.enter_context(nc.semaphore(f"ex_{n}{i}")) for i in range(2)]
                      for n in ("rows_landed", "y_stored"))

    def experts(eng, body):
        for e in range(2):
            body(e, e)
        with eng.Fori(1, E // 2 - 1) as pair:
            for par in range(2):
                body(2 * pair + par, par)
        for e in range(E - 2, E):
            body(e, e % 2)

    def later(e, n):
        return not (isinstance(e, int) and e < n)

    def is_last(e):
        return isinstance(e, int) and e == E - 1

    with nc.Block() as block:
        @block.sync
        def _(sp):
            def load_rows(e, par):
                if later(e, 2):
                    sp.wait_ge(s["turned"], KD * (e - 1))
                src = rows_d[bass.ds(e * CAP, CAP), :].rearrange("(a p) d -> p a d", p=P)
                sp.dma_start(rows[par], src).then_inc(landed[par], 16)

            load_rows(0, 0)

            def one(e, par):
                if later(e, 1):
                    sp.wait_ge(s["wk_ready"], KD * e)
                sp.dma_start(wk_raw, ins["wk"][:, bass.ds(e * KD, KD), :]).then_inc(s["wk_landed"], 16)
                if not is_last(e):
                    load_rows(e + 1, 1 - par)
                if later(e, 1):
                    sp.wait_ge(s["wv_ready"], KF * e)
                sp.dma_start(wv_raw, ins["wv"][:, bass.ds(e * KF, KF), :]).then_inc(s["wv_landed"], 16)

            experts(sp, one)

        @block.gpsimd
        def _(pool):
            def one(e, par):
                for a in range(NS):
                    pool.wait_ge(s["y_ready"], NS * e + a + 1)
                    pool.dma_start(y_d[bass.ds(e * CAP + a * P, P), :], y[a % 2]).then_inc(stored[a % 2], 16)

            experts(pool, one)
            for par in range(2):
                pool.wait_ge(stored[par], 16 * E * NS // 2)

        @block.tensor
        def _(pe):
            def turn(e, par, k):
                pe.wait_ge(landed[par], 16 * (e // 2 + 1) if isinstance(e, int) else 8 * (e - par) + 16)
                if later(e, 1) or k >= 2:
                    pe.wait_ge(s["xT_ready"], KD * e + k - 1)
                for a in range(NS):
                    last = nc.tensor.transpose(t_ps[k % 2][:, a * P:(a + 1) * P],
                                               rows[par][:, a, k * P:(k + 1) * P], ident)
                last.then_inc(s["turned"], 1)

            for k in range(KD):
                turn(0, 0, k)

            def one(e, par):
                pe.wait_ge(s["xT_ready"], KD * (e + 1))
                for f in range(KF):
                    if later(e, 1) or f >= 4:
                        pe.wait_ge(s["relu_ready"], KF * e + f - 3)
                    cols = slice(f * P, (f + 1) * P)
                    for k in range(KD):
                        if f == 0:
                            pe.wait_ge(s["wk_ready"], KD * e + k + 1)
                        last = split_products(nc, h_ps[f % 4][:, :], (wk_hi[:, k, cols], wk_lo[:, k, cols]),
                                              (xT_hi[par][:, k, :], xT_lo[par][:, k, :]), k == 0, k == KD - 1)
                    last.then_inc(s["h_summed"], 1)
                    if f >= TURN_FROM and f < TURN_FROM + KD and not is_last(e):
                        turn(e + 1, 1 - par, f - TURN_FROM)
                for a in range(NS):
                    if later(e, 1) or a >= 2:
                        pe.wait_ge(s["y_ready"], NS * e + a - 1)
                    cols = slice(a * P, (a + 1) * P)
                    for f in range(KF):
                        if a == 0:
                            pe.wait_ge(s["hid_ready"], KF * e + f + 1)
                            pe.wait_ge(s["wv_ready"], KF * e + f + 1)
                        last = split_products(nc, y_ps[a % 2][:, :], (hid_hi[:, f, cols], hid_lo[:, f, cols]),
                                              (wv_hi[:, f, :], wv_lo[:, f, :]), f == 0, f == KF - 1)
                    last.then_inc(s["y_summed"], 1)

            experts(pe, one)

        @block.scalar
        def _(act):
            def split_wk(e):
                act.wait_ge(s["wk_landed"], 16 * (e + 1))
                if later(e, 1):
                    act.wait_ge(s["h_summed"], KF * e)
                for k in range(KD):
                    nc.scalar.activation(wk_hi[:, k, :], wk_raw[:, k, :], ACT.Copy).then_inc(s["wk_hi_ready"], 1)

            split_wk(0)

            def one(e, par):
                act.wait_ge(s["wv_landed"], 16 * (e + 1))
                if later(e, 1):
                    act.wait_ge(s["y_summed"], NS * e)
                for f in range(KF):
                    act.wait_ge(s["h_summed"], KF * e + f + 1)
                    if later(e, 1) or f >= 2:
                        act.wait_ge(s["square_ready"], KF * e + f - 1)
                    nc.scalar.activation(relu[f % 2], h_ps[f % 4][:, :], ACT.Relu).then_inc(s["relu_ready"], 1)
                    act.wait_ge(s["relu_ready"], KF * e + f + 1)
                    if later(e, 1) or f >= 2:
                        act.wait_ge(s["hid_ready"], KF * e + f - 1)
                    nc.scalar.activation(square[f % 2], relu[f % 2], ACT.Square).then_inc(s["square_ready"], 1)
                    nc.scalar.activation(wv_hi[:, f, :], wv_raw[:, f, :], ACT.Copy).then_inc(s["wv_hi_ready"], 1)
                if not is_last(e):
                    split_wk(e + 1)
                for a in range(NS):
                    act.wait_ge(s["y_summed"], NS * e + a + 1)
                    if later(e, 1):
                        act.wait_ge(stored[a % 2], 8 * NS * e + 16 * (a // 2))
                    elif a >= 2:
                        act.wait_ge(stored[a % 2], 16 * (a // 2))
                    nc.scalar.activation(y[a % 2], y_ps[a % 2][:, :], ACT.Copy).then_inc(s["y_ready"], 1)

            experts(act, one)

        @block.vector
        def _(dve):
            v = nc.vector

            def split_x(e, par, k):
                dve.wait_ge(s["turned"], KD * e + k + 1)
                v.tensor_copy(xT_hi[par][:, k, :], t_ps[k % 2][:, :]).then_inc(s["xT_hi_ready"], 1)
                dve.wait_ge(s["xT_hi_ready"], KD * e + k + 1)
                v.tensor_tensor(xT_lo[par][:, k, :], t_ps[k % 2][:, :], xT_hi[par][:, k, :].bitcast(F32),
                                ALU.subtract).then_inc(s["xT_ready"], 1)

            def split_wk(e):
                for k in range(KD):
                    dve.wait_ge(s["wk_hi_ready"], KD * e + k + 1)
                    v.tensor_tensor(wk_lo[:, k, :], wk_raw[:, k, :], wk_hi[:, k, :].bitcast(F32),
                                    ALU.subtract).then_inc(s["wk_ready"], 1)

            for k in range(KD):
                split_x(0, 0, k)
            split_wk(0)

            def one(e, par):
                for f in range(KF):
                    dve.wait_ge(s["square_ready"], KF * e + f + 1)
                    if f == 0 and later(e, 1):
                        dve.wait_ge(s["y_summed"], NS * e)
                    v.tensor_copy(hid_hi[:, f, :], square[f % 2]).then_inc(s["hid_hi_ready"], 1)
                    dve.wait_ge(s["hid_hi_ready"], KF * e + f + 1)
                    v.tensor_tensor(hid_lo[:, f, :], square[f % 2], hid_hi[:, f, :].bitcast(F32),
                                    ALU.subtract).then_inc(s["hid_ready"], 1)
                    dve.wait_ge(s["wv_hi_ready"], KF * e + f + 1)
                    v.tensor_tensor(wv_lo[:, f, :], wv_raw[:, f, :], wv_hi[:, f, :].bitcast(F32),
                                    ALU.subtract).then_inc(s["wv_ready"], 1)
                    if f > TURN_FROM and f <= TURN_FROM + KD and not is_last(e):
                        split_x(e + 1, 1 - par, f - TURN_FROM - 1)
                if not is_last(e):
                    split_wk(e + 1)

            experts(dve, one)


def combine_phase(nc, ctx, ins, carve, banks, keep, x2_d, y_d):
    ident, cond, slot, x3 = keep["ident"], keep["cond"], keep["slot"], keep["x3"]
    wr_lo = carve(KD, D, dt=F32R)
    wr_raw = carve(KD, D, at=carve.last)
    wr_hi = carve(KD, D, dt=F32R)
    maa_r = carve(KD)
    win = [carve(KD, B + MIX) for _ in range(2)]
    shift, xr = carve(KD, MIX), carve(KD, MIX)
    xr_hi, xr_lo = ([carve(KD, MIX, dt=F32R) for _ in range(2)] for _ in range(2))
    gate = [carve(KD, MIX) for _ in range(2)]
    rows = [carve(D) for _ in range(2 * SUB)]
    index = [carve(1).bitcast(I32) for _ in range(2 * SUB)]
    gated = [carve(KD, P) for _ in range(SUB)]
    r_ps, t_ps = banks[0:4], banks[4:8]
    names = ["weights_landed", "halo_ready", "shift_ready", "xr_ready", "xr_hi_ready", "xr_split",
             "wr_hi_ready", "wr_ready", "r_summed", "gate_ready", "index_ready", "passed", "passed_sp",
             "turned", "gated_ready", "base_ready", "x3_ready"]
    s = {n: ctx.enter_context(nc.semaphore("cb_" + n)) for n in names}
    landed = [ctx.enter_context(nc.semaphore(f"cb_x2_landed{i}")) for i in range(2)]
    gathered = [ctx.enter_context(nc.semaphore(f"cb_gathered{i}")) for i in range(2 * SUB)]

    def tiles(eng, body):
        for par in range(2):
            body(par, 0, par)
        with eng.Fori(1, NMIX // 2 - 1) as pair:
            for par in range(2):
                body(2 * pair + par, pair, par)
        for par in range(2):
            body(NMIX - 2 + par, NMIX // 2 - 1, par)

    def later(n, first):
        return not (isinstance(n, int) and n < first)

    def two_ahead(n):
        return not (isinstance(n, int) and n + 2 >= NMIX)

    def times(h):
        t = slice(h * STEPS, (h + 1) * STEPS) if isinstance(h, int) else bass.ds(h * STEPS, STEPS)
        return x3[:, :, :, t].rearrange("p c b t -> p c t b")

    x2v = x2_d.rearrange("c p n -> p c n")
    with nc.Block() as block:
        @block.sync
        def _(sp):
            sp.dma_start(wr_raw, ins["wr"]).then_inc(s["weights_landed"], 16)
            sp.dma_start(maa_r, ins["maa_r"]).then_inc(s["weights_landed"], 16)

            def tile(n, pair, par):
                if later(n, 2):
                    sp.wait_ge(s["xr_ready"], KD * (n - 1))
                    sp.sem_inc(s["passed_sp"], 1)
                    sp.wait_ge(s["base_ready"], SUB * (n - 1))
                    sp.sem_inc(s["passed_sp"], 1)
                if later(n, 1):
                    sp.dma_start(win[par], x2v[:, :, bass.ds(n * MIX - B, B + MIX)]).then_inc(landed[par], 16)
                else:
                    sp.dma_start(win[0][:, :, B:], x2v[:, :, 0:MIX]).then_inc(landed[0], 16)

            tiles(sp, tile)

        @block.gpsimd
        def _(pool):
            g = nc.gpsimd

            def gather(n, par):
                for u in range(SUB):
                    i, h = par * SUB + u, SUB * n + u
                    if later(n, 2):
                        pool.wait_ge(s["turned"], h - 3)
                        pool.sem_inc(s["passed"], 1)
                    g.tensor_copy(index[i], slot[:, h:h + 1] if isinstance(h, int) else slot[:, bass.ds(h, 1)])\
                        .then_inc(s["index_ready"], 1)
                for u in range(SUB):
                    i, h = par * SUB + u, SUB * n + u
                    pool.wait_ge(s["index_ready"], h + 1)
                    pool.sem_inc(s["passed"], 1)
                    g.indirect_dma_start(out=rows[i], out_offset=None, in_=y_d,
                                         in_offset=bass.IndirectOffsetOnAxis(ap=index[i], axis=0)
                                         ).then_inc(gathered[i], 16)

            def shift_of(m, pair, par):
                pool.wait_ge(landed[par], 16 * (pair + 1))
                if later(m, 1):
                    pool.wait_ge(s["xr_ready"], KD * m)
                else:
                    pool.wait_ge(s["halo_ready"], 1)
                g.tensor_tensor(shift, win[par][:, :, 0:MIX], win[par][:, :, B:], ALU.subtract)\
                    .then_inc(s["shift_ready"], 1)

            g.tensor_copy(win[0][:, :, 0:B], cond).then_inc(s["halo_ready"], 1)
            for n in range(2):
                shift_of(n, 0, n)
                gather(n, n)

            def tile(n, pair, par):
                if two_ahead(n):
                    shift_of(n + 2, pair + 1, par)
                    gather(n + 2, par)

            tiles(pool, tile)

        @block.tensor
        def _(pe):
            pe.wait_ge(s["wr_ready"], KD)

            def tile(n, pair, par):
                pe.wait_ge(s["xr_split"], n + 1)
                for m in range(KD):
                    if later(n, 1):
                        pe.wait_ge(s["gate_ready"], KD * n + m - KD + 1)
                    cols = slice(m * P, (m + 1) * P)
                    for k in range(KD):
                        last = split_products(nc, r_ps[m][:, 0:MIX], (wr_hi[:, k, cols], wr_lo[:, k, cols]),
                                              (xr_hi[par][:, k, :], xr_lo[par][:, k, :]), k == 0, k == KD - 1)
                    last.then_inc(s["r_summed"], 1)
                for u in range(SUB):
                    i, h = par * SUB + u, SUB * n + u
                    pe.wait_ge(gathered[i], 16 * (pair + 1))
                    if later(n, 2):
                        pe.wait_ge(s["gated_ready"], h - 3)
                    for k in range(KD):
                        last = nc.tensor.transpose(t_ps[i][:, k * P:(k + 1) * P], rows[i][:, k * P:(k + 1) * P],
                                                   ident)
                    last.then_inc(s["turned"], 1)

            tiles(pe, tile)

        @block.scalar
        def _(act):
            act.wait_ge(s["weights_landed"], 32)
            for k in range(KD):
                nc.scalar.activation(wr_hi[:, k, :], wr_raw[:, k, :], ACT.Copy).then_inc(s["wr_hi_ready"], 1)

            def split_high(n, par):
                act.wait_ge(s["xr_ready"], KD * (n + 1))
                if later(n, 2):
                    act.wait_ge(s["r_summed"], KD * (n - 1))
                nc.scalar.activation(xr_hi[par], xr, ACT.Copy).then_inc(s["xr_hi_ready"], 1)
                for u in range(SUB):
                    src = win[par][:, :, B + u * P:B + (u + 1) * P].rearrange("p c (t b) -> p c t b", b=B)
                    nc.scalar.activation(times(SUB * n + u), src, ACT.Copy).then_inc(s["base_ready"], 1)

            for n in range(2):
                split_high(n, n)

            def tile(n, pair, par):
                if later(n, 2):
                    act.wait_ge(s["gated_ready"], SUB * (n - 1))
                for m in range(KD):
                    act.wait_ge(s["r_summed"], KD * n + m + 1)
                    nc.scalar.activation(gate[par][:, m, :], r_ps[m][:, 0:MIX], ACT.Sigmoid)\
                        .then_inc(s["gate_ready"], 1)
                if two_ahead(n):
                    split_high(n + 2, par)

            tiles(act, tile)

        @block.vector
        def _(dve):
            v = nc.vector
            dve.wait_ge(s["weights_landed"], 32)
            for k in range(KD):
                dve.wait_ge(s["wr_hi_ready"], k + 1)
                v.tensor_tensor(wr_lo[:, k, :], wr_raw[:, k, :], wr_hi[:, k, :].bitcast(F32), ALU.subtract)\
                    .then_inc(s["wr_ready"], 1)

            def mix(n, par):
                dve.wait_ge(s["shift_ready"], n + 1)
                if later(n, 1):
                    dve.wait_ge(s["xr_split"], n)
                for k in range(KD):
                    v.scalar_tensor_tensor(out=xr[:, k, :], in0=shift[:, k, :], scalar=maa_r[:, k:k + 1],
                                           in1=win[par][:, k, B:], op0=ALU.mult,
                                           op1=ALU.add).then_inc(s["xr_ready"], 1)

            def split_low(n, par):
                dve.wait_ge(s["xr_hi_ready"], n + 1)
                v.tensor_tensor(xr_lo[par], xr, xr_hi[par].bitcast(F32), ALU.subtract).then_inc(s["xr_split"], 1)

            for n in range(2):
                mix(n, n)
                split_low(n, n)

            def tile(n, pair, par):
                if two_ahead(n):
                    mix(n + 2, par)
                dve.wait_ge(s["gate_ready"], KD * (n + 1))
                for u in range(SUB):
                    i, h = par * SUB + u, SUB * n + u
                    dve.wait_ge(s["turned"], h + 1)
                    if later(n, 1):
                        dve.wait_ge(s["x3_ready"], h - 1)
                    v.tensor_tensor(gated[u], t_ps[i][:, :].rearrange("p (c n) -> p c n", c=KD),
                                    gate[par][:, :, u * P:(u + 1) * P], ALU.mult).then_inc(s["gated_ready"], 1)
                dve.wait_ge(s["base_ready"], SUB * (n + 1))
                for u in range(SUB):
                    h = SUB * n + u
                    dve.wait_ge(s["gated_ready"], h + 1)
                    v.tensor_tensor(times(h), times(h), gated[u].rearrange("p c (t b) -> p c t b", b=B), ALU.add)\
                        .then_inc(s["x3_ready"], 1)
                if two_ahead(n):
                    split_low(n + 2, par)

            tiles(dve, tile)


def mask_phase(nc, ctx, carve, keep, out):
    cond, x3 = keep["cond"], keep["x3"]
    DEEP = 4
    ax = [carve(T + 1) for _ in range(DEEP)]
    pi = [carve(T) for _ in range(DEEP)]
    cum = [carve(T) for _ in range(2)]
    flag, places, ones = carve(T + 1), carve(T + 1), carve(T)
    masked = [carve(T) for _ in range(2)]
    final = [carve(T) for _ in range(2)]
    total, half, inv, pi_sum, limit, chosen, level = [carve(DEEP) for _ in range(7)]
    rv = carve(KD * B)
    names = ["places_made", "abs_ready", "half_ready", "inv_ready", "pi_ready", "rv_ready", "limit_ready",
             "cum_ready", "chosen_ready", "level_ready", "masked_ready", "final_ready"]
    s = {n: ctx.enter_context(nc.semaphore("mk_" + n)) for n in names}
    stored = [ctx.enter_context(nc.semaphore(f"mk_stored{i}")) for i in range(2)]
    NU = KD * B

    def units(eng, body):
        for i in range(DEEP):
            body(i, i, i // 2)
        with eng.Fori(1, NU // DEEP - 1) as lot:
            for i in range(DEEP):
                body(DEEP * lot + i, i, DEEP // 2 * lot + i // 2)
        for i in range(DEEP):
            body(NU - DEEP + i, i, (NU - DEEP + i) // 2)

    def later(u, n):
        return not (isinstance(u, int) and u < n)

    def there(u):
        return not (isinstance(u, int) and u >= NU)

    x3_flat = x3.rearrange("p c b t -> p (c b t)")

    def x3_of(u):
        return x3_flat[:, u * T:(u + 1) * T] if isinstance(u, int) else x3_flat[:, bass.ds(u * T, T)]

    def column(buf, i):
        return buf[:, i % DEEP:i % DEEP + 1]

    with nc.Block() as block:
        @block.sync
        def _(sp):
            def unit(u, i, before):
                sp.wait_ge(s["final_ready"], u + 1)
                sp.dma_start(out[:, bass.ds(u * T, T)], final[i % 2]).then_inc(stored[i % 2], 16)

            units(sp, unit)
            for par in range(2):
                sp.wait_ge(stored[par], 16 * NU // 2)

        @block.gpsimd
        def _(pool):
            g = nc.gpsimd
            g.iota(places, pattern=[[1, T + 1]], base=0, channel_multiplier=0,
                   allow_small_or_imprecise_dtypes=True).then_inc(s["places_made"], 1)
            for i in range(DEEP):
                g.memset(ax[i][:, T:T + 1], 3.0e38).then_inc(s["places_made"], 1)
            g.memset(ones, 1.0).then_inc(s["places_made"], 1)

            def unit(u, i, before):
                pool.wait_ge(s["masked_ready"], u + 1)
                if later(u, 2):
                    pool.wait_ge(stored[i % 2], 16 * before)
                g.tensor_tensor(final[i % 2], masked[i % 2], x3_of(u), ALU.add).then_inc(s["final_ready"], 1)

            units(pool, unit)

        @block.scalar
        def _(act):
            def absolute(u, i):
                if later(u, DEEP):
                    act.wait_ge(s["masked_ready"], u - DEEP + 1)
                nc.scalar.activation(ax[i % DEEP][:, 0:T], x3_of(u), ACT.Abs,
                                     accum_out=column(total, i)).then_inc(s["abs_ready"], 1)

            def exponent(u, i):
                act.wait_ge(s["inv_ready"], u + 1)
                if later(u, DEEP):
                    act.wait_ge(s["limit_ready"], u - DEEP + 1)
                    act.wait_ge(s["cum_ready"], u - DEEP + 1)
                nc.scalar.activation(pi[i % DEEP], ax[i % DEEP][:, 0:T], ACT.Exp, scale=column(inv, i),
                                     accum_out=column(pi_sum, i)).then_inc(s["pi_ready"], 1)

            for u in range(3):
                absolute(u, u)
            for u in range(2):
                exponent(u, u)

            def unit(u, i, before):
                if there(u + 2):
                    exponent(u + 2, i + 2)
                if there(u + 3):
                    absolute(u + 3, i + 3)

            units(act, unit)

        @block.vector
        def _(dve):
            v = nc.vector
            v.tensor_scalar(rv, cond.rearrange("p c b -> p (c b)"), -0.001, None, ALU.add)\
                .then_inc(s["rv_ready"], 1)

            def halve(u, i):
                dve.wait_ge(s["abs_ready"], u + 1)
                v.tensor_scalar(column(half, i), column(total, i), 0.5, None, ALU.mult).then_inc(s["half_ready"], 1)

            def invert(u, i):
                dve.wait_ge(s["half_ready"], u + 1)
                if later(u, DEEP):
                    dve.wait_ge(s["pi_ready"], u - DEEP + 1)
                v.reciprocal(column(inv, i), column(half, i)).then_inc(s["inv_ready"], 1)

            def scan(u, i):
                dve.wait_ge(s["pi_ready"], u + 1)
                v.tensor_tensor_scan(cum[i % 2], ones, pi[i % DEEP], 0.0, ALU.mult, ALU.add)\
                    .then_inc(s["cum_ready"], 1)

            def bound(u, i):
                r_col = rv[:, u:u + 1] if isinstance(u, int) else rv[:, bass.ds(u, 1)]
                v.tensor_tensor(column(limit, i), r_col, column(pi_sum, i), ALU.mult).then_inc(s["limit_ready"], 1)

            for u in range(3):
                halve(u, u)
                invert(u, u)
            dve.wait_ge(s["places_made"], DEEP + 2)
            scan(0, 0)
            dve.wait_ge(s["rv_ready"], 1)
            bound(0, 0)

            def unit(u, i, before):
                dve.wait_ge(s["cum_ready"], u + 1)
                dve.wait_ge(s["limit_ready"], u + 1)
                v.tensor_scalar(flag[:, 0:T], cum[i % 2], column(limit, i), None, ALU.is_le, ALU.add,
                                accum_out=column(chosen, i)).then_inc(s["chosen_ready"], 1)
                if there(u + 1):
                    scan(u + 1, i + 1)
                dve.wait_ge(s["chosen_ready"], u + 1)
                v.scalar_tensor_tensor(out=flag, in0=places, scalar=column(chosen, i), in1=ax[i], op0=ALU.is_equal,
                                       op1=ALU.mult, accum_out=column(level, i)).then_inc(s["level_ready"], 1)
                if there(u + 1):
                    bound(u + 1, i + 1)
                if there(u + 3):
                    halve(u + 3, i + 3)
                dve.wait_ge(s["level_ready"], u + 1)
                if later(u, 2):
                    dve.wait_ge(s["final_ready"], u - 1)
                v.scalar_tensor_tensor(out=masked[i % 2], in0=ax[i][:, 0:T], scalar=column(level, i),
                                       in1=x3_of(u), op0=ALU.is_ge, op1=ALU.mult).then_inc(s["masked_ready"], 1)
                if there(u + 3):
                    invert(u + 3, i + 3)

            units(dve, unit)


def kernel(**inputs):
    import numpy as _np
    import concourse.bacc as _bacc
    from concourse.bass_utils import run_bass_kernel_spmd as _run

    a = {k: _np.asarray(v) for k, v in inputs.items()}

    def gate_blocks(w):
        lead = w.shape[:-1]
        by_gate = w.reshape(lead + (4, KD, P))[..., (0, 1, 3, 2), :, :]
        return _np.swapaxes(by_gate, -3, -2).reshape(lead + (4 * H,))

    def spread(w, axis=0):
        axis %= w.ndim
        parts = w.reshape(w.shape[:axis] + (KD, KD, P // KD) + w.shape[axis + 1:])
        return _np.swapaxes(parts, axis, axis + 1).reshape(w.shape)

    arrays = {
        "xT": spread(a["x"].transpose(2, 1, 0)).reshape(KD, P, NTOK),
        "ids": a["itok_BxS_2_50255"].reshape(P, NTOK // P),
        "condT": spread(a["cond_1024"].T),
        "Wh": spread(gate_blocks(a["L1_cond_Wh"])), "Wx": spread(gate_blocks(a["L1_cond_Wx"])),
        "b": gate_blocks(a["L1_cond_b"]),
        "Wp": spread(a["L0_cond_Wp"]), "Ws": spread(a["L0_cond_Ws"]), "Wo": spread(a["L0_cond_Wo"], 1),
        "conv_b": spread(a["L0_cond_conv_b"]), "bo": spread(a["L0_cond_bo"]), "bp": a["L0_cond_bp"],
        "bs": a["L0_cond_bs"], "A_log": a["L0_cond_A_log"], "dt_log": a["L0_cond_dt_log"],
        "wr": spread(spread(a["L2_cond_w_recept"].T, 0), 1),
        "maa_k": spread(a["L2_cond_time_maa_k"]), "maa_r": spread(a["L2_cond_time_maa_r"]),
        "wk": spread(a["L2_cond_w_key"], 1).reshape(E * D, FF),
        "wv": spread(a["L2_cond_w_value"], 2).reshape(E * FF, D),
    }
    arrays = {k: _np.ascontiguousarray(v) for k, v in arrays.items()}
    nc = _bacc.Bacc("TRN2", target_bir_lowering=False, num_devices=1)
    ins = {k: nc.dram_tensor("in_" + k, v.shape, mybir.dt.from_np(v.dtype), kind="ExternalInput").ap()
           for k, v in arrays.items()}
    ins["xT"] = ins["xT"].rearrange("c p n -> p c n")
    for k in ("condT", "Wh", "Wx", "Wp", "Ws", "wr", "wk", "wv"):
        ins[k] = ins[k].rearrange("(k p) n -> p k n", p=P)
    ins["bo"] = ins["bo"].rearrange("(o n) -> o n", o=1)
    for k in ("conv_b", "maa_k", "maa_r"):
        ins[k] = ins[k].rearrange("(k p) -> p k", p=P)
    for k in ("bs", "A_log", "dt_log"):
        ins[k] = ins[k].rearrange("(p o) -> p o", o=1)
    ins["bp"] = ins["bp"].rearrange("(h p o) -> h p o", h=2, o=1)
    out = nc.dram_tensor("out_0", (P, KD * B * T), F32, kind="ExternalOutput").ap()
    with nc.allow_non_contiguous_dma(reason="a few per-feature parameter columns"):
        build(nc, ins, out)
    r = _run(nc, [{"in_" + k: v for k, v in arrays.items()}], core_ids=[0])
    got = r.results[0]["out_0"].reshape(P, KD, B, T)
    return _np.ascontiguousarray(spread(got.transpose(2, 3, 1, 0).reshape(B, T, D), 2))
```
